# Optimizing a Trainium2 kernel written in Bass

```python
import numpy as np
import jax
import jax.numpy as jnp

def _softmax(x, axis=-1):
    return jax.nn.softmax(x, axis=axis)

def _gelu(x):
    return jax.nn.gelu(x, approximate=True)

def _silu(x):
    return jax.nn.silu(x)

def _sigmoid(x):
    return jax.nn.sigmoid(x)

def _layernorm(x, axis=-1, eps=1e-05):
    m = jnp.mean(x, axis=axis, keepdims=True)
    v = jnp.var(x, axis=axis, keepdims=True)
    return (x - m) / jnp.sqrt(v + eps)

def _scatter_add(tgt, idx, src, axis=0):
    return tgt.at[idx].add(src)

def _segment_sum(src, seg, n):
    return jax.ops.segment_sum(src, seg, n)
kernel_name = 'mk_decoder_postln_d2_seqx_r8_7eb2ee'

def setup_inputs(seed: int=0):
    np.random.seed(seed)
    _w = jnp.asarray

    def _rec_inputs():
        import jax
        import jax.numpy as jnp
        _rk = jax.random.key(seed)
        x = 7.22e-05 + 1 * jax.random.normal(jax.random.fold_in(_rk, 1), (8, 128, 256), jnp.float32)
        _lenS = 128 - jax.random.randint(jax.random.fold_in(_rk, 7), (8,), 0, max(1, 128 // 4) + 1, jnp.int32)
        _lenS2 = 128 - jax.random.randint(jax.random.fold_in(_rk, 8), (8,), 0, max(1, 128 // 4) + 1, jnp.int32)
        _ctx_2048P = jax.random.normal(jax.random.fold_in(_rk, 12), (8, 16, 256), jnp.float32)
        _ctx_2048c = jax.random.dirichlet(jax.random.fold_in(_rk, 512), 0.3 * jnp.ones((16,), jnp.float32), (8, 128))
        _ctx_2048t = jnp.einsum('bsk,bkd->bsd', _ctx_2048c, _ctx_2048P)
        _ctx_2048t = _ctx_2048t * jax.lax.rsqrt(jnp.mean(jnp.square(_ctx_2048t)) + 1e-12) * 0.953939
        ctx_2048 = 0.00424091 + 1.0017 * (_ctx_2048t + 0.3 * jax.random.normal(jax.random.fold_in(_rk, 612), (8, 128, 256), jnp.float32))
        _validS = jnp.arange(128)[None, :] < _lenS[:, None]
        _validS2 = jnp.arange(128)[None, :] < _lenS2[:, None]
        _causal = jnp.tril(jnp.ones((128, 128), dtype=bool))
        mask_Bx1xSxS_fk0 = jnp.where(jnp.broadcast_to(_validS[:, None, None, :], (8, 1, 128, 128)), -1000000000.0, 0.0).astype(jnp.float32)
        return (x, ctx_2048, mask_Bx1xSxS_fk0)
    x, ctx_2048, mask_Bx1xSxS_fk0 = _rec_inputs()

    def _L0_attn_setup():
        import jax, jax.numpy as jnp
        import numpy as np
        N_HEADS = 32
        N_KV_HEADS = 8
        HEAD_DIM = 64
        D_MODEL = 256
        SLIDING_WINDOW = 64
        ROPE_THETA = 10000.0
        PAST_LENGTH = 0
        EPS = 1e-06

        def _rms_norm(x, w):
            xf = x.astype(jnp.float32)
            rms = jax.lax.rsqrt(jnp.mean(xf * xf, axis=-1, keepdims=True) + EPS)
            return (xf * rms).astype(x.dtype) * w

        def _rope(q, k, past_length):
            s, d = (q.shape[2], q.shape[3])
            inv_freq = 1.0 / ROPE_THETA ** (jnp.arange(0, d, 2, dtype=jnp.float32) / d)
            pos = jnp.arange(s, dtype=jnp.float32) + past_length
            ang = pos[:, None] * inv_freq[None, :]
            emb = jnp.concatenate([ang, ang], axis=-1)
            cos, sin = (jnp.cos(emb), jnp.sin(emb))

            def rot_half(x):
                x1, x2 = jnp.split(x, 2, axis=-1)
                return jnp.concatenate([-x2, x1], axis=-1)
            q = q * cos + rot_half(q) * sin
            k = k * cos + rot_half(k) * sin
            return (q, k)

        def _sliding_mask(seq_len, total_len, past_length):
            q_idx = jnp.arange(seq_len)[:, None]
            k_idx = jnp.arange(total_len)[None, :]
            causal = q_idx + past_length >= k_idx
            window = q_idx + past_length - k_idx < SLIDING_WINDOW
            keep = causal & window
            return jnp.where(keep, 0.0, -jnp.inf).astype(jnp.float32)[None, None]
        key = jax.random.key(seed)
        k1, k2, k3 = jax.random.split(key, 3)
        B, S = (1, 256)
        q_size = N_HEADS * HEAD_DIM
        kv_size = N_KV_HEADS * HEAD_DIM
        return {'x': jax.random.normal(k1, (B, S, D_MODEL), dtype=jnp.float32), 'w_qkv': jax.random.normal(k2, (q_size + 2 * kv_size, D_MODEL), dtype=jnp.float32) * D_MODEL ** (-0.5), 'w_out': jax.random.normal(k3, (D_MODEL, q_size), dtype=jnp.float32) * q_size ** (-0.5), 'q_norm_w': jnp.ones((HEAD_DIM,), dtype=jnp.float32), 'k_norm_w': jnp.ones((HEAD_DIM,), dtype=jnp.float32)}
    _L0_attn_all = _L0_attn_setup()
    _L0_attn_in = {k: v for k, v in _L0_attn_all.items() if k in ('w_qkv', 'w_out', 'q_norm_w', 'k_norm_w')}
    del _L0_attn_all

    def _L0_xattn_setup():
        import jax, jax.numpy as jnp
        import numpy as np
        import math
        B, S, HID, H = (2, 256, 256, 32)
        D = HID // H
        AL = 10

        def _rope_tables(seq_len, dim, dtype):
            inv_freq = 1.0 / 10000.0 ** (np.arange(0, dim, 2, dtype=np.float32) / dim)
            t = np.arange(seq_len, dtype=np.float32)
            freqs = np.outer(t, inv_freq)
            emb = np.concatenate([freqs, freqs], -1)
            return (jnp.asarray(np.cos(emb), dtype), jnp.asarray(np.sin(emb), dtype))

        def _rotate_half(x):
            x1, x2 = jnp.split(x, 2, axis=-1)
            return jnp.concatenate([-x2, x1], axis=-1)
        key = jax.random.key(seed)
        ks = jax.random.split(key, 8)
        hidden_states = jax.random.normal(ks[0], (B, S, HID), dtype=jnp.float32)
        adapter = jax.random.normal(ks[1], (B, AL, HID), dtype=jnp.float32)
        causal = jnp.tril(jnp.ones((S, S), dtype=bool))
        attention_mask = jnp.broadcast_to(jnp.where(causal, 0.0, -1000000000.0).astype(jnp.float32)[None, None], (B, 1, S, S))
        scale = 0.02
        Wq = jax.random.normal(ks[2], (HID, HID), dtype=jnp.float32) * scale
        Wk = jax.random.normal(ks[3], (HID, HID), dtype=jnp.float32) * scale
        Wv = jax.random.normal(ks[4], (HID, HID), dtype=jnp.float32) * scale
        Wo = jax.random.normal(ks[5], (HID, HID), dtype=jnp.float32) * scale
        gate = jax.random.normal(ks[6], (1, H, 1, 1), dtype=jnp.float32) * 0.1
        return {'hidden_states': hidden_states, 'attention_mask': attention_mask, 'adapter': adapter, 'Wq': Wq, 'Wk': Wk, 'Wv': Wv, 'Wo': Wo, 'gate': gate}
    _L0_xattn_all = _L0_xattn_setup()
    _L0_xattn_in = {k: v for k, v in _L0_xattn_all.items() if k in ('Wq', 'Wk', 'Wv', 'Wo', 'gate')}
    del _L0_xattn_all

    def _L0_ffn_setup():
        import jax, jax.numpy as jnp
        import numpy as np
        B, S, D = (2, 256, 256)
        MOE_D = 176
        E = 16
        K = 6
        ALPHA = 0.001

        def _moe_forward(x, gate_w, w_gate, w_up, w_down):
            b, s, d = x.shape
            T = b * s
            h = x.reshape(T, d)
            logits = h @ gate_w.T
            scores = jax.nn.softmax(logits.astype(jnp.float32), axis=-1)
            topk_w, topk_idx = jax.lax.top_k(scores, K)
            cw = jnp.zeros((T, E), jnp.float32)
            cw = cw.at[jnp.arange(T)[:, None], topk_idx].add(topk_w)
            y = jnp.zeros((T, d), x.dtype)
            for e in range(E):
                g = h @ w_gate[e].T
                u = h @ w_up[e].T
                out = jax.nn.silu(g) * u @ w_down[e].T
                y = y + cw[:, e:e + 1].astype(x.dtype) * out
            counts = jnp.sum(jax.nn.one_hot(topk_idx.reshape(b, s * K), E, dtype=jnp.float32), axis=1)
            ce = counts * (E / (s * K))
            scores_bse = scores.reshape(b, s, E)
            aux = jnp.mean(jnp.sum(ce * scores_bse.mean(axis=1), axis=1)) * ALPHA
            return (y.reshape(b, s, d), aux)
        key = jax.random.key(seed)
        ks = jax.random.split(key, 5)
        sd = 1.0 / np.sqrt(D)
        sm = 1.0 / np.sqrt(MOE_D)
        return {'x': jax.random.normal(ks[0], (B, S, D), jnp.float32), 'gate_w': jax.random.normal(ks[1], (E, D), jnp.float32) * sd, 'w_gate': jax.random.normal(ks[2], (E, MOE_D, D), jnp.float32) * sd, 'w_up': jax.random.normal(ks[3], (E, MOE_D, D), jnp.float32) * sd, 'w_down': jax.random.normal(ks[4], (E, D, MOE_D), jnp.float32) * sm}
    _L0_ffn_all = _L0_ffn_setup()
    _L0_ffn_in = {k: v for k, v in _L0_ffn_all.items() if k in ('gate_w', 'w_gate', 'w_up', 'w_down')}
    del _L0_ffn_all

    def _L1_attn_setup():
        import jax, jax.numpy as jnp
        import numpy as np
        HIDDEN = 256
        NUM_HEADS = 16
        HEAD_DIM = HIDDEN // NUM_HEADS
        key = jax.random.key(seed)
        ks = jax.random.split(key, 5)
        B, S, H = (2, 256, HIDDEN)
        qkv_bound = float(np.sqrt(6.0 / (H + 3 * H)))
        out_bound = float(np.sqrt(6.0 / (H + H)))
        return {'x': jax.random.normal(ks[0], (B, S, H), dtype=jnp.float32), 'W_qkv': jax.random.uniform(ks[1], (3 * H, H), minval=-qkv_bound, maxval=qkv_bound, dtype=jnp.float32), 'b_qkv': jnp.zeros((3 * H,), dtype=jnp.float32), 'W_out': jax.random.uniform(ks[2], (H, H), minval=-out_bound, maxval=out_bound, dtype=jnp.float32), 'b_out': jnp.zeros((H,), dtype=jnp.float32)}
    _L1_attn_all = _L1_attn_setup()
    _L1_attn_in = {k: v for k, v in _L1_attn_all.items() if k in ('W_qkv', 'b_qkv', 'W_out', 'b_out')}
    del _L1_attn_all

    def _L1_xattn_setup():
        import jax, jax.numpy as jnp
        import numpy as np
        D_MODEL = 256
        NUM_HEADS = 16
        HEAD_DIM = D_MODEL // NUM_HEADS

        def _fq_sym(x, axis):
            s = jnp.max(jnp.abs(x), axis=axis, keepdims=True) / 127.0
            s = jnp.maximum(s, 1e-08)
            q = jnp.clip(jnp.round(x / s), -127.0, 127.0) * s
            return x + jax.lax.stop_gradient(q - x)

        def _fq_unsigned(x, axis):
            s = jnp.max(x, axis=axis, keepdims=True) / 255.0
            s = jnp.maximum(s, 1e-08)
            q = jnp.clip(jnp.round(x / s), 0.0, 255.0) * s
            return x + jax.lax.stop_gradient(q - x)
        key = jax.random.key(seed)
        ks = jax.random.split(key, 8)
        B, N, M, C = (2, 256, 64, D_MODEL)
        return {'x': jax.random.normal(ks[0], (B, N, C), jnp.float32), 'cond': jax.random.normal(ks[1], (B, M, C), jnp.float32), 'Wq': jax.random.normal(ks[2], (C, C), jnp.float32) * 0.02, 'bq': jnp.zeros((C,), jnp.float32), 'Wkv': jax.random.normal(ks[3], (C, 2 * C), jnp.float32) * 0.02, 'bkv': jnp.zeros((2 * C,), jnp.float32), 'Wp': jax.random.normal(ks[4], (C, C), jnp.float32) * 0.02, 'bp': jnp.zeros((C,), jnp.float32)}
    _L1_xattn_all = _L1_xattn_setup()
    _L1_xattn_in = {k: v for k, v in _L1_xattn_all.items() if k in ('Wq', 'bq', 'Wkv', 'bkv', 'Wp', 'bp')}
    del _L1_xattn_all

    def _L1_ffn_setup():
        import jax, jax.numpy as jnp
        import numpy as np
        B, S, H, I = (1, 64, 256, 768)

        def _quantized_matmul(x, w, scale):
            wq = w.astype(jnp.float8_e4m3fn).astype(x.dtype)
            y = jnp.einsum('bsi,io->bso', x, wq)
            return y * scale
        key = jax.random.key(seed)
        ks = jax.random.split(key, 7)
        return {'x': jax.random.normal(ks[0], (B, S, H), dtype=jnp.float32), 'gate_w': jax.random.normal(ks[1], (H, I), dtype=jnp.float32) * 0.02, 'up_w': jax.random.normal(ks[2], (H, I), dtype=jnp.float32) * 0.02, 'down_w': jax.random.normal(ks[3], (I, H), dtype=jnp.float32) * 0.02, 'gate_scale': jax.random.uniform(ks[4], (I,), dtype=jnp.float32, minval=0.5, maxval=1.5), 'up_scale': jax.random.uniform(ks[5], (I,), dtype=jnp.float32, minval=0.5, maxval=1.5), 'down_scale': jax.random.uniform(ks[6], (H,), dtype=jnp.float32, minval=0.5, maxval=1.5)}
    _L1_ffn_all = _L1_ffn_setup()
    _L1_ffn_in = {k: v for k, v in _L1_ffn_all.items() if k in ('gate_w', 'up_w', 'down_w', 'gate_scale', 'up_scale', 'down_scale')}
    del _L1_ffn_all
    return {'x': x, 'ctx_2048': ctx_2048, 'mask_Bx1xSxS_fk0': mask_Bx1xSxS_fk0, 'L0_attn_w_qkv': _L0_attn_in['w_qkv'], 'L0_attn_w_out': _L0_attn_in['w_out'], 'L0_attn_q_norm_w': _L0_attn_in['q_norm_w'], 'L0_attn_k_norm_w': _L0_attn_in['k_norm_w'], 'L0_xattn_Wq': _L0_xattn_in['Wq'], 'L0_xattn_Wk': _L0_xattn_in['Wk'], 'L0_xattn_Wv': _L0_xattn_in['Wv'], 'L0_xattn_Wo': _L0_xattn_in['Wo'], 'L0_xattn_gate': _L0_xattn_in['gate'], 'L0_ffn_gate_w': _L0_ffn_in['gate_w'], 'L0_ffn_w_gate': _L0_ffn_in['w_gate'], 'L0_ffn_w_up': _L0_ffn_in['w_up'], 'L0_ffn_w_down': _L0_ffn_in['w_down'], 'L1_attn_W_qkv': _L1_attn_in['W_qkv'], 'L1_attn_b_qkv': _L1_attn_in['b_qkv'], 'L1_attn_W_out': _L1_attn_in['W_out'], 'L1_attn_b_out': _L1_attn_in['b_out'], 'L1_xattn_Wq': _L1_xattn_in['Wq'], 'L1_xattn_bq': _L1_xattn_in['bq'], 'L1_xattn_Wkv': _L1_xattn_in['Wkv'], 'L1_xattn_bkv': _L1_xattn_in['bkv'], 'L1_xattn_Wp': _L1_xattn_in['Wp'], 'L1_xattn_bp': _L1_xattn_in['bp'], 'L1_ffn_gate_w': _L1_ffn_in['gate_w'], 'L1_ffn_up_w': _L1_ffn_in['up_w'], 'L1_ffn_down_w': _L1_ffn_in['down_w'], 'L1_ffn_gate_scale': _L1_ffn_in['gate_scale'], 'L1_ffn_up_scale': _L1_ffn_in['up_scale'], 'L1_ffn_down_scale': _L1_ffn_in['down_scale']}

def reference(x, ctx_2048, mask_Bx1xSxS_fk0, L0_attn_w_qkv, L0_attn_w_out, L0_attn_q_norm_w, L0_attn_k_norm_w, L0_xattn_Wq, L0_xattn_Wk, L0_xattn_Wv, L0_xattn_Wo, L0_xattn_gate, L0_ffn_gate_w, L0_ffn_w_gate, L0_ffn_w_up, L0_ffn_w_down, L1_attn_W_qkv, L1_attn_b_qkv, L1_attn_W_out, L1_attn_b_out, L1_xattn_Wq, L1_xattn_bq, L1_xattn_Wkv, L1_xattn_bkv, L1_xattn_Wp, L1_xattn_bp, L1_ffn_gate_w, L1_ffn_up_w, L1_ffn_down_w, L1_ffn_gate_scale, L1_ffn_up_scale, L1_ffn_down_scale):
    import jax
    import jax.numpy as jnp

    def _L0_attn_ref(x, w_qkv, w_out, q_norm_w, k_norm_w):
        import jax, jax.numpy as jnp
        import numpy as np
        N_HEADS = 32
        N_KV_HEADS = 8
        HEAD_DIM = 64
        D_MODEL = 256
        SLIDING_WINDOW = 64
        ROPE_THETA = 10000.0
        PAST_LENGTH = 0
        EPS = 1e-06

        def _rms_norm(x, w):
            xf = x.astype(jnp.float32)
            rms = jax.lax.rsqrt(jnp.mean(xf * xf, axis=-1, keepdims=True) + EPS)
            return (xf * rms).astype(x.dtype) * w

        def _rope(q, k, past_length):
            s, d = (q.shape[2], q.shape[3])
            inv_freq = 1.0 / ROPE_THETA ** (jnp.arange(0, d, 2, dtype=jnp.float32) / d)
            pos = jnp.arange(s, dtype=jnp.float32) + past_length
            ang = pos[:, None] * inv_freq[None, :]
            emb = jnp.concatenate([ang, ang], axis=-1)
            cos, sin = (jnp.cos(emb), jnp.sin(emb))

            def rot_half(x):
                x1, x2 = jnp.split(x, 2, axis=-1)
                return jnp.concatenate([-x2, x1], axis=-1)
            q = q * cos + rot_half(q) * sin
            k = k * cos + rot_half(k) * sin
            return (q, k)

        def _sliding_mask(seq_len, total_len, past_length):
            q_idx = jnp.arange(seq_len)[:, None]
            k_idx = jnp.arange(total_len)[None, :]
            causal = q_idx + past_length >= k_idx
            window = q_idx + past_length - k_idx < SLIDING_WINDOW
            keep = causal & window
            return jnp.where(keep, 0.0, -jnp.inf).astype(jnp.float32)[None, None]
        b, s, _ = x.shape
        n_rep = N_HEADS // N_KV_HEADS
        q_size = N_HEADS * HEAD_DIM
        kv_size = N_KV_HEADS * HEAD_DIM
        qkv = jnp.einsum('bsd,od->bso', x, w_qkv)
        q, k, v = jnp.split(qkv, [q_size, q_size + kv_size], axis=-1)
        q = q.reshape(b, s, N_HEADS, HEAD_DIM).transpose(0, 2, 1, 3)
        k = k.reshape(b, s, N_KV_HEADS, HEAD_DIM).transpose(0, 2, 1, 3)
        v = v.reshape(b, s, N_KV_HEADS, HEAD_DIM).transpose(0, 2, 1, 3)
        q = _rms_norm(q, q_norm_w)
        k = _rms_norm(k, k_norm_w)
        q, k = _rope(q, k, PAST_LENGTH)
        k_rep = jnp.repeat(k, n_rep, axis=1)
        v_rep = jnp.repeat(v, n_rep, axis=1)
        scale = HEAD_DIM ** (-0.5)
        scores = jnp.einsum('bhqd,bhkd->bhqk', q, k_rep) * scale
        scores = scores + _sliding_mask(s, s, PAST_LENGTH)
        probs = jax.nn.softmax(scores, axis=-1)
        attn = jnp.einsum('bhqk,bhkd->bhqd', probs, v_rep)
        attn = attn.transpose(0, 2, 1, 3).reshape(b, s, q_size)
        return jnp.einsum('bso,do->bsd', attn, w_out)

    def _L0_xattn_ref(hidden_states, attention_mask, adapter, Wq, Wk, Wv, Wo, gate):
        import jax, jax.numpy as jnp
        import numpy as np
        import math
        B, S, HID, H = (2, 256, 256, 32)
        D = HID // H
        AL = 10

        def _rope_tables(seq_len, dim, dtype):
            inv_freq = 1.0 / 10000.0 ** (np.arange(0, dim, 2, dtype=np.float32) / dim)
            t = np.arange(seq_len, dtype=np.float32)
            freqs = np.outer(t, inv_freq)
            emb = np.concatenate([freqs, freqs], -1)
            return (jnp.asarray(np.cos(emb), dtype), jnp.asarray(np.sin(emb), dtype))

        def _rotate_half(x):
            x1, x2 = jnp.split(x, 2, axis=-1)
            return jnp.concatenate([-x2, x1], axis=-1)
        bsz, q_len, hid = hidden_states.shape
        n_heads = gate.shape[1]
        head_dim = hid // n_heads
        inv_sqrt_d = 1.0 / math.sqrt(head_dim)

        def split_heads(x, length):
            return x.reshape(bsz, length, n_heads, head_dim).transpose(0, 2, 1, 3)
        q = split_heads(hidden_states @ Wq, q_len)
        k = split_heads(hidden_states @ Wk, q_len)
        v = split_heads(hidden_states @ Wv, q_len)
        cos, sin = _rope_tables(q_len, head_dim, q.dtype)
        q = q * cos + _rotate_half(q) * sin
        k = k * cos + _rotate_half(k) * sin
        scores = jnp.einsum('bhqd,bhkd->bhqk', q, k) * inv_sqrt_d
        scores = scores + attention_mask
        scores = jnp.maximum(scores, jnp.finfo(scores.dtype).min)
        w = jax.nn.softmax(scores.astype(jnp.float32), axis=-1).astype(q.dtype)
        attn_output = jnp.einsum('bhqk,bhkd->bhqd', w, v)
        adapter_len = adapter.shape[1]
        a_k = split_heads(adapter @ Wk, adapter_len)
        a_v = split_heads(adapter @ Wv, adapter_len)
        a_scores = jnp.einsum('bhqd,bhkd->bhqk', q, a_k) * inv_sqrt_d
        a_scores = jnp.tanh(gate) * jax.nn.softmax(a_scores.astype(jnp.float32), axis=-1).astype(q.dtype)
        attn_output = attn_output + jnp.einsum('bhqk,bhkd->bhqd', a_scores, a_v)
        attn_output = attn_output.transpose(0, 2, 1, 3).reshape(bsz, q_len, hid)
        return attn_output @ Wo

    def _L0_ffn_ref(x, gate_w, w_gate, w_up, w_down):
        import jax, jax.numpy as jnp
        import numpy as np
        B, S, D = (2, 256, 256)
        MOE_D = 176
        E = 16
        K = 6
        ALPHA = 0.001

        def _moe_forward(x, gate_w, w_gate, w_up, w_down):
            b, s, d = x.shape
            T = b * s
            h = x.reshape(T, d)
            logits = h @ gate_w.T
            scores = jax.nn.softmax(logits.astype(jnp.float32), axis=-1)
            topk_w, topk_idx = jax.lax.top_k(scores, K)
            cw = jnp.zeros((T, E), jnp.float32)
            cw = cw.at[jnp.arange(T)[:, None], topk_idx].add(topk_w)
            y = jnp.zeros((T, d), x.dtype)
            for e in range(E):
                g = h @ w_gate[e].T
                u = h @ w_up[e].T
                out = jax.nn.silu(g) * u @ w_down[e].T
                y = y + cw[:, e:e + 1].astype(x.dtype) * out
            counts = jnp.sum(jax.nn.one_hot(topk_idx.reshape(b, s * K), E, dtype=jnp.float32), axis=1)
            ce = counts * (E / (s * K))
            scores_bse = scores.reshape(b, s, E)
            aux = jnp.mean(jnp.sum(ce * scores_bse.mean(axis=1), axis=1)) * ALPHA
            return (y.reshape(b, s, d), aux)
        y, _aux = _moe_forward(x, gate_w, w_gate, w_up, w_down)
        return y

    def _L1_attn_ref(x, W_qkv, b_qkv, W_out, b_out):
        import jax, jax.numpy as jnp
        import numpy as np
        HIDDEN = 256
        NUM_HEADS = 16
        HEAD_DIM = HIDDEN // NUM_HEADS
        B, S, H = x.shape
        qkv = x @ W_qkv.T + b_qkv
        q, k, v = jnp.split(qkv, 3, axis=-1)

        def to_heads(t):
            return t.reshape(B, S, NUM_HEADS, HEAD_DIM).transpose(0, 2, 1, 3)
        q, k, v = (to_heads(q), to_heads(k), to_heads(v))
        scale = HEAD_DIM ** (-0.5)
        scores = jnp.einsum('bnqd,bnkd->bnqk', q, k) * scale
        causal = jnp.triu(jnp.ones((S, S), dtype=bool), k=1)
        scores = jnp.where(causal, -jnp.inf, scores)
        attn = jax.nn.softmax(scores, axis=-1)
        out = jnp.einsum('bnqk,bnkd->bnqd', attn, v)
        out = out.transpose(0, 2, 1, 3).reshape(B, S, H)
        return out @ W_out.T + b_out

    def _L1_xattn_ref(x, cond, Wq, bq, Wkv, bkv, Wp, bp):
        import jax, jax.numpy as jnp
        import numpy as np
        D_MODEL = 256
        NUM_HEADS = 16
        HEAD_DIM = D_MODEL // NUM_HEADS

        def _fq_sym(x, axis):
            s = jnp.max(jnp.abs(x), axis=axis, keepdims=True) / 127.0
            s = jnp.maximum(s, 1e-08)
            q = jnp.clip(jnp.round(x / s), -127.0, 127.0) * s
            return x + jax.lax.stop_gradient(q - x)

        def _fq_unsigned(x, axis):
            s = jnp.max(x, axis=axis, keepdims=True) / 255.0
            s = jnp.maximum(s, 1e-08)
            q = jnp.clip(jnp.round(x / s), 0.0, 255.0) * s
            return x + jax.lax.stop_gradient(q - x)
        B, N, C = x.shape
        H, hd = (NUM_HEADS, HEAD_DIM)
        q = (x @ Wq + bq).reshape(1, B * N, H, hd)
        kv = (cond @ Wkv + bkv).reshape(1, -1, 2, H, hd)
        k, v = (kv[:, :, 0], kv[:, :, 1])
        scale = 1.0 / np.sqrt(hd).astype(np.float32)
        q = jnp.transpose(q * scale, (0, 2, 1, 3))
        k = jnp.transpose(k, (0, 2, 1, 3))
        v = jnp.transpose(v, (0, 2, 1, 3))
        q = _fq_sym(q, axis=-1)
        k = _fq_sym(k, axis=-1)
        v = _fq_sym(v, axis=2)
        attn = jnp.einsum('bhqd,bhkd->bhqk', q, k)
        attn = jax.nn.softmax(attn.astype(jnp.float32), axis=-1)
        attn = _fq_unsigned(attn, axis=-1)
        out = jnp.einsum('bhqk,bhkd->bhqd', attn, v)
        out = jnp.transpose(out, (0, 2, 1, 3)).reshape(B, N, C)
        return out @ Wp + bp

    def _L1_ffn_ref(x, gate_w, up_w, down_w, gate_scale, up_scale, down_scale):
        import jax, jax.numpy as jnp
        import numpy as np
        B, S, H, I = (1, 64, 256, 768)

        def _quantized_matmul(x, w, scale):
            wq = w.astype(jnp.float8_e4m3fn).astype(x.dtype)
            y = jnp.einsum('bsi,io->bso', x, wq)
            return y * scale
        gate = jax.nn.silu(_quantized_matmul(x, gate_w, gate_scale))
        up = _quantized_matmul(x, up_w, up_scale)
        fuse = gate * up
        return _quantized_matmul(fuse, down_w, down_scale)
    x = _layernorm(x + _L0_attn_ref(x, L0_attn_w_qkv, L0_attn_w_out, L0_attn_q_norm_w, L0_attn_k_norm_w), axis=-1)
    x = _layernorm(x + _L0_xattn_ref(x, mask_Bx1xSxS_fk0, ctx_2048, L0_xattn_Wq, L0_xattn_Wk, L0_xattn_Wv, L0_xattn_Wo, L0_xattn_gate), axis=-1)
    x = _layernorm(x + _L0_ffn_ref(x, L0_ffn_gate_w, L0_ffn_w_gate, L0_ffn_w_up, L0_ffn_w_down), axis=-1)
    x = _layernorm(x + _L1_attn_ref(x, L1_attn_W_qkv, L1_attn_b_qkv, L1_attn_W_out, L1_attn_b_out), axis=-1)
    x = _layernorm(x + _L1_xattn_ref(x, ctx_2048, L1_xattn_Wq, L1_xattn_bq, L1_xattn_Wkv, L1_xattn_bkv, L1_xattn_Wp, L1_xattn_bp), axis=-1)
    x = _layernorm(x + _L1_ffn_ref(x, L1_ffn_gate_w, L1_ffn_up_w, L1_ffn_down_w, L1_ffn_gate_scale, L1_ffn_up_scale, L1_ffn_down_scale), axis=-1)
    return x

_drawn_inputs = setup_inputs


def setup_inputs(seed=0):
    import zlib

    import numpy as np

    out = dict(_drawn_inputs(seed))
    spreads = {'L0_attn_q_norm_w': (1.0, 0.2),
     'L0_attn_k_norm_w': (1.0, 0.2),
     'L1_attn_b_qkv': (0.0, 0.1),
     'L1_attn_b_out': (0.0, 0.1),
     'L1_xattn_bq': (0.0, 0.8),
     'L1_xattn_bkv': (0.0, 0.275),
     'L1_xattn_bp': (0.0, 0.1)}
    factors = {'ctx_2048': 2.855,
     'L0_xattn_Wq': 8.0,
     'L0_xattn_Wk': 8.0,
     'L0_xattn_gate': 6.321,
     'L1_xattn_Wq': 8.0,
     'L1_xattn_Wkv': 3.058,
     'L1_ffn_gate_scale': 5.332,
     'L1_ffn_up_scale': 6.191,
     'L1_ffn_down_scale': 5.985}
    for name, (base, spread) in spreads.items():
        noise = np.random.default_rng([zlib.crc32(name.encode()), seed]).standard_normal(out[name].shape)
        drawn = base * np.exp(spread * noise) if base else spread * noise
        out[name] = jnp.asarray(drawn.astype(out[name].dtype))
    for name, factor in factors.items():
        out[name] = (out[name] * factor).astype(out[name].dtype)
    return out
```

```python
from contextlib import ExitStack

import numpy as np
import concourse.bass as bass
from concourse import mybir

F32 = mybir.dt.float32
BF16 = mybir.dt.bfloat16
FP8 = mybir.dt.float8e4
U32 = mybir.dt.uint32
ALU = mybir.AluOpType
ACT = mybir.ActivationFunctionType
X = mybir.AxisListType.X
REDUCE_ABSMAX = bass.bass_isa.ReduceOp.absmax

P = 128
TILES = 8
D = 256
KD = D // P
H0, KV0, HD0 = 32, 8, 64
HX, HDX = 32, 8
H1, HD1 = 16, 16
E, F, TOPK = 16, 176, 6
EF = E * F
FB = EF // P
I1 = 768
IB = I1 // P
PAD = 32
STK = 64
GH = 4
EC = 2
ROUND = float(3 << 22)
LN_EPS, RMS_EPS = 1e-5, 1e-6
LN255 = float(np.log(255.0))
FP8_MAX = 240.0

HB = [3] * 6 + [4]
HB0 = [sum(HB[:j]) for j in range(len(HB))]
FBS = [2, 2, 1, 1]
FB0 = [sum(FBS[:j]) for j in range(len(FBS))]
WIDE = 128
GX = HX // GH
G1 = H1 // GH


class Order:

    def __init__(self, keys):
        self.at = {key: n for n, key in enumerate(keys)}
        self.count = len(keys)
        assert self.count % 2 == 0

    def done(self, tile, key):
        return tile * self.count + self.at[key] + 1


T0 = Order([("k0", j) for j in range(2)] + [("q0", j) for j in range(4)] + [("p", g) for g in range(KV0)]
           + [("o0", j) for j in range(4)] + [("ak", j) for j in range(2)] + [("x", 1)]
           + [("qk", j) for j in range(4)] + [("p", KV0 + g) for g in range(2 * GX)] + [("ox", 0), ("x", 2)]
           + [("h", j) for j in range(len(HB))])
T1 = Order([("x", 3)] + [("qk1", j) for j in range(2)] + [("p", g) for g in range(G1)] + [("o1", 0), ("x", 4)]
           + [("qs", 0)] + [("n", h) for h in range(H1)] + [("oq", 0), ("x", 5)] + [("f", j) for j in range(len(FBS))])
P0 = Order(["k", "q0", "q1", "q2", "q3", "v", "out0", "ck", "cv", "qkx", "vx", "outx", "logits", "down"])
P1 = Order(["q1", "k1", "v1", "out1", "q2x", "av2x", "out2x", "down1"])
GROUPS0, GROUPS1 = KV0 + 2 * GX, G1

CHUNKS = E // EC
CW = EC * F
HBATCH = 4 * P
FW = I1 // 2


def head0(g, i):
    return 8 * (g // 2) + g % 2 + 2 * i


def headx(g, i):
    return 4 * (4 * (g % 2) + i) + g // 2


def head1(g, i):
    return 4 * i + g


def h_ready(j):
    return min(CHUNKS - 1, -(-P * (HB0[j] + HB[j]) // CW) - 1)


class Layer:

    def __init__(self, sem, name, transposes, projections, groups, chain):
        self.t, self.p, self.groups, self.steps = transposes, projections, groups, chain
        self.proj = sem(f"proj{name}")
        self.proj_taken = sem(f"proj_taken{name}")
        self.trans = sem(f"trans{name}")
        self.trans_taken = sem(f"trans_taken{name}")
        self.scores = sem(f"scores{name}")
        self.masked = sem(f"masked{name}")
        self.maxed = sem(f"maxed{name}")
        self.shifted = sem(f"shifted{name}")
        self.exped = sem(f"exped{name}")
        self.summed = sem(f"summed{name}")
        self.varied = sem(f"varied{name}")
        self.rstd_ready = sem(f"rstd_ready{name}")
        self.x_ready = sem(f"x_ready{name}")
        self.chain = sem(f"chain{name}")


def decoder(nc, a, mid, out, debug=6):
    ctx = ExitStack()
    with ctx:
        def sb(name, shape, dt=F32):
            return ctx.enter_context(nc.sbuf_tensor(name, shape, dt))

        def ps(name, shape, dt=F32):
            return ctx.enter_context(nc.psum_tensor(name, shape, dt))

        def sem(name):
            return ctx.enter_context(nc.semaphore(name))

        w_qkv0 = sb("w_qkv0", [P, KD, (H0 + 2 * KV0) * HD0])
        w_out0 = sb("w_out0", [P, H0 * HD0 // P, D])
        w_x = sb("w_x", [P, KD, 3 * D])
        w_outx = sb("w_outx", [P, KD, D])
        w_router = sb("w_router", [P, KD, E])
        w_moe = sb("w_moe", [P, 3 * KD * EF])
        w_gate = w_moe[:, 0:KD * EF].rearrange("p (k n) -> p k n", k=KD)
        w_up = w_moe[:, KD * EF:2 * KD * EF].rearrange("p (k n) -> p k n", k=KD)
        w_down = w_moe[:, 2 * KD * EF:3 * KD * EF].rearrange("p (k n) -> p k n", k=FB)

        class Region:

            def __init__(self, ap):
                self.ap, self.at = ap, 0

            def take(self, *dims, dt=F32):
                n = int(np.prod(dims)) // (1 if dt is F32 else 2)
                v = self.ap[:, self.at:self.at + n]
                self.at += n
                if dt is not F32:
                    v = v.bitcast(dt)
                if len(dims) == 1:
                    return v
                names = "abc"[:len(dims)]
                return v.rearrange(f"p ({' '.join(names)}) -> p {' '.join(names)}",
                                   **{c: d for c, d in zip(names[:-1], dims)})

        over = Region(w_qkv0[:].rearrange("p a b -> p (a b)"))
        w_qkv1 = over.take(KD, 3 * D)
        w_out1 = over.take(KD, D)
        w_q2 = over.take(KD, D)
        w_p2 = over.take(KD, D)
        b_qkv1 = over.take(3 * D)
        b_out1, b_q2, b_p2, s_down1 = (over.take(D) for _ in range(4))
        over = Region(w_out0[:].rearrange("p a b -> p (a b)"))
        ffn_gate, ffn_up = over.take(KD * I1), over.take(KD * I1)
        over = Region(w_moe)
        w_gate1 = over.take(KD, I1, dt=BF16)
        w_up1 = over.take(KD, I1, dt=BF16)
        w_down1 = over.take(IB, D, dt=BF16)
        s_gate1, s_up1 = over.take(I1), over.take(I1)
        ffn_down = over.take(IB * D)
        round_low, round_high = over.take(I1, dt=BF16), over.take(I1, dt=BF16)
        round_sel = over.take(KD * I1)
        round_two = over.take(KD * I1, dt=BF16)
        e2 = over.take(2, TILES * P)
        n2 = over.take(2, TILES * P, dt=BF16)
        n2T = over.take(2, TILES * P, dt=BF16)
        stackT = over.take(8, P, dt=BF16)
        x5p = over.take(3, KD, P, dt=BF16)
        fuse = over.take(I1)
        fuseT = over.take(IB, P)
        fusep = over.take(3, IB, P, dt=BF16)
        v1_wide = over.take(H1 * (HD1 + 1) + WIDE - HD1 - 1)
        v1 = v1_wide[:, 0:H1 * (HD1 + 1)].rearrange("p (h d) -> p h d", h=H1)
        q2 = over.take(D)
        max2 = over.take(2, H1)
        assert over.at <= 3 * KD * EF

        ident = sb("ident", [P, P])
        ident_b = sb("ident_b", [P, P], BF16)
        mask_window = sb("mask_window", [P, P])
        mask_causal = sb("mask_causal", [P, P])
        rope_q = sb("rope_q", [P, 2, HD0])
        rope_k = sb("rope_k", [P, 2, HD0])
        rope_x = sb("rope_x", [P, 2, 2, HDX])
        tanh_gate = sb("tanh_gate", [P, HX])
        neg_half = sb("neg_half", [P, 8])
        keys2T = sb("keys2T", [P, H1 // 2, TILES * P], BF16)
        vals2 = sb("vals2", [P, TILES, D], BF16)
        v_scale = sb("v_scale", [P, D])
        xin = sb("xin", [P, D])
        xinT = sb("xinT", [P, KD, P])
        ctxT = sb("ctxT", [P, KD, P])
        mask_in = sb("mask_in", [P, P])
        xa, xb, xc = (sb(n, [P, D]) for n in ("xa", "xb", "xc"))
        xaT, xbT = (sb(n, [P, KD, P]) for n in ("xaT", "xbT"))
        xn = {0: xin, 1: xa, 2: xb, 3: xc}
        xm = {3: xin, 4: xa, 5: xb, 6: xc}
        xT = {0: xinT, 1: xaT, 2: xbT, 3: xinT, 4: xaT, 5: xbT}
        res = sb("res", [P, D])
        stats = sb("stats", [P, 6])
        mean_var = sb("mean_var", [P, 2])
        rstd = sb("rstd", [P, 1])
        carrier = sb("carrier", [P, 1])
        big = sb("big", [P, EF])
        bigT = sb("bigT", [P, FB, P])
        squares = sb("squares", [P, 2, 512])
        ropes = sb("ropes", [P, 3, 512])
        mean_sq = sb("mean_sq", [P, 2, 8])
        rms = sb("rms", [P, 2, 8])
        kdup = sb("kdup", [P, KV0, 2, HD0])
        k0T = sb("k0T", [P, KV0, P])
        nv0, nvx = KV0 * (HD0 + 1), HX * (HDX + 1)
        v_all = sb("v_all", [P, nv0 + 2 * nvx + WIDE])
        v0_wide, vx_wide, avx_wide = v_all[:, 0:], v_all[:, nv0:], v_all[:, nv0 + nvx:]
        v0 = v0_wide[:, 0:KV0 * (HD0 + 1)].rearrange("p (h d) -> p h d", h=KV0)
        probs = sb("probs", [P, 4, 512])
        probsT = sb("probsT", [P, 2, 512])
        row_max = sb("row_max", [P, 4, GH])
        recips = sb("recips", [P, 2, 32])
        qk_pad = big[:, 0:2 * HX * PAD].rearrange("p (h d) -> p h d", d=PAD)
        qkT = bigT[:, 0:16, :]
        ak_pad = kdup[:].rearrange("p a b c -> p (a b c)").rearrange("p (h d) -> p h d", d=PAD)
        akT = k0T
        vx, avx = (w[:, 0:HX * (HDX + 1)].rearrange("p (h d) -> p h d", h=HX) for w in (vx_wide, avx_wide))
        att = sb("att", [P, D])
        attT = sb("attT", [P, KD, P])
        router = sb("router", [P, 7, 20])
        th = squares[:].rearrange("p a b -> p (a b)")[:, 0:2 * CW].rearrange("p (a b) -> p a b", a=2)
        gg = ropes[:].rearrange("p a b -> p (a b)")[:, 0:2 * CW].rearrange("p (a b) -> p a b", a=2)
        qk1_pad = big[:, 0:2 * H1 * PAD].rearrange("p (h d) -> p h d", d=PAD)
        q2s = sb("q2s", [P, 4, H1])
        stack = big[:, 1536:1536 + H1 * STK // 2].bitcast(BF16).rearrange("p (h d) -> p h d", h=H1)
        w_kv2 = big[:, 0:KD * 2 * D].rearrange("p (k n) -> p k n", k=KD)
        b_kv2 = big[:, 1024:1536]
        values = bigT[:].rearrange("p a b -> p (a b)")[:, 0:TILES * D].rearrange("p (t n) -> p t n", t=TILES)

        ps_s = ps("ps_s", [P, 2, 512])
        ps_o = ps("ps_o", [P, 2, 512])
        ps_t = ps("ps_t", [P, 2, 512])
        ps_p = ps("ps_p", [P, 2, 512])

        ld_prep = sem("ld_prep")
        ld_ctx = sem("ld_ctx")
        ld_const = sem("ld_const")
        ld_w = {n: sem(f"ld_{n}") for n in ("qkv0", "att0", "moe", "l1", "ffn", "down1")}
        ld_x = sem("ld_x")
        ld_tilectx = sem("ld_tilectx")
        stored = sem("stored")
        dve_prep = sem("dve_prep")
        dve_done = sem("dve_done")
        act_prep = sem("act_prep")
        pool_prep = sem("pool_prep")
        c_kv = sem("c_kv")
        c_taken = sem("c_taken")
        c_stack = sem("c_stack")
        c_T = sem("c_T")
        c_evac = sem("c_evac")
        c_chain = sem("c_chain")
        c_vals = sem("c_vals")
        c_amax = sem("c_amax")
        squared = sem("squared")
        msq = sem("msq")
        rmsed = sem("rmsed")
        normed = sem("normed")
        out0_ready = sem("out0_ready")
        heads_x = sem("heads_x")
        heads_1 = sem("heads_1")
        heads_2 = sem("heads_2")
        qkx_ready = sem("qkx_ready")
        logit_max = sem("logit_max")
        logit_exp = sem("logit_exp")
        gate_up = sem("gate_up")
        tanhed = sem("tanhed")
        hidden = sem("hidden")
        q2_ready = sem("q2_ready")
        s2 = sem("s2")
        max2_ready = sem("max2_ready")
        exp2 = sem("exp2")
        round2 = sem("round2")
        out2 = sem("out2")
        parts5 = sem("parts5")
        gate_up1 = sem("gate_up1")
        scaled1 = sem("scaled1")
        tanhed1 = sem("tanhed1")
        fused = sem("fused")
        fparts = sem("fparts")

        ld_mid = sem("ld_mid")
        mid_stored = sem("mid_stored")
        L0 = Layer(sem, "0", T0, P0, GROUPS0, CHAIN0)
        L1 = Layer(sem, "1", T1, P1, GROUPS1, CHAIN1)

        block = ctx.enter_context(nc.Block())

        def heads(ap, n):
            return ap.rearrange("p (h d) -> p h d", h=n)

        def row(name, n):
            return a[name].rearrange("(o n) -> o n", o=1).broadcast_to([P, n])

        def two(name):
            return a[name].rearrange("(k p) n -> p k n", p=P)

        @block.sync
        def _(sp):
            sp.dma_start(ident[:], a["ident"]).then_inc(ld_prep, 16)
            sp.dma_start(w_kv2, two("L1_xattn_Wkv"))\
                .then_inc(ld_prep, 16)
            sp.dma_start(b_kv2, row("L1_xattn_bkv", 2 * D)).then_inc(ld_prep, 16)
            sp.dma_start(w_qkv0[:], two("wT_qkv0")).then_inc(ld_w["qkv0"], 16)
            for t, n in ((mask_window, "mask_window"), (mask_causal, "mask_causal")):
                sp.dma_start(t[:], a[n]).then_inc(ld_const, 16)
            sp.dma_start(rope_q[:], a["rope_q"]).then_inc(ld_const, 16)
            sp.dma_start(rope_k[:], a["rope_k"]).then_inc(ld_const, 16)
            sp.dma_start(rope_x[:], a["rope_x"]).then_inc(ld_const, 16)
            sp.dma_start(squares[:, 0, 0:HD0], row("L0_attn_q_norm_w", HD0)).then_inc(ld_const, 16)
            sp.dma_start(squares[:, 1, 0:HD0], row("L0_attn_k_norm_w", HD0)).then_inc(ld_const, 16)
            sp.dma_start(tanh_gate[:], row("gate", HX)).then_inc(ld_const, 16)
            sp.dma_start(xin[:], a["x"][0]).then_inc(ld_x, 16)
            sp.dma_start(xinT[:], a["xT"][0]).then_inc(ld_x, 16)
            for t, src in ((w_out0[:], a["wT_out0"].rearrange("(k p) n -> p k n", p=P)),
                           (w_x[:, :, 0:D], two("L0_xattn_Wq")), (w_x[:, :, D:2 * D], two("L0_xattn_Wk")),
                           (w_x[:, :, 2 * D:3 * D], two("L0_xattn_Wv")),
                           (w_outx[:], two("L0_xattn_Wo"))):
                sp.dma_start(t, src).then_inc(ld_w["att0"], 16)
            sp.wait_ge(c_kv, TILES)
            sp.dma_start(ctxT[:], a["ctxT"][0]).then_inc(ld_tilectx, 16)
            sp.dma_start(mask_in[:], a["mask"][0]).then_inc(ld_tilectx, 16)
            for t, src in ((w_router[:], two("wT_router")), (w_gate, two("wT_gate")), (w_up, two("wT_up")),
                           (w_down, a["wT_down"].rearrange("(k p) n -> p k n", p=P))):
                sp.dma_start(t, src).then_inc(ld_w["moe"], 16)
            sp.sem_inc(mid_stored, 16)
            with sp.Fori(0, TILES - 1) as b:
                sp.wait_ge(L0.x_ready, b * 3 + 1)
                sp.dma_start(xin[:], a["x"][b + 1]).then_inc(ld_x, 16)
                sp.dma_start(xinT[:], a["xT"][b + 1]).then_inc(ld_x, 16)
                sp.wait_ge(L0.x_ready, b * 3 + 2)
                sp.dma_start(ctxT[:], a["ctxT"][b + 1]).then_inc(ld_tilectx, 16)
                sp.dma_start(mask_in[:], a["mask"][b + 1]).then_inc(ld_tilectx, 16)
                sp.wait_ge(L0.x_ready, b * 3 + 3)
                sp.dma_start(mid[b], xn[min(debug, 3)][:]).then_inc(mid_stored, 16)
            sp.wait_ge(L0.x_ready, TILES * 3)
            sp.dma_start(mid[TILES - 1], xn[min(debug, 3)][:]).then_inc(mid_stored, 16)
            if debug <= 3:
                sp.wait_ge(mid_stored, 16 * TILES + 16)
                return
            sp.wait_ge(mid_stored, 16 * TILES + 16)
            sp.dma_start(xin[:], mid[0]).then_inc(ld_mid, 16)
            for t, src in ((w_qkv1, two("wT_qkv1")), (b_qkv1, row("L1_attn_b_qkv", 3 * D)),
                           (w_out1, two("wT_out1")), (w_q2, two("L1_xattn_Wq")), (w_p2, two("L1_xattn_Wp")),
                           (b_out1, row("L1_attn_b_out", D)), (b_q2, row("L1_xattn_bq", D)),
                           (b_p2, row("L1_xattn_bp", D)), (s_gate1, row("L1_ffn_gate_scale", I1)),
                           (s_up1, row("L1_ffn_up_scale", I1)), (s_down1, row("L1_ffn_down_scale", D))):
                sp.dma_start(t, src).then_inc(ld_w["l1"], 16)
            for t, src in ((ffn_gate.rearrange("p (k n) -> p k n", k=KD), two("L1_ffn_gate_w")),
                           (ffn_up.rearrange("p (k n) -> p k n", k=KD), two("L1_ffn_up_w")),
                           (ffn_down.rearrange("p (k n) -> p k n", k=IB),
                            a["L1_ffn_down_w"].rearrange("(k p) n -> p k n", p=P))):
                sp.dma_start(t, src).then_inc(ld_w["ffn"], 16)
            sp.sem_inc(stored, 16)
            with sp.Fori(0, TILES - 1) as b:
                sp.wait_ge(L1.x_ready, b * 3 + 1)
                sp.dma_start(xin[:], mid[b + 1]).then_inc(ld_mid, 16)
                sp.wait_ge(L1.x_ready, b * 3 + 3)
                sp.dma_start(out[b], xm[debug][:]).then_inc(stored, 16)
            sp.wait_ge(L1.x_ready, TILES * 3)
            sp.dma_start(out[TILES - 1], xm[debug][:]).then_inc(stored, 16)
            sp.wait_ge(stored, 16 * TILES + 16)

        @block.gpsimd
        def _(pool):
            nc.gpsimd.memset(neg_half[:], -0.5).then_inc(pool_prep, 1)
            nc.gpsimd.memset(v_all[:], 1.0).then_inc(pool_prep, 1)
            pool.wait_ge(c_vals, 1)
            nc.gpsimd.partition_all_reduce(res[:], att[:], P, REDUCE_ABSMAX).then_inc(c_amax, 1)
            pool.wait_ge(pool_prep, 1)
            with pool.Fori(0, TILES) as b:
                for c in range(5):
                    pool.wait_ge(msq, b * 5 + c + 1)
                    if c >= 2:
                        pool.wait_ge(normed, b * 5 + c - 1)
                    nc.gpsimd.tensor_tensor(rms[:, c % 2, :], mean_sq[:, c % 2, :], neg_half[:], ALU.pow)\
                        .then_inc(rmsed, 1)
                for i in range(3):
                    pool.wait_ge(L0.varied, b * 3 + i + 1)
                    nc.gpsimd.tensor_tensor(rstd[:], mean_var[:, 1:2], neg_half[:, 0:1], ALU.pow)\
                        .then_inc(L0.rstd_ready, 1)
            if debug <= 3:
                return
            with pool.Fori(0, TILES) as b:
                for i in range(3):
                    pool.wait_ge(L1.varied, b * 3 + i + 1)
                    nc.gpsimd.tensor_tensor(rstd[:], mean_var[:, 1:2], neg_half[:, 0:1], ALU.pow)\
                        .then_inc(L1.rstd_ready, 1)

        @block.scalar
        def _(act):
            def stack_evac(j):
                act.wait_ge(c_T, j + 1)
                nc.scalar.activation(keys2T[:, :, bass.ts(j, P)],
                                     ps_t[:, 0, :].bitcast(BF16).rearrange("p (a q) -> p a q", a=8),
                                     ACT.Copy).then_inc(c_evac, 1)

            act.dma_start(ctxT[:], a["ctxT"][0]).then_inc(ld_ctx, 16)
            with act.Fori(0, TILES - 1) as j:
                act.wait_ge(c_kv, j + 1)
                act.dma_start(ctxT[:], a["ctxT"][j + 1]).then_inc(ld_ctx, 16)
                stack_evac(j)
            stack_evac(TILES - 1)
            act.wait_ge(ld_const, 16 * 8)
            nc.scalar.activation(tanh_gate[:], tanh_gate[:], ACT.Tanh).then_inc(act_prep, 1)

            def evac(L, b, key, dst, n=512):
                act.wait_ge(L.trans, L.t.done(b, key))
                src = ps_t[:, L.t.at[key] % 2, 0:n]
                nc.scalar.activation(dst, src.bitcast(BF16) if dst.dtype == BF16 else src, ACT.Copy)\
                    .then_inc(L.trans_taken, 1)

            def flat(ap):
                return ap.rearrange("p a b -> p (a b)")

            def groups(L, b, g0, n, scale=1.0):
                for s in range(n + 2):
                    g = g0 + s
                    if s >= 2:
                        if g - 2 >= 2:
                            act.wait_ge(L.summed, b * L.groups + g - 3)
                        evac(L, b, ("p", g - 2), probsT[:, g % 2, :])
                    if s < n:
                        act.wait_ge(L.shifted, b * L.groups + g + 1)
                        nc.scalar.activation(probs[:, g % 4, :], probs[:, g % 4, :], ACT.Exp, scale=scale)\
                            .then_inc(L.exped, 1)

            with act.Fori(0, TILES) as b:
                def square(c):
                    act.wait_ge(L0.proj, b * P0.count + c + 1)
                    if c >= 2:
                        act.wait_ge(msq, b * 5 + c - 1)
                    nc.scalar.activation(squares[:, c % 2, :], ps_p[:, c % 2, :], ACT.Square).then_inc(squared, 1)

                square(0)
                square(1)
                square(2)
                for j in range(2):
                    evac(L0, b, ("k0", j), flat(k0T[:, 4 * j:4 * j + 4, :]))
                square(3)
                evac(L0, b, ("q0", 0), flat(bigT[:, 0:4, :]))
                square(4)
                for j in range(1, 4):
                    evac(L0, b, ("q0", j), flat(bigT[:, 4 * j:4 * j + 4, :]))
                groups(L0, b, 0, KV0)
                for j in range(4):
                    evac(L0, b, ("o0", j), flat(bigT[:, 4 * j:4 * j + 4, :]))

                for j in range(2):
                    evac(L0, b, ("ak", j), flat(akT[:, 4 * j:4 * j + 4, :]))
                evac(L0, b, ("x", 1), flat(xT[1][:]), D)
                for j in range(4):
                    evac(L0, b, ("qk", j), flat(qkT[:, 4 * j:4 * j + 4, :]))
                groups(L0, b, KV0, 2 * GX)
                evac(L0, b, ("ox", 0), flat(attT[:]), D)
                evac(L0, b, ("x", 2), flat(xT[2][:]), D)

                act.wait_ge(logit_max, b + 1)
                nc.scalar.activation(router[:, 1, 0:E], ps_p[:, P0.at["logits"] % 2, 0:E], ACT.Exp,
                                     bias=router[:, 0, 0:1], accum_out=router[:, 0, 1:2]).then_inc(logit_exp, 1)
                jt = 0
                for c in range(CHUNKS + 2):
                    if c < CHUNKS:
                        act.wait_ge(gate_up, b * CHUNKS + c + 1)
                        if c >= 2:
                            act.wait_ge(hidden, b * CHUNKS + c - 1)
                        nc.scalar.activation(th[:, c % 2, :], (ps_p if c % 2 == 0 else ps_s)[:, 0, 0:CW], ACT.Tanh,
                                             scale=0.5).then_inc(tanhed, 1)
                    while jt < len(HB) and (h_ready(jt) <= c - 2 or c == CHUNKS + 1):
                        n, k = HB[jt], HB0[jt]
                        evac(L0, b, ("h", jt), flat(bigT[:, k:k + n, :]), n * P)
                        jt += 1

            if debug <= 3:
                return
            with act.Fori(0, TILES) as b:
                evac(L1, b, ("x", 3), flat(xT[3][:]), D)
                for j in range(2):
                    evac(L1, b, ("qk1", j), flat(qkT[:, 4 * j:4 * j + 4, :]))
                groups(L1, b, 0, G1, scale=HD1 ** -0.5)
                evac(L1, b, ("o1", 0), flat(attT[:]), D)
                evac(L1, b, ("x", 4), flat(xT[4][:]), D)

                evac(L1, b, ("qs", 0), flat(stackT))
                for h in range(H1 + 2):
                    if h >= 2:
                        if h >= 4:
                            act.wait_ge(out2, b * (H1 - 1) + h - 3)
                        evac(L1, b, ("n", h - 2), n2T[:, h % 2, :])
                    if h < H1:
                        act.wait_ge(max2_ready, b * H1 + h + 1)
                        if h >= 2:
                            act.wait_ge(round2, b * H1 + h - 1)
                        nc.scalar.activation(e2[:, h % 2, :], flat((ps_s if h % 2 == 0 else ps_o)[:]),
                                             ACT.Exp, scale=q2s[:, 0, h:h + 1], bias=max2[:, 1, h:h + 1],
                                             accum_out=q2s[:, 3, h:h + 1]).then_inc(exp2, 1)
                evac(L1, b, ("oq", 0), flat(attT[:]), D)
                evac(L1, b, ("x", 5), flat(xT[5][:]), D)

                for c in range(2):
                    act.wait_ge(scaled1, b * 2 + c + 1)
                    nc.scalar.activation(flat(th)[:, 0:FW], flat(gg)[:, 0:FW], ACT.Tanh, scale=0.5).then_inc(tanhed1, 1)
                for j in range(len(FBS)):
                    evac(L1, b, ("f", j), flat(fuseT[:, FB0[j]:FB0[j] + FBS[j], :]), FBS[j] * P)

        @block.vector
        def _(dve):
            count = [0]

            def step(ins):
                count[0] += 1
                ins.then_inc(dve_prep, 1)
                dve.wait_ge(dve_prep, count[0])

            step(nc.vector.memset(stack, 0.0))

            def quantise(src, dst_int, scales, tmp, link):
                link(nc.vector.tensor_reduce(scales[:, 0, :], heads(src, H1), X, ALU.max, apply_absolute_value=True))
                link(nc.vector.tensor_scalar(scales[:, 0, :], scales[:, 0, :], 1.0 / 127.0, 1e-8, ALU.mult, ALU.max))
                link(nc.vector.reciprocal(scales[:, 1, :], scales[:, 0, :]))
                link(nc.vector.tensor_tensor(heads(tmp, H1), heads(src, H1),
                                             scales[:, 1, :].unsqueeze(2).broadcast_to([P, H1, HD1]), ALU.mult))
                link(nc.vector.tensor_scalar(tmp, tmp, ROUND, ROUND, ALU.add, ALU.subtract))
                link(nc.vector.tensor_scalar(dst_int, tmp, 127.0, -127.0, ALU.min, ALU.max))

            kf, kq, r1, r2 = (ropes[:].rearrange("p a b -> p (a b)")[:, i * D:(i + 1) * D] for i in range(4))
            CH = 12
            dve.wait_ge(ld_prep, 16 * 3)
            step(nc.vector.tensor_copy(ident_b[:], ident[:]))
            with dve.Fori(0, TILES) as j:
                n = [0]

                def clink(ins):
                    n[0] += 1
                    ins.then_inc(c_chain, 1)
                    dve.wait_ge(c_chain, j * CH + n[0])

                dve.wait_ge(c_kv, j + 1)
                clink(nc.vector.tensor_tensor(kf, ps_p[:, 0, 0:D], b_kv2[:, 0:D], ALU.add))
                nc.vector.tensor_tensor(values[:, j, :], ps_p[:, 0, D:2 * D], b_kv2[:, D:2 * D], ALU.add)\
                    .then_inc(c_taken, 1)
                quantise(kf, kq, q2s, kq, clink)
                clink(nc.vector.tensor_tensor(heads(kf, H1), heads(kq, H1),
                                              q2s[:, 0, :].unsqueeze(2).broadcast_to([P, H1, HD1]), ALU.mult))
                clink(nc.vector.tensor_copy(stack[:, :, 0:16], heads(kf, H1)))
                clink(nc.vector.tensor_tensor(heads(r1, H1), heads(kf, H1), stack[:, :, 0:16], ALU.subtract))
                clink(nc.vector.tensor_copy(stack[:, :, 16:32], heads(r1, H1)))
                clink(nc.vector.tensor_tensor(heads(r2, H1), heads(r1, H1), stack[:, :, 16:32], ALU.subtract))
                nc.vector.tensor_copy(stack[:, :, 32:48], heads(r2, H1)).then_inc(c_stack, 1)
                assert n[0] == CH
                dve.wait_ge(c_T, j + 1)

            dve.wait_ge(c_taken, TILES)
            nc.vector.tensor_reduce(att[:], values.rearrange("p t n -> p n t"), X, ALU.max,
                                    apply_absolute_value=True).then_inc(c_vals, 1)
            dve.wait_ge(c_amax, 1)
            step(nc.vector.tensor_scalar(v_scale[:], res[:], 1.0 / 127.0, 1e-8, ALU.mult, ALU.max))
            step(nc.vector.reciprocal(att[:], v_scale[:]))
            step(nc.vector.tensor_tensor(values, values, att[:].unsqueeze(1).broadcast_to([P, TILES, D]),
                                         ALU.mult))
            step(nc.vector.tensor_scalar(values, values, ROUND, ROUND, ALU.add, ALU.subtract))
            step(nc.vector.tensor_scalar(vals2[:], values, 127.0, -127.0, ALU.min, ALU.max))

            dve.wait_ge(ld_const, 16 * 8)
            half = HD0 // 2
            for t, wrow in ((rope_q, squares[:, 0, 0:HD0]), (rope_k, squares[:, 1, 0:HD0])):
                step(nc.vector.tensor_tensor(t[:, 0, :], t[:, 0, :], wrow, ALU.mult))
                step(nc.vector.tensor_tensor(t[:, 1, 0:half], t[:, 1, 0:half], wrow[:, half:HD0], ALU.mult))
                step(nc.vector.tensor_tensor(t[:, 1, half:HD0], t[:, 1, half:HD0], wrow[:, 0:half], ALU.mult))

            dve.wait_ge(pool_prep, 2)
            dve.wait_ge(act_prep, 1)
            nc.vector.memset(row_max[:], 0.0).then_inc(dve_done, 1)

            n = [0]

            def link(L, b, ins):
                n[0] += 1
                ins.then_inc(L.chain, 1)
                dve.wait_ge(L.chain, b * L.steps + n[0])

            def carry_wait():
                nc.vector.memset(carrier[:], 0.0)

            def bank(L, key, w=512):
                return ps_p[:, L.p.at[key] % 2, 0:w]

            def taken(L, b, key, ins):
                ins.then_inc(L.proj_taken, 1)
                dve.wait_ge(L.proj_taken, L.p.done(b, key))

            def normalise(L, b, i, key, src, dst, add=None, scale=None):
                dve.wait_ge(L.proj, L.p.done(b, key))
                if scale is not None:
                    taken(L, b, key, nc.vector.tensor_tensor(res[:], bank(L, key, D), scale, ALU.mult))
                    link(L, b, nc.vector.tensor_tensor(res[:], res[:], src[:], ALU.add))
                else:
                    taken(L, b, key, nc.vector.tensor_tensor(res[:], bank(L, key, D), src[:], ALU.add))
                if add is not None:
                    link(L, b, nc.vector.tensor_tensor(res[:], res[:], add, ALU.add))
                link(L, b, nc.vector.bn_stats(stats[:], res[:]))
                carry_wait()
                link(L, b, nc.vector.bn_aggr(mean_var[:], stats[:]))
                nc.vector.tensor_scalar(mean_var[:, 1:2], mean_var[:, 1:2], LN_EPS, None, ALU.add)\
                    .then_inc(L.varied, 1)
                dve.wait_ge(L.rstd_ready, b * 3 + i + 1)
                nc.vector.tensor_scalar(dst[:], res[:], mean_var[:, 0:1], rstd[:], ALU.subtract, ALU.mult)\
                    .then_inc(L.x_ready, 1)

            def group_step(L, b, g0, count, mask, s):
                g = g0 + s
                if s < count:
                    dve.wait_ge(L.scores, b * L.groups + g + 1)
                    if g >= 4:
                        dve.wait_ge(L.trans, L.t.done(b, ("p", g - 4)))
                    p = heads(probs[:, g % 4, :], GH)
                    if mask is not None:
                        nc.vector.tensor_tensor(p, heads(ps_s[:, g % 2, :], GH),
                                                mask.unsqueeze(1).broadcast_to([P, GH, P]), ALU.add)\
                            .then_inc(L.masked, 1)
                    else:
                        nc.vector.tensor_copy(p, heads(ps_s[:, g % 2, :], GH)).then_inc(L.masked, 1)
                if s >= 1:
                    q = heads(probs[:, (g - 1) % 4, :], GH)
                    dve.wait_ge(L.maxed, b * L.groups + g)
                    nc.vector.tensor_tensor(q, q, row_max[:, (g - 1) % 4, :].unsqueeze(2)
                                            .broadcast_to([P, GH, P]), ALU.subtract).then_inc(L.shifted, 1)
                if s < count:
                    dve.wait_ge(L.masked, b * L.groups + g + 1)
                    nc.vector.tensor_reduce(row_max[:, g % 4, :], p, X, ALU.max).then_inc(L.maxed, 1)

            with dve.Fori(0, TILES) as b:
                n[0] = 0
                half = HD0 // 2

                def rotate(c):
                    table = rope_k if c == 0 else rope_q
                    src = heads(ps_p[:, c % 2, :], 8)
                    t1, t2 = heads(ropes[:, c % 2, :], 8), heads(ropes[:, 2, :], 8)
                    dve.wait_ge(squared, b * 5 + c + 1)
                    if c >= 2:
                        dve.wait_ge(normed, b * 5 + c - 1)
                    if c >= 1:
                        dve.wait_ge(L0.proj_taken, b * P0.count + c)
                    nc.vector.tensor_tensor(t1, src, table[:, 0, :].unsqueeze(1).broadcast_to([P, 8, HD0]), ALU.mult)
                    nc.vector.tensor_tensor(t2[:, :, 0:half], src[:, :, half:HD0],
                                            table[:, 1, 0:half].unsqueeze(1).broadcast_to([P, 8, half]), ALU.mult)
                    link(L0, b, nc.vector.tensor_tensor(t2[:, :, half:HD0], src[:, :, 0:half],
                                                 table[:, 1, half:HD0].unsqueeze(1).broadcast_to([P, 8, half]),
                                                 ALU.mult))
                    nc.vector.tensor_tensor(t1, t1, t2, ALU.add).then_inc(L0.proj_taken, 1)
                    if c >= 2:
                        dve.wait_ge(rmsed, b * 5 + c - 1)
                    link(L0, b, nc.vector.tensor_reduce(mean_sq[:, c % 2, :], heads(squares[:, c % 2, :], 8), X, ALU.add))
                    nc.vector.tensor_scalar(mean_sq[:, c % 2, :], mean_sq[:, c % 2, :], 1.0 / HD0, RMS_EPS,
                                            ALU.mult, ALU.add).then_inc(msq, 1)

                def scale_heads(c):
                    dve.wait_ge(rmsed, b * 5 + c + 1)
                    dve.wait_ge(L0.proj_taken, b * P0.count + c + 1)
                    r = rms[:, c % 2, :].unsqueeze(2).broadcast_to([P, 8, HD0])
                    t1 = heads(ropes[:, c % 2, :], 8)
                    if c == 0:
                        nc.vector.tensor_tensor(kdup[:, :, 0, :], t1, r, ALU.mult)
                        nc.vector.tensor_tensor(kdup[:, :, 1, :], t1, r, ALU.mult).then_inc(normed, 1)
                    else:
                        nc.vector.tensor_tensor(heads(big[:, 512 * (c - 1):512 * c], 8), t1, r, ALU.mult)\
                            .then_inc(normed, 1)

                for c in range(6):
                    if c < 5:
                        rotate(c)
                    if c >= 1:
                        scale_heads(c - 1)
                dve.wait_ge(L0.proj, L0.p.done(b, "v"))
                nc.vector.tensor_copy(v0[:, :, 0:HD0], heads(bank(L0, "v"), KV0)).then_inc(L0.proj_taken, 1)

                def out0_norm(g):
                    dve.wait_ge(L0.summed, b * GROUPS0 + g + 1)
                    o = heads(ps_o[:, g % 2, :], GH)
                    if g >= 2:
                        dve.wait_ge(out0_ready, b * KV0 + g - 1)
                    r = recips[:, g % 2, 0:GH]
                    link(L0, b, nc.vector.reciprocal(r, o[:, :, HD0]))
                    nc.vector.tensor_tensor(heads(big[:, 512 * (g // 2):512 * (g // 2 + 1)], 8)[:, g % 2::2, :], o[:, :, 0:HD0],
                                            r.unsqueeze(2).broadcast_to([P, GH, HD0]), ALU.mult)\
                        .then_inc(out0_ready, 1)

                for s in range(KV0 + 1):
                    group_step(L0, b, 0, KV0, mask_window[:], s)
                    if s >= 4:
                        out0_norm(s - 4)
                for g in range(KV0 - 3, KV0):
                    out0_norm(g)

                dve.wait_ge(ld_tilectx, b * 32 + 32)
                link(L0, b, nc.vector.tensor_scalar(mask_in[:], mask_in[:], float(np.finfo(np.float32).min), None, ALU.max))
                if debug <= 3:
                    dve.wait_ge(mid_stored, b * 16 + 16)
                normalise(L0, b, 0, "out0", xin, xa)
                dve.wait_ge(L0.proj, P0.done(b, "ck"))
                nc.vector.tensor_copy(ak_pad[:, :, 0:HDX], heads(bank(L0, "ck", D), HX)).then_inc(L0.proj_taken, 1)
                dve.wait_ge(L0.proj, P0.done(b, "cv"))
                nc.vector.tensor_copy(avx[:, :, 0:HDX], heads(bank(L0, "cv", D), HX)).then_inc(L0.proj_taken, 1)

                hh = HDX // 2
                dve.wait_ge(L0.proj, L0.p.done(b, "qkx"))
                src = bank(L0, "qkx").rearrange("p (s h d) -> p s h d", s=2, h=HX)
                t1 = ropes[:, 0, :].rearrange("p (s h d) -> p s h d", s=2, h=HX)
                t2 = ropes[:, 1, :].rearrange("p (s h d) -> p s h d", s=2, h=HX)
                for s in range(2):
                    nc.vector.tensor_tensor(t1[:, s], src[:, s], rope_x[:, 0, s, :].unsqueeze(1)
                                            .broadcast_to([P, HX, HDX]), ALU.mult)
                    nc.vector.tensor_tensor(t2[:, s, :, 0:hh], src[:, s, :, hh:HDX], rope_x[:, 1, s, 0:hh].unsqueeze(1)
                                            .broadcast_to([P, HX, hh]), ALU.mult)
                    ins = nc.vector.tensor_tensor(t2[:, s, :, hh:HDX], src[:, s, :, 0:hh], rope_x[:, 1, s, hh:HDX]
                                                  .unsqueeze(1).broadcast_to([P, HX, hh]), ALU.mult)
                ins.then_inc(L0.proj_taken, 1)
                dve.wait_ge(L0.proj_taken, L0.p.done(b, "qkx"))
                nc.vector.tensor_tensor(qk_pad[:, :, 0:HDX], heads(ropes[:, 0, :], 2 * HX),
                                        heads(ropes[:, 1, :], 2 * HX), ALU.add).then_inc(qkx_ready, 1)
                dve.wait_ge(L0.proj, L0.p.done(b, "vx"))
                nc.vector.tensor_copy(vx[:, :, 0:HDX], heads(bank(L0, "vx", D), HX)).then_inc(L0.proj_taken, 1)
                for s in range(GX + 1):
                    group_step(L0, b, KV0, GX, mask_in[:], s)
                for s in range(GX + 1):
                    group_step(L0, b, KV0 + GX, GX, None, s)
                wx = HX * (HDX + 1)
                o1, o2 = (ps_o[:, i, 0:wx].rearrange("p (a m d) -> p m a d", a=4, d=HDX + 1) for i in range(2))

                def hx(ap):
                    return ap.rearrange("p (m a d) -> p m a d", a=4, d=HDX)

                def rx(i):
                    return recips[:, i, :].rearrange("p (m a) -> p m a", a=4)

                dve.wait_ge(L0.summed, b * GROUPS0 + GROUPS0)
                link(L0, b, nc.vector.reciprocal(rx(0), o1[:, :, :, HDX]))
                link(L0, b, nc.vector.reciprocal(rx(1), o2[:, :, :, HDX]))
                link(L0, b, nc.vector.tensor_tensor(recips[:, 1, :], recips[:, 1, :], tanh_gate[:], ALU.mult))
                link(L0, b, nc.vector.tensor_tensor(hx(att[:]), o1[:, :, :, 0:HDX],
                                             rx(0).unsqueeze(3).broadcast_to([P, HX // 4, 4, HDX]), ALU.mult))
                link(L0, b, nc.vector.tensor_tensor(hx(res[:]), o2[:, :, :, 0:HDX],
                                             rx(1).unsqueeze(3).broadcast_to([P, HX // 4, 4, HDX]), ALU.mult))
                nc.vector.tensor_tensor(att[:], att[:], res[:], ALU.add).then_inc(heads_x, 1)
                normalise(L0, b, 1, "outx", xa, xb)

                dve.wait_ge(L0.proj, L0.p.done(b, "logits"))
                lg = bank(L0, "logits", E)
                nc.vector.tensor_reduce(router[:, 0, 0:1], lg, X, ALU.max, negate=True).then_inc(logit_max, 1)
                dve.wait_ge(logit_exp, b + 1)
                nc.vector.reciprocal(router[:, 0, 2:3], router[:, 0, 1:2]).then_inc(L0.proj_taken, 1)
                dve.wait_ge(L0.proj_taken, L0.p.done(b, "logits"))
                link(L0, b, nc.vector.memset(router[:, 2, E:E + 1], -1.0))
                link(L0, b, nc.vector.memset(router[:, 2, E + 1:E + 2], -2.0))
                link(L0, b, nc.vector.tensor_scalar(router[:, 2, 0:E], router[:, 1, 0:E], router[:, 0, 2:3], None, ALU.mult))
                carry_wait()
                link(L0, b, nc.vector.max(router[:, 3, 0:8], router[:, 2, 0:E]))
                link(L0, b, nc.vector.tensor_copy(router[:, 3, TOPK:8], router[:, 2, E:E + 2]))
                carry_wait()
                link(L0, b, nc.vector.match_replace(router[:, 4, 0:E + 2], router[:, 3, 0:8], router[:, 2, 0:E + 2], -3.0))
                link(L0, b, nc.vector.tensor_scalar(router[:, 5, 0:E], router[:, 4, 0:E], -3.0, 0.5, ALU.is_equal, ALU.mult))
                link(L0, b, nc.vector.tensor_tensor(router[:, 6, 0:E], router[:, 5, 0:E], router[:, 2, 0:E], ALU.mult))
                for c in range(CHUNKS):
                    g = (ps_p if c % 2 == 0 else ps_s)[:, 0, 0:CW]
                    u = (ps_p if c % 2 == 0 else ps_s)[:, 1, 0:CW]
                    dve.wait_ge(tanhed, b * CHUNKS + c + 1)
                    link(L0, b, nc.vector.scalar_tensor_tensor(gg[:, c % 2, :], th[:, c % 2, :], 1.0, g, ALU.add, ALU.mult))
                    for e in range(EC):
                        ins = nc.vector.scalar_tensor_tensor(
                            big[:, c * CW + e * F:c * CW + (e + 1) * F], gg[:, c % 2, e * F:(e + 1) * F],
                            router[:, 6, c * EC + e:c * EC + e + 1], u[:, e * F:(e + 1) * F], ALU.mult, ALU.mult)
                    ins.then_inc(hidden, 1)
                dve.wait_ge(mid_stored, b * 16 + 16)
                normalise(L0, b, 2, "down", xb, xc)
                assert n[0] == CHAIN0, n[0]

            if debug <= 3:
                return

            dve.wait_ge(ld_w["ffn"], 16 * 3)
            step(nc.vector.memset(v1_wide, 1.0))
            step(nc.vector.memset(stack, 0.0))
            for src, dst, w in ((ffn_gate, w_gate1, KD * I1), (ffn_up, w_up1, KD * I1), (ffn_down, w_down1, IB * D)):
                dst = dst.rearrange("p a b -> p (a b)")
                f8a, f8b = round_low.bitcast(FP8)[:, 0:w], round_high.bitcast(FP8)[:, 0:w]
                step(nc.vector.tensor_scalar(f8a, src, FP8_MAX, -FP8_MAX, ALU.min, ALU.max, saturate=False))
                step(nc.vector.tensor_scalar(f8b, src, 0.5, None, ALU.mult, saturate=False))
                step(nc.vector.tensor_scalar(round_sel.bitcast(U32)[:, 0:w], src.bitcast(U32), 1, 31,
                                             ALU.logical_shift_left, ALU.logical_shift_right))
                step(nc.vector.tensor_copy(dst, f8a))
                step(nc.vector.tensor_scalar(round_two[:, 0:w], f8b, 2.0, None, ALU.mult))
                step(nc.vector.copy_predicated(dst, round_sel.bitcast(U32)[:, 0:w], round_two[:, 0:w]))

            with dve.Fori(0, TILES) as b:
                n[0] = 0
                dve.wait_ge(ld_w["l1"], 16 * 11)
                for i, key in enumerate(("q1", "k1")):
                    dve.wait_ge(L1.proj, P1.done(b, key))
                    nc.vector.tensor_tensor(qk1_pad[:, H1 * i:H1 * (i + 1), 0:HD1], heads(bank(L1, key, D), H1),
                                            heads(b_qkv1[:, D * i:D * (i + 1)], H1), ALU.add)\
                        .then_inc(L1.proj_taken, 1)
                dve.wait_ge(L1.proj, L1.p.done(b, "v1"))
                nc.vector.tensor_tensor(v1[:, :, 0:HD1], heads(bank(L1, "v1", D), H1),
                                        heads(b_qkv1[:, 2 * D:3 * D], H1), ALU.add).then_inc(L1.proj_taken, 1)
                for s in range(G1 + 1):
                    group_step(L1, b, 0, G1, mask_causal[:], s)
                o1 = ps_o[:, 0, 0:H1 * (HD1 + 1)].rearrange("p (a m d) -> p m a d", a=4, d=HD1 + 1)
                r1x = recips[:, 0, 0:H1].rearrange("p (m a) -> p m a", a=4)
                dve.wait_ge(L1.summed, b * GROUPS1 + GROUPS1)
                link(L1, b, nc.vector.reciprocal(r1x, o1[:, :, :, HD1]))
                nc.vector.tensor_tensor(att[:].rearrange("p (m a d) -> p m a d", a=4, d=HD1), o1[:, :, :, 0:HD1],
                                        r1x.unsqueeze(3).broadcast_to([P, H1 // 4, 4, HD1]), ALU.mult)\
                    .then_inc(heads_1, 1)
                normalise(L1, b, 0, "out1", xin, xa, add=b_out1)

                dve.wait_ge(L1.proj, L1.p.done(b, "q2x"))
                nc.vector.tensor_tensor(q2, bank(L1, "q2x", D), b_q2, ALU.add).then_inc(L1.proj_taken, 1)
                dve.wait_ge(L1.proj_taken, L1.p.done(b, "q2x"))
                link(L1, b, nc.vector.tensor_scalar(q2, q2, HD1 ** -0.5, None, ALU.mult))
                quantise(q2, q2, q2s, q2, lambda ins: link(L1, b, ins))
                link(L1, b, nc.vector.tensor_scalar(q2s[:, 2, :], q2s[:, 0, :], -1.0, None, ALU.mult))
                for part in range(3):
                    ins = nc.vector.tensor_copy(stack[:, :, 16 * part:16 * part + 16], heads(q2, H1))
                ins.then_inc(q2_ready, 1)
                for h in range(H1 + 1):
                    if h < H1:
                        dve.wait_ge(s2, b * H1 + h + 1)
                        link(L1, b, nc.vector.tensor_reduce(max2[:, 0, h:h + 1],
                                                     (ps_s if h % 2 == 0 else ps_o)[:].rearrange("p a b -> p (a b)"),
                                                     X, ALU.max))
                        nc.vector.tensor_scalar(max2[:, 1, h:h + 1], max2[:, 0, h:h + 1], q2s[:, 2, h:h + 1], LN255,
                                                ALU.mult, ALU.add).then_inc(max2_ready, 1)
                    if h >= 1:
                        dve.wait_ge(exp2, b * H1 + h)
                        if h >= 3:
                            dve.wait_ge(L1.trans, T1.done(b, ("n", h - 3)))
                        nc.vector.tensor_scalar(n2[:, (h - 1) % 2, :], e2[:, (h - 1) % 2, :], ROUND, ROUND,
                                                ALU.add, ALU.subtract).then_inc(round2, 1)
                dve.wait_ge(L1.proj, L1.p.done(b, "av2x"))
                link(L1, b, nc.vector.reciprocal(recips[:, 0, 0:H1], q2s[:, 3, :]))
                nc.vector.tensor_tensor(heads(att[:], H1), heads(bank(L1, "av2x", D), H1),
                                        recips[:, 0, 0:H1].unsqueeze(2).broadcast_to([P, H1, HD1]), ALU.mult)\
                    .then_inc(L1.proj_taken, 1)
                dve.wait_ge(L1.proj_taken, L1.p.done(b, "av2x"))
                nc.vector.tensor_tensor(att[:], att[:], v_scale[:], ALU.mult).then_inc(heads_2, 1)
                normalise(L1, b, 1, "out2x", xa, xb, add=b_p2)

                def split(src, parts, tmp):
                    link(L1, b, nc.vector.tensor_copy(parts[0], src))
                    link(L1, b, nc.vector.tensor_tensor(tmp, src, parts[0], ALU.subtract))
                    link(L1, b, nc.vector.tensor_copy(parts[1], tmp))
                    return nc.vector.tensor_tensor(parts[2], tmp, parts[1], ALU.subtract)

                dve.wait_ge(L1.trans_taken, T1.done(b, ("x", 5)))
                r = res[:].rearrange("p (k q) -> p k q", k=KD)
                split(xT[5][:], [x5p[:, i] for i in range(3)], r).then_inc(parts5, 1)
                gs = gg.rearrange("p a b -> p (a b)")[:, 0:FW]
                tt = th.rearrange("p a b -> p (a b)")[:, 0:FW]
                us = ropes[:].rearrange("p a b -> p (a b)")[:, 2 * CW:2 * CW + FW]
                for c in range(2):
                    cols = slice(c * FW, (c + 1) * FW)
                    gp, up = (ps_p if c == 0 else ps_s)[:, 0, 0:FW], (ps_p if c == 0 else ps_s)[:, 1, 0:FW]
                    dve.wait_ge(gate_up1, b * 2 + c + 1)
                    if c:
                        dve.wait_ge(fused, b * 2 + c)
                    nc.vector.tensor_tensor(gs, gp, s_gate1[:, cols], ALU.mult).then_inc(scaled1, 1)
                    link(L1, b, nc.vector.tensor_tensor(us, up, s_up1[:, cols], ALU.mult))
                    dve.wait_ge(tanhed1, b * 2 + c + 1)
                    link(L1, b, nc.vector.scalar_tensor_tensor(gs, tt, 1.0, gs, ALU.add, ALU.mult))
                    nc.vector.scalar_tensor_tensor(fuse[:, cols], gs, 0.5, us, ALU.mult, ALU.mult).then_inc(fused, 1)
                for j, (k, w) in enumerate(zip(FB0, FBS)):
                    dve.wait_ge(L1.trans_taken, T1.done(b, ("f", j)))
                    if j:
                        dve.wait_ge(fparts, b * len(FBS) + j)
                    split(fuseT[:, k:k + w, :], [fusep[:, i, k:k + w, :] for i in range(3)], r[:, 0:w, :])\
                        .then_inc(fparts, 1)
                dve.wait_ge(stored, b * 16 + 16)
                normalise(L1, b, 2, "down1", xb, xc, scale=s_down1)
                assert n[0] == CHAIN1, n[0]

        @block.tensor
        def _(pe):
            pe.wait_ge(ld_prep, 16 * 3)
            with pe.Fori(0, TILES) as j:
                pe.wait_ge(ld_ctx, j * 16 + 16)
                for k in range(KD):
                    ins = nc.tensor.matmul(ps_p[:, 0, :], ctxT[:, k, :], w_kv2[:, k, :], start=(k == 0), stop=(k == KD - 1))
                ins.then_inc(c_kv, 1)
                pe.wait_ge(c_stack, j + 1)
                for i in range(8):
                    ins = nc.tensor.transpose(ps_t[:, 0, :].bitcast(BF16)[:, i * P:(i + 1) * P],
                                              stack[:, 2 * i:2 * i + 2, :].rearrange("p a b -> p (a b)"), ident_b[:])
                ins.then_inc(c_T, 1)
                pe.wait_ge(c_taken, j + 1)
                pe.wait_ge(c_evac, j + 1)
            pe.wait_ge(dve_done, 1)
            pe.wait_ge(ld_w["qkv0"], 16)

            def project(L, b, key, xTi, w, col, width):
                n = L.p.at[key]
                if n >= 2:
                    pe.wait_ge(L.proj_taken, b * L.p.count + n - 1)
                kk = w.shape[1]
                for k in range(kk):
                    ins = nc.tensor.matmul(ps_p[:, n % 2, 0:width], xTi[:, k, :], w[:, k, col:col + width],
                                           start=(k == 0), stop=(k == kk - 1))
                ins.then_inc(L.proj, 1)

            def transpose(L, b, key, src, nblocks, bf=False):
                t = L.t.at[key]
                if t >= 2:
                    pe.wait_ge(L.trans_taken, b * L.t.count + t - 1)
                dst = ps_t[:, t % 2, :].bitcast(BF16) if bf else ps_t[:, t % 2, :]
                for i in range(nblocks):
                    ins = nc.tensor.transpose(dst[:, i * P:(i + 1) * P], src(i), ident_b[:] if bf else ident[:])
                ins.then_inc(L.trans, 1)

            def group_scores(L, b, g, q, k):
                if g >= 2:
                    pe.wait_ge(L.masked, b * L.groups + g - 1)
                for i in range(GH):
                    ins = nc.tensor.matmul(ps_s[:, g % 2, i * P:(i + 1) * P], q(i), k(i), start=True, stop=True)
                ins.then_inc(L.scores, 1)

            def group_transpose(L, b, g):
                pe.wait_ge(L.exped, b * L.groups + g + 1)
                transpose(L, b, ("p", g), lambda i: probs[:, g % 4, i * P:(i + 1) * P], GH)

            def group_sum(L, b, g, dst, v):
                pe.wait_ge(L.trans_taken, L.t.done(b, ("p", g)))
                for i in range(GH):
                    ins = nc.tensor.matmul(dst(i), probsT[:, g % 2, i * P:(i + 1) * P], v(i), start=True, stop=True)
                ins.then_inc(L.summed, 1)

            def wide(ap, n, w):
                return ap[:, n * w:n * w + WIDE]

            def x_transpose(L, b, i, x):
                transpose(L, b, ("x", i), lambda k: x[:, k * P:(k + 1) * P], KD)
                pe.wait_ge(L.trans_taken, L.t.done(b, ("x", i)))

            def padded(ap, first):
                return ap[:, first:first + 4, :].rearrange("p a b -> p (a b)")

            with pe.Fori(0, TILES) as b:
                pe.wait_ge(ld_x, b * 32 + 32)
                nq = H0 * HD0
                project(L0, b, "k", xT[0], w_qkv0, nq, 512)
                project(L0, b, "q0", xT[0], w_qkv0, 0, 512)
                project(L0, b, "q1", xT[0], w_qkv0, 512, 512)
                pe.wait_ge(normed, b * 5 + 1)
                for j in range(2):
                    transpose(L0, b, ("k0", j), lambda i: kdup[:, 4 * j + i].rearrange("p a b -> p (a b)"), 4)
                project(L0, b, "q2", xT[0], w_qkv0, 1024, 512)

                def q0_transpose(j):
                    pe.wait_ge(normed, b * 5 + j + 2)
                    transpose(L0, b, ("q0", j), lambda i: big[:, (4 * j + i) * P:(4 * j + i + 1) * P], 4)

                q0_transpose(0)
                project(L0, b, "q3", xT[0], w_qkv0, 1536, 512)
                q0_transpose(1)
                project(L0, b, "v", xT[0], w_qkv0, nq + 512, 512)
                q0_transpose(2)
                q0_transpose(3)
                pe.wait_ge(L0.trans_taken, L0.t.done(b, ("q0", 3)))
                pe.wait_ge(L0.proj_taken, L0.p.done(b, "v"))

                def rows(i):
                    return slice(HD0 * (i % 2), HD0 * (i % 2) + HD0)

                for s in range(KV0 + 3):
                    if s < KV0:
                        group_scores(L0, b, s, lambda i: bigT[rows(s), head0(s, i) // 2, :],
                                     lambda i: k0T[rows(s), head0(s, i) // 4, :])
                    if 2 <= s < KV0 + 2:
                        group_transpose(L0, b, s - 2)
                    if s >= 3:
                        g = s - 3
                        if g >= 2:
                            pe.wait_ge(out0_ready, b * KV0 + g - 1)
                        group_sum(L0, b, g, lambda i: ps_o[:, g % 2, i * WIDE:(i + 1) * WIDE],
                                  lambda i: wide(v0_wide, head0(g, i) // 4, HD0 + 1))
                for j in range(4):
                    pe.wait_ge(out0_ready, b * KV0 + 2 * j + 2)
                    transpose(L0, b, ("o0", j), lambda i: big[:, (4 * j + i) * P:(4 * j + i + 1) * P], 4)
                pe.wait_ge(L0.trans_taken, L0.t.done(b, ("o0", 3)))
                pe.wait_ge(ld_w["att0"], 16 * 5)
                project(L0, b, "out0", bigT, w_out0, 0, D)

                pe.wait_ge(ld_tilectx, b * 32 + 32)
                project(L0, b, "ck", ctxT, w_x, D, D)
                project(L0, b, "cv", ctxT, w_x, 2 * D, D)
                pe.wait_ge(L0.proj_taken, P0.done(b, "ck"))
                for j in range(2):
                    transpose(L0, b, ("ak", j), lambda i: padded(ak_pad, 16 * j + 4 * i), 4)
                pe.wait_ge(L0.x_ready, b * 3 + 1)
                x_transpose(L0, b, 1, xa)
                project(L0, b, "qkx", xT[1], w_x, 0, 2 * D)
                project(L0, b, "vx", xT[1], w_x, 2 * D, D)
                pe.wait_ge(qkx_ready, b + 1)
                for j in range(4):
                    transpose(L0, b, ("qk", j), lambda i: padded(qk_pad, 16 * j + 4 * i), 4)
                pe.wait_ge(L0.trans_taken, L0.t.done(b, ("qk", 3)))
                pe.wait_ge(L0.proj_taken, L0.p.done(b, "vx"))
                gx, g0 = GX, KV0
                for s in range(2 * gx + 3):
                    if s < 2 * gx:
                        keysT, m = (qkT[:, 8:16, :], s) if s < gx else (akT, s - gx)
                        r = slice(PAD * (m // 2), PAD * (m // 2) + HDX)
                        group_scores(L0, b, g0 + s, lambda i: qkT[r, headx(m, i) // 4, :],
                                     lambda i: keysT[r, headx(m, i) // 4, :])
                    if 2 <= s < 2 * gx + 2:
                        group_transpose(L0, b, g0 + s - 2)
                    if s >= 3:
                        g = s - 3
                        vv, m, w = (vx_wide if g < gx else avx_wide), g % gx, HDX + 1
                        group_sum(L0, b, g0 + g, lambda i: wide(ps_o[:, g // gx, :], GH * m + i, w),
                                  lambda i: wide(vv, headx(m, i), w))
                pe.wait_ge(heads_x, b + 1)
                transpose(L0, b, ("ox", 0), lambda k: att[:, k * P:(k + 1) * P], KD)
                pe.wait_ge(L0.trans_taken, L0.t.done(b, ("ox", 0)))
                project(L0, b, "outx", attT, w_outx, 0, D)

                pe.wait_ge(L0.x_ready, b * 3 + 2)
                x_transpose(L0, b, 2, xb)
                pe.wait_ge(ld_w["moe"], 16 * 4)
                project(L0, b, "logits", xT[2], w_router, 0, E)
                pe.wait_ge(L0.proj_taken, L0.p.done(b, "logits"))
                down = P0.at["down"]

                def h_transpose(j):
                    nb, k0 = HB[j], HB0[j]
                    pe.wait_ge(hidden, b * CHUNKS + h_ready(j) + 1)
                    transpose(L0, b, ("h", j), lambda i: big[:, (k0 + i) * P:(k0 + i + 1) * P], nb)

                jt = 0
                for c in range(CHUNKS):
                    if c >= 2:
                        pe.wait_ge(hidden, b * CHUNKS + c - 1)
                    bank = ps_p if c % 2 == 0 else ps_s
                    for half, w in ((0, w_gate), (1, w_up)):
                        for k in range(KD):
                            ins = nc.tensor.matmul(bank[:, half, 0:CW], xT[2][:, k, :], w[:, k, c * CW:(c + 1) * CW],
                                                   start=(k == 0), stop=(k == KD - 1))
                    ins.then_inc(gate_up, 1)
                    while jt < len(HB) and h_ready(jt) <= c - 2:
                        h_transpose(jt)
                        jt += 1
                while jt < len(HB):
                    h_transpose(jt)
                    jt += 1
                for k in range(FB):
                    if k in HB0:
                        pe.wait_ge(L0.trans_taken, T0.done(b, ("h", HB0.index(k))))
                    ins = nc.tensor.matmul(ps_p[:, down % 2, 0:D], bigT[:, k, :], w_down[:, k, :], start=(k == 0),
                                           stop=(k == FB - 1))
                ins.then_inc(L0.proj, 1)
                pe.wait_ge(L0.x_ready, b * 3 + 3)

            if debug <= 3:
                return
            with pe.Fori(0, TILES) as b:
                pe.wait_ge(ld_mid, b * 16 + 16)
                x_transpose(L1, b, 3, xin)
                pe.wait_ge(ld_w["l1"], 16 * 11)
                for i, key in enumerate(("q1", "k1", "v1")):
                    project(L1, b, key, xT[3], w_qkv1, i * D, D)
                pe.wait_ge(L1.proj_taken, P1.done(b, "k1"))
                for j in range(2):
                    transpose(L1, b, ("qk1", j), lambda i: padded(qk1_pad, 16 * j + 4 * i), 4)
                pe.wait_ge(L1.trans_taken, L1.t.done(b, ("qk1", 1)))
                pe.wait_ge(L1.proj_taken, L1.p.done(b, "v1"))
                g0, g1 = 0, G1
                for s in range(g1 + 3):
                    if s < g1:
                        group_scores(L1, b, g0 + s, lambda i: qkT[PAD * s:PAD * s + HD1, head1(s, i) // 4, :],
                                     lambda i: qkT[PAD * s:PAD * s + HD1, 4 + head1(s, i) // 4, :])
                    if 2 <= s < g1 + 2:
                        group_transpose(L1, b, g0 + s - 2)
                    if s >= 3:
                        g = s - 3
                        w = HD1 + 1
                        group_sum(L1, b, g0 + g, lambda i: wide(ps_o[:, 0, :], GH * g + i, w),
                                  lambda i: wide(v1_wide, head1(g, i), w))
                pe.wait_ge(heads_1, b + 1)
                transpose(L1, b, ("o1", 0), lambda k: att[:, k * P:(k + 1) * P], KD)
                pe.wait_ge(L1.trans_taken, L1.t.done(b, ("o1", 0)))
                project(L1, b, "out1", attT, w_out1, 0, D)

                pe.wait_ge(L1.x_ready, b * 3 + 1)
                x_transpose(L1, b, 4, xa)
                project(L1, b, "q2x", xT[4], w_q2, 0, D)
                pe.wait_ge(q2_ready, b + 1)
                transpose(L1, b, ("qs", 0), lambda i: stack[:, 2 * i:2 * i + 2, :].rearrange("p a b -> p (a b)"), 8, bf=True)
                pe.wait_ge(L1.trans_taken, L1.t.done(b, ("qs", 0)))
                av = P1.at["av2x"]
                pe.wait_ge(L1.proj_taken, b * P1.count + av - 1)
                for s in range(H1 + 3):
                    if s < H1:
                        bank = ps_s if s % 2 == 0 else ps_o
                        r = slice(STK * (s % 2), STK * (s % 2) + 3 * HD1)
                        if s >= 2:
                            pe.wait_ge(exp2, b * H1 + s - 1)
                        for i in range(2):
                            ins = nc.tensor.matmul(bank[:, i, :], stackT[r, s // 2, :],
                                                   keys2T[r, s // 2, i * 512:(i + 1) * 512], start=True, stop=True)
                        ins.then_inc(s2, 1)
                    if 2 <= s < H1 + 2:
                        h = s - 2
                        pe.wait_ge(round2, b * H1 + h + 1)
                        transpose(L1, b, ("n", h), lambda i: n2[:, h % 2, i * P:(i + 1) * P], 8, bf=True)
                    if s >= 3:
                        h = s - 3
                        pe.wait_ge(L1.trans_taken, L1.t.done(b, ("n", h)))
                        for i in range(TILES):
                            ins = nc.tensor.matmul(ps_p[:, av % 2, h * HD1:(h + 1) * HD1],
                                                   n2T[:, h % 2, i * P:(i + 1) * P],
                                                   vals2[:, i, h * HD1:(h + 1) * HD1], start=(i == 0), stop=(i == TILES - 1))
                        ins.then_inc(out2 if h < H1 - 1 else L1.proj, 1)
                pe.wait_ge(heads_2, b + 1)
                transpose(L1, b, ("oq", 0), lambda k: att[:, k * P:(k + 1) * P], KD)
                pe.wait_ge(L1.trans_taken, L1.t.done(b, ("oq", 0)))
                project(L1, b, "out2x", attT, w_p2, 0, D)

                pe.wait_ge(L1.x_ready, b * 3 + 2)
                transpose(L1, b, ("x", 5), lambda k: xb[:, k * P:(k + 1) * P], KD)
                pe.wait_ge(parts5, b + 1)
                pe.wait_ge(L1.proj_taken, L1.p.done(b, "out2x"))
                for c in range(2):
                    bank = ps_p if c == 0 else ps_s
                    for half, w in ((0, w_gate1), (1, w_up1)):
                        for k in range(KD):
                            for part in range(3):
                                ins = nc.tensor.matmul(bank[:, half, 0:FW], x5p[:, part, k, :],
                                                       w[:, k, c * FW:(c + 1) * FW], start=(k + part == 0),
                                                       stop=(k == KD - 1 and part == 2))
                    ins.then_inc(gate_up1, 1)
                for j, (k, w) in enumerate(zip(FB0, FBS)):
                    pe.wait_ge(fused, b * 2 + (1 if j == 0 else 2))
                    transpose(L1, b, ("f", j), lambda i: fuse[:, (k + i) * P:(k + i + 1) * P], w)
                d1 = P1.at["down1"]
                for k in range(IB):
                    if k in FB0:
                        pe.wait_ge(fparts, b * len(FBS) + FB0.index(k) + 1)
                    for part in range(3):
                        ins = nc.tensor.matmul(ps_p[:, d1 % 2, 0:D], fusep[:, part, k, :], w_down1[:, k, :],
                                               start=(k + part == 0), stop=(k == IB - 1 and part == 2))
                ins.then_inc(L1.proj, 1)
                pe.wait_ge(L1.x_ready, b * 3 + 3)


CHAIN0, CHAIN1 = 46, 54

_OUT = (TILES, P, D)
_DIRECT = ["L0_attn_q_norm_w", "L0_attn_k_norm_w", "L0_xattn_Wq", "L0_xattn_Wk", "L0_xattn_Wv", "L0_xattn_Wo",
           "L1_attn_b_qkv", "L1_attn_b_out", "L1_xattn_Wq", "L1_xattn_bq", "L1_xattn_Wkv", "L1_xattn_bkv",
           "L1_xattn_Wp", "L1_xattn_bp", "L1_ffn_gate_w", "L1_ffn_up_w", "L1_ffn_down_w", "L1_ffn_gate_scale",
           "L1_ffn_up_scale", "L1_ffn_down_scale"]


def constants():
    pos = np.arange(P, dtype=np.float32)

    def tables(d):
        inv = (1.0 / 10000.0 ** (np.arange(0, d, 2, dtype=np.float32) / d)).astype(np.float32)
        ang = pos[:, None] * inv[None, :]
        ang = np.concatenate([ang, ang], -1)
        sign = np.where(np.arange(d) < d // 2, -1.0, 1.0).astype(np.float32)
        return np.stack([np.cos(ang), np.sin(ang) * sign], 1).astype(np.float32)

    c = {"ident": np.eye(P, dtype=np.float32)}
    q, k = np.arange(P)[:, None], np.arange(P)[None, :]
    c["mask_causal"] = np.where(q >= k, 0.0, -1e30).astype(np.float32)
    c["mask_window"] = np.where((q >= k) & (q - k < 64), 0.0, -1e30).astype(np.float32)
    c["rope_k"] = tables(HD0)
    c["rope_q"] = (tables(HD0) * np.float32(HD0 ** -0.5)).astype(np.float32)
    x = tables(HDX)
    c["rope_x"] = np.stack([x * np.float32(HDX ** -0.5), x], 2).astype(np.float32)
    return c


def lay_out(inputs):
    g = {n: np.asarray(v) for n, v in inputs.items()}

    def tiles_T(x):
        return np.ascontiguousarray(x.reshape(TILES, P, KD, P).transpose(0, 3, 2, 1))

    arrays = {n: np.ascontiguousarray(g[n]) for n in _DIRECT}
    arrays["x"] = np.ascontiguousarray(g["x"])
    arrays["xT"] = tiles_T(g["x"])
    arrays["ctxT"] = tiles_T(g["ctx_2048"])
    arrays["mask"] = np.ascontiguousarray(g["mask_Bx1xSxS_fk0"].reshape(TILES, P, P))
    arrays["gate"] = np.ascontiguousarray(g["L0_xattn_gate"].reshape(HX))
    arrays["wT_qkv0"] = np.ascontiguousarray(g["L0_attn_w_qkv"].T)
    arrays["wT_out0"] = np.ascontiguousarray(g["L0_attn_w_out"].T)
    arrays["wT_router"] = np.ascontiguousarray(g["L0_ffn_gate_w"].T)
    arrays["wT_gate"] = np.ascontiguousarray(g["L0_ffn_w_gate"].reshape(EF, D).T)
    arrays["wT_up"] = np.ascontiguousarray(g["L0_ffn_w_up"].reshape(EF, D).T)
    arrays["wT_down"] = np.ascontiguousarray(g["L0_ffn_w_down"].transpose(0, 2, 1).reshape(EF, D))
    arrays["wT_qkv1"] = np.ascontiguousarray(g["L1_attn_W_qkv"].T)
    arrays["wT_out1"] = np.ascontiguousarray(g["L1_attn_W_out"].T)
    arrays.update(constants())
    return arrays


def build(nc, arrays, debug=6):
    a = {n: nc.dram_tensor(f"in_{n}", v.shape, mybir.dt.from_np(v.dtype), kind="ExternalInput").ap()
         for n, v in arrays.items()}
    out = nc.dram_tensor("out_0", _OUT, F32, kind="ExternalOutput").ap()
    mid = nc.dram_tensor("mid", _OUT, F32, kind="Internal").ap() if debug > 3 else out
    decoder(nc, a, mid, out, debug)


def kernel(**inputs):
    import concourse.bacc as bacc
    from concourse.bass_utils import run_bass_kernel_spmd

    arrays = lay_out(inputs)
    nc = bacc.Bacc("TRN2", target_bir_lowering=False, num_devices=1)
    build(nc, arrays)
    r = run_bass_kernel_spmd(nc, [{f"in_{n}": v for n, v in arrays.items()}], core_ids=[0])
    return r.results[0]["out_0"]
```

```python
from contextlib import ExitStack

import numpy as np
import concourse.bass as bass
from concourse import mybir

F32 = mybir.dt.float32
BF16 = mybir.dt.bfloat16
FP8 = mybir.dt.float8e4
U32 = mybir.dt.uint32
ALU = mybir.AluOpType
ACT = mybir.ActivationFunctionType
X = mybir.AxisListType.X
REDUCE_ABSMAX = bass.bass_isa.ReduceOp.absmax

P = 128
TILES = 8
D = 256
KD = D // P
H0, KV0, HD0 = 32, 8, 64
HX, HDX = 32, 8
H1, HD1 = 16, 16
E, F, TOPK = 16, 176, 6
EF = E * F
FB = EF // P
I1 = 768
IB = I1 // P
PAD = 32
STK = 64
GH = 4
EC = 2
ROUND = float(3 << 22)
LN_EPS, RMS_EPS = 1e-5, 1e-6
LN255 = float(np.log(255.0))
FP8_MAX = 240.0

HB = [3] * 6 + [4]
HB0 = [sum(HB[:j]) for j in range(len(HB))]
FBS = [2, 2, 1, 1]
FB0 = [sum(FBS[:j]) for j in range(len(FBS))]
WARM = 20
WIDE = 128
GX = HX // GH
G1 = H1 // GH


class Order:

    def __init__(self, keys):
        self.at = {key: n for n, key in enumerate(keys)}
        self.count = len(keys)
        assert self.count % 2 == 0

    def done(self, tile, key):
        return tile * self.count + self.at[key] + 1


T0 = Order([("k0", j) for j in range(2)] + [("q0", j) for j in range(4)] + [("p", g) for g in range(KV0)]
           + [("o0", j) for j in range(4)] + [("ak", j) for j in range(2)] + [("x", 1)]
           + [("qk", j) for j in range(4)] + [("p", KV0 + g) for g in range(2 * GX)] + [("ox", 0), ("x", 2)]
           + [("h", j) for j in range(len(HB))] + [("c", 0), ("c", 1)])
STEPS = {"qkv": ([("x", 3), ("qk1", 0), ("qk1", 1)], ["q1", "k1", "v1"]),
         "heads": ([("p", g) for g in range(G1)], []),
         "out": ([("o1", 0)], ["out1"]),
         "query": ([("x", 4), ("qs", 0)], ["q2x"]),
         "shared": ([("n", h) for h in range(H1)], ["av2x"]),
         "mix": ([("oq", 0)], ["out2x"]),
         "gate": ([("x", 5)], []),
         "down": ([("f", j) for j in range(len(FBS))], ["down1"])}
SCHEDULE = [("qkv", 0), ("qkv", 1), ("heads", 0), ("out", 0), ("heads", 1), ("query", 0), ("out", 1), ("shared", 0),
            ("query", 1), ("mix", 0), ("shared", 1), ("gate", 0), ("mix", 1), ("down", 0), ("gate", 1), ("down", 1)]
NORM_OF = {"out": 0, "mix": 1, "down": 2}
LANES = 2
PAIRS = TILES // LANES
T1 = Order([(key, lane) for step, lane in SCHEDULE for key in STEPS[step][0]])
P0 = Order(["k", "q0", "q1", "q2", "q3", "v", "out0", "ck", "cv", "k2", "v2", "qkx", "vx", "outx", "logits", "down"])
P1 = Order([(key, lane) for step, lane in SCHEDULE for key in STEPS[step][1]])
GROUPS0, GROUPS1 = KV0 + 2 * GX, LANES * G1

CHUNKS = E // EC
CW = EC * F
HBATCH = 4 * P
FW = I1 // 2


def head0(g, i):
    return 8 * (g // 2) + g % 2 + 2 * i


def headx(g, i):
    return 4 * (4 * (g % 2) + i) + g // 2


def head1(g, i):
    return 4 * i + g


def h_ready(j):
    return min(CHUNKS - 1, -(-P * (HB0[j] + HB[j]) // CW) - 1)


class Layer:

    def __init__(self, sem, name, transposes, projections, groups, chain, group_key):
        self.t, self.p, self.groups, self.steps, self.group_key = transposes, projections, groups, chain, group_key
        self.proj = sem(f"proj{name}")
        self.proj_taken = sem(f"proj_taken{name}")
        self.trans = sem(f"trans{name}")
        self.trans_taken = sem(f"trans_taken{name}")
        self.scores = sem(f"scores{name}")
        self.masked = sem(f"masked{name}")
        self.maxed = sem(f"maxed{name}")
        self.shifted = sem(f"shifted{name}")
        self.exped = sem(f"exped{name}")
        self.summed = sem(f"summed{name}")
        self.chain = sem(f"chain{name}")


class Norms:

    def __init__(self, sem, name, res, stats, mean_var, rstd):
        self.res, self.stats, self.mean_var, self.rstd = res, stats, mean_var, rstd
        self.varied = sem(f"varied{name}")
        self.rstd_ready = sem(f"rstd_ready{name}")
        self.x_ready = sem(f"x_ready{name}")


class Lane(Norms):

    def __init__(self, sem, i, norms, xin, xinT, xa, xaT, xb, xbT, xc, qk_pad, qkT, v_wide, att, attT, stack,
                 stackT, q2, q2s, max2, x5p, fuse, fuseT, fusep):
        super().__init__(sem, f"_lane{i}", *norms)
        self.i = i
        self.x = {3: xin, 4: xa, 5: xb, 6: xc}
        self.xT = {3: xinT, 4: xaT, 5: xbT}
        self.qk_pad, self.qkT, self.v_wide, self.att, self.attT = qk_pad, qkT, v_wide, att, attT
        self.v = v_wide[:, 0:H1 * (HD1 + 1)].rearrange("p (h d) -> p h d", h=H1)
        self.stack, self.stackT, self.q2, self.q2s, self.max2 = stack, stackT, q2, q2s, max2
        self.x5p, self.fuse, self.fuseT, self.fusep = x5p, fuse, fuseT, fusep

        def lane(name):
            return sem(f"{name}_lane{i}")

        self.ld_mid, self.stored = lane("ld_mid"), lane("stored")
        self.heads_1 = lane("heads_1")
        self.heads_2 = lane("heads_2")
        self.q2_ready = lane("q2_ready")
        self.s2 = lane("s2")
        self.max2_ready = lane("max2_ready")
        self.exp2 = lane("exp2")
        self.round2 = lane("round2")
        self.out2 = lane("out2")
        self.parts5 = lane("parts5")
        self.gate_up1 = lane("gate_up1")
        self.scaled1 = lane("scaled1")
        self.tanhed1 = lane("tanhed1")
        self.fused = lane("fused")
        self.fparts = lane("fparts")


def decoder(nc, a, mid, keys_dram, values_dram, out, debug=6):
    ctx = ExitStack()
    with ctx:
        def sb(name, shape, dt=F32):
            return ctx.enter_context(nc.sbuf_tensor(name, shape, dt))

        def ps(name, shape, dt=F32):
            return ctx.enter_context(nc.psum_tensor(name, shape, dt))

        def sem(name):
            return ctx.enter_context(nc.semaphore(name))

        w_qkv0 = sb("w_qkv0", [P, KD, (H0 + 2 * KV0) * HD0])
        w_out0 = sb("w_out0", [P, H0 * HD0 // P, D])
        w_x = sb("w_x", [P, KD, 3 * D])
        w_outx = sb("w_outx", [P, KD, D])
        w_router = sb("w_router", [P, KD, E])
        w_moe = sb("w_moe", [P, 3 * KD * EF])
        w_gate = w_moe[:, 0:KD * EF].rearrange("p (k n) -> p k n", k=KD)
        w_up = w_moe[:, KD * EF:2 * KD * EF].rearrange("p (k n) -> p k n", k=KD)
        w_down = w_moe[:, 2 * KD * EF:3 * KD * EF].rearrange("p (k n) -> p k n", k=FB)

        class Region:

            def __init__(self, ap):
                self.ap, self.at = ap, 0

            def take(self, *dims, dt=F32):
                n = int(np.prod(dims)) // (1 if dt is F32 else 2)
                v = self.ap[:, self.at:self.at + n]
                self.at += n
                if dt is not F32:
                    v = v.bitcast(dt)
                if len(dims) == 1:
                    return v
                names = "abc"[:len(dims)]
                return v.rearrange(f"p ({' '.join(names)}) -> p {' '.join(names)}",
                                   **{c: d for c, d in zip(names[:-1], dims)})

        over = Region(w_qkv0[:].rearrange("p a b -> p (a b)"))
        w_qkv1 = over.take(KD, 3 * D)
        w_out1 = over.take(KD, D)
        w_q2 = over.take(KD, D)
        w_p2 = over.take(KD, D)
        b_qkv1 = over.take(3 * D)
        b_out1, b_q2, b_p2, s_down1 = (over.take(D) for _ in range(4))
        over = Region(w_out0[:].rearrange("p a b -> p (a b)"))
        ffn_gate, ffn_up = over.take(KD * I1), over.take(KD * I1)
        over = Region(w_moe)
        w_gate1 = over.take(KD, I1, dt=BF16)
        w_up1 = over.take(KD, I1, dt=BF16)
        w_down1 = over.take(IB, D, dt=BF16)
        s_gate1, s_up1 = over.take(I1), over.take(I1)
        e2 = over.take(2, TILES * P)
        values = e2.rearrange("p a b -> p (a b)").rearrange("p (t n) -> p t n", t=TILES)
        n2 = over.take(2, TILES * P, dt=BF16)
        n2T = over.take(2, TILES * P, dt=BF16)
        words = IB * D + I1 + KD * I1 + KD * I1 // 2
        rounding = Region(over.take(words))
        ffn_down = rounding.take(IB * D)
        round_low, round_high = rounding.take(I1, dt=BF16), rounding.take(I1, dt=BF16)
        round_sel = rounding.take(KD * I1)
        round_two = rounding.take(KD * I1, dt=BF16)
        assert rounding.at == words
        rounding.at = 0
        rest = Region(w_moe[:, over.at:])

        ident = sb("ident", [P, P])
        ident_b = sb("ident_b", [P, P], BF16)
        mask_window = sb("mask_window", [P, P])
        mask_causal = sb("mask_causal", [P, P])
        rope_q = sb("rope_q", [P, 2, HD0])
        rope_k = sb("rope_k", [P, 2, HD0])
        rope_x = sb("rope_x", [P, 2, 2, HDX])
        tanh_gate = sb("tanh_gate", [P, HX])
        neg_half = sb("neg_half", [P, 8])
        keys2T = sb("keys2T", [P, TILES, H1 // 2, P], BF16)
        over = Region(keys2T[:].rearrange("p a b c -> p (a b c)").bitcast(F32))
        w_kv2 = over.take(KD, 2 * D)
        b_kv2 = over.take(2 * D)
        key_stack = over.take(H1, STK, dt=BF16)
        key_stackT = over.take(8, P, dt=BF16)
        value_tile = over.take(D)
        kf, kq, r1, r2 = (over.take(D) for _ in range(4))
        key_scale = over.take(2, H1)
        vals2 = sb("vals2", [P, TILES, D], BF16)
        v_scale = sb("v_scale", [P, D])
        xin = sb("xin", [P, D])
        xinT = sb("xinT", [P, KD, P])
        ctxT = sb("ctxT", [P, KD, P])
        mask_in = sb("mask_in", [P, P])
        xa, xb, xc = (sb(n, [P, D]) for n in ("xa", "xb", "xc"))
        xaT, xbT = (sb(n, [P, KD, P]) for n in ("xaT", "xbT"))
        xn = {0: xin, 1: xa, 2: xb, 3: xc}
        xT = {0: xinT, 1: xaT, 2: xbT}
        res = sb("res", [P, D])
        stats = sb("stats", [P, 6])
        mean_var = sb("mean_var", [P, 2])
        rstd = sb("rstd", [P, 1])
        carrier = sb("carrier", [P, 1])
        big = sb("big", [P, EF])
        bigT = sb("bigT", [P, FB, P])
        squares = sb("squares", [P, 2, 512])
        ropes = sb("ropes", [P, 3, 512])
        mean_sq = sb("mean_sq", [P, 2, 8])
        rms = sb("rms", [P, 2, 8])
        kdup = sb("kdup", [P, KV0, 2, HD0])
        k0T = sb("k0T", [P, KV0, P])
        nv0, nvx = KV0 * (HD0 + 1), HX * (HDX + 1)
        v_all = sb("v_all", [P, nv0 + 2 * nvx + WIDE])
        v0_wide, vx_wide, avx_wide = v_all[:, 0:], v_all[:, nv0:], v_all[:, nv0 + nvx:]
        v0 = v0_wide[:, 0:KV0 * (HD0 + 1)].rearrange("p (h d) -> p h d", h=KV0)
        probs = sb("probs", [P, 4, 512])
        probsT = sb("probsT", [P, 2, 512])
        row_max = sb("row_max", [P, 4, GH])
        recips = sb("recips", [P, 2, 32])
        qk_pad = big[:, 0:2 * HX * PAD].rearrange("p (h d) -> p h d", d=PAD)
        qkT = bigT[:, 0:16, :]
        ak_pad = kdup[:].rearrange("p a b c -> p (a b c)").rearrange("p (h d) -> p h d", d=PAD)
        akT = k0T
        vx, avx = (w[:, 0:HX * (HDX + 1)].rearrange("p (h d) -> p h d", h=HX) for w in (vx_wide, avx_wide))
        att = sb("att", [P, D])
        attT = sb("attT", [P, KD, P])
        router = sb("router", [P, 7, 20])
        th = squares[:].rearrange("p a b -> p (a b)")[:, 0:2 * CW].rearrange("p (a b) -> p a b", a=2)
        gg = ropes[:].rearrange("p a b -> p (a b)")[:, 0:2 * CW].rearrange("p (a b) -> p a b", a=2)
        q2s = sb("q2s", [P, 4, H1])
        stack = big[:, 1536:1536 + H1 * STK // 2].bitcast(BF16).rearrange("p (h d) -> p h d", h=H1)
        ps_s = ps("ps_s", [P, 2, 512])
        ps_o = ps("ps_o", [P, 2, 512])
        ps_t = ps("ps_t", [P, 2, 512])
        ps_p = ps("ps_p", [P, 2, 512])

        ld_prep = sem("ld_prep")
        ld_const = sem("ld_const")
        ld_w = {n: sem(f"ld_{n}") for n in ("k0", "qkv0", "att0", "moe", "l1", "scales1", "ffn", "down1")}
        ld_x = sem("ld_x")
        ld_tilectx = sem("ld_tilectx")
        dve_prep = sem("dve_prep")
        dve_done = sem("dve_done")
        pair_done = sem("pair_done")
        tile_done = sem("tile_done")
        act_prep = sem("act_prep")
        pool_prep = sem("pool_prep")
        c_stack = sem("c_stack")
        v_scaled = sem("v_scaled")
        v_quantised = sem("v_quantised")
        keys_stored = sem("keys_stored")
        values_stored = sem("values_stored")
        ld_keys = sem("ld_keys")
        ld_values = sem("ld_values")
        c_vals = sem("c_vals")
        c_amax = sem("c_amax")
        squared = sem("squared")
        msq = sem("msq")
        rmsed = sem("rmsed")
        normed = sem("normed")
        out0_ready = sem("out0_ready")
        heads_x = sem("heads_x")
        qkx_ready = sem("qkx_ready")
        logit_max = sem("logit_max")
        logit_exp = sem("logit_exp")
        gate_up = sem("gate_up")
        tanhed = sem("tanhed")
        hidden = sem("hidden")

        mid_stored = sem("mid_stored")
        L0 = Layer(sem, "0", T0, P0, GROUPS0, CHAIN0, lambda g: ("p", g))
        L1 = Layer(sem, "1", T1, P1, GROUPS1, CHAIN1, lambda g: (("p", g % G1), g // G1))
        N0 = Norms(sem, "0", res, stats, mean_var, rstd)

        nv1 = H1 * (HD1 + 1) + WIDE - HD1 - 1

        def pads(ap):
            return ap.rearrange("p (h d) -> p h d", d=PAD)

        def stack_of(ap):
            return ap.bitcast(BF16).rearrange("p (h d) -> p h d", h=H1)

        spare = Region(bigT[:, 8:, :].rearrange("p a b -> p (a b)"))
        freed = Region(w_out0[:].rearrange("p a b -> p (a b)"))
        lanes = [
            Lane(sem, 0, (res[:], stats[:], mean_var[:], rstd[:]), xin[:], xinT[:], xa[:], xaT[:], xb[:],
                 xbT[:], xc[:], qk_pad=pads(big[:, 0:2 * H1 * PAD]), qkT=bigT[:, 0:8, :], att=att[:], attT=attT[:],
                 stack=stack, stackT=rest.take(8, P, dt=BF16), q2=rest.take(D), q2s=q2s, max2=rest.take(2, H1),
                 x5p=rest.take(3, KD, P, dt=BF16), fuse=rest.take(I1), fuseT=rest.take(IB, P),
                 fusep=rest.take(3, IB, P, dt=BF16), v_wide=rest.take(nv1)),
            Lane(sem, 1, (rounding.take(D), rounding.take(6), rounding.take(2), rounding.take(1)),
                 spare.take(D), spare.take(KD, P), rounding.take(D), rounding.take(KD, P), rounding.take(D),
                 rounding.take(KD, P), rounding.take(D), qk_pad=pads(freed.take(2 * H1 * PAD)), qkT=spare.take(8, P),
                 att=rounding.take(D), attT=rounding.take(KD, P), stack=stack_of(rounding.take(H1 * STK // 2)),
                 stackT=rounding.take(8, P, dt=BF16), q2=rounding.take(D), q2s=rounding.take(4, H1),
                 max2=rounding.take(2, H1), x5p=freed.take(3, KD, P, dt=BF16), fuse=freed.take(I1),
                 fuseT=freed.take(IB, P), fusep=freed.take(3, IB, P, dt=BF16), v_wide=rounding.take(nv1))]
        for region in (rest, rounding, spare, freed):
            assert region.at <= region.ap.shape[-1]

        block = ctx.enter_context(nc.Block())

        def heads(ap, n):
            return ap.rearrange("p (h d) -> p h d", h=n)

        def row(name, n):
            return a[name].rearrange("(o n) -> o n", o=1).broadcast_to([P, n])

        def two(name):
            return a[name].rearrange("(k p) n -> p k n", p=P)

        @block.sync
        def _(sp):
            sp.dma_start(ident[:], a["ident"]).then_inc(ld_prep, 16)
            sp.dma_start(w_kv2, two("L1_xattn_Wkv"))\
                .then_inc(ld_prep, 16)
            sp.dma_start(b_kv2, row("L1_xattn_bkv", 2 * D)).then_inc(ld_prep, 16)
            nq = H0 * HD0
            sp.dma_start(w_qkv0[:, :, nq:nq + 512], two("wT_qkv0")[:, :, nq:nq + 512]).then_inc(ld_w["k0"], 16)
            sp.dma_start(xin[:], a["x"][0]).then_inc(ld_x, 16)
            sp.dma_start(xinT[:], a["xT"][0]).then_inc(ld_x, 16)
            sp.dma_start(w_qkv0[:, :, 0:nq], two("wT_qkv0")[:, :, 0:nq]).then_inc(ld_w["qkv0"], 16)
            sp.dma_start(w_qkv0[:, :, nq + 512:], two("wT_qkv0")[:, :, nq + 512:]).then_inc(ld_w["qkv0"], 16)
            for t, n in ((mask_window, "mask_window"), (mask_causal, "mask_causal")):
                sp.dma_start(t[:], a[n]).then_inc(ld_const, 16)
            sp.dma_start(rope_q[:], a["rope_q"]).then_inc(ld_const, 16)
            sp.dma_start(rope_k[:], a["rope_k"]).then_inc(ld_const, 16)
            sp.dma_start(rope_x[:], a["rope_x"]).then_inc(ld_const, 16)
            sp.dma_start(squares[:, 0, 0:HD0], row("L0_attn_q_norm_w", HD0)).then_inc(ld_const, 16)
            sp.dma_start(squares[:, 1, 0:HD0], row("L0_attn_k_norm_w", HD0)).then_inc(ld_const, 16)
            sp.dma_start(tanh_gate[:], row("gate", HX)).then_inc(ld_const, 16)
            for t, src in ((w_out0[:], a["wT_out0"].rearrange("(k p) n -> p k n", p=P)),
                           (w_x[:, :, 0:D], two("L0_xattn_Wq")), (w_x[:, :, D:2 * D], two("L0_xattn_Wk")),
                           (w_x[:, :, 2 * D:3 * D], two("L0_xattn_Wv")),
                           (w_outx[:], two("L0_xattn_Wo"))):
                sp.dma_start(t, src).then_inc(ld_w["att0"], 16)
            sp.dma_start(ctxT[:], a["ctxT"][0]).then_inc(ld_tilectx, 16)
            sp.dma_start(mask_in[:], a["mask"][0]).then_inc(ld_tilectx, 16)
            for t, src in ((w_router[:], two("wT_router")), (w_gate, two("wT_gate")), (w_up, two("wT_up")),
                           (w_down, a["wT_down"].rearrange("(k p) n -> p k n", p=P))):
                sp.dma_start(t, src).then_inc(ld_w["moe"], 16)
            sp.sem_inc(mid_stored, 16)
            sp.sem_inc(keys_stored, 16)
            sp.sem_inc(values_stored, 16)

            def store_context(b):
                sp.wait_ge(L0.proj_taken, L0.p.done(b, "v2"))
                sp.dma_start(values_dram[b], value_tile).then_inc(values_stored, 16)

            def store_keys(b):
                sp.wait_ge(L0.trans_taken, L0.t.done(b, ("c", 1)))
                sp.dma_start(keys_dram[b], key_stackT).then_inc(keys_stored, 16)

            with sp.Fori(0, TILES - 1) as b:
                sp.wait_ge(N0.x_ready, b * 3 + 1)
                sp.dma_start(xin[:], a["x"][b + 1]).then_inc(ld_x, 16)
                sp.dma_start(xinT[:], a["xT"][b + 1]).then_inc(ld_x, 16)
                store_context(b)
                sp.wait_ge(N0.x_ready, b * 3 + 2)
                sp.dma_start(ctxT[:], a["ctxT"][b + 1]).then_inc(ld_tilectx, 16)
                sp.dma_start(mask_in[:], a["mask"][b + 1]).then_inc(ld_tilectx, 16)
                sp.wait_ge(N0.x_ready, b * 3 + 3)
                sp.dma_start(mid[b], xn[min(debug, 3)][:]).then_inc(mid_stored, 16)
                store_keys(b)
            store_context(TILES - 1)
            sp.wait_ge(L0.proj, L0.p.done(TILES - 1, "out0"))
            for t, src in ((ffn_gate, "L1_ffn_gate_w"), (ffn_up, "L1_ffn_up_w")):
                sp.dma_start(t.rearrange("p (k n) -> p k n", k=KD), two(src)).then_inc(ld_w["ffn"], 16)
            for t, src in ((w_qkv1, two("wT_qkv1")), (b_qkv1, row("L1_attn_b_qkv", 3 * D)),
                           (w_out1, two("wT_out1")), (w_q2, two("L1_xattn_Wq")), (w_p2, two("L1_xattn_Wp")),
                           (b_out1, row("L1_attn_b_out", D)), (b_q2, row("L1_xattn_bq", D)),
                           (b_p2, row("L1_xattn_bp", D)), (s_down1, row("L1_ffn_down_scale", D))):
                sp.dma_start(t, src).then_inc(ld_w["l1"], 16)
            sp.wait_ge(N0.x_ready, TILES * 3)
            sp.dma_start(mid[TILES - 1], xn[min(debug, 3)][:]).then_inc(mid_stored, 16)
            store_keys(TILES - 1)
            sp.wait_ge(values_stored, 16 * TILES + 16)
            sp.wait_ge(keys_stored, 16 * TILES + 16)
            if debug <= 3:
                sp.wait_ge(mid_stored, 16 * TILES + 16)
                return
            sp.wait_ge(mid_stored, 16 * TILES + 16)
            for lane in lanes:
                sp.dma_start(lane.x[3], mid[lane.i]).then_inc(lane.ld_mid, 16)
            sp.dma_start(values, values_dram.rearrange("t p n -> p t n")).then_inc(ld_values, 16)
            sp.dma_start(ffn_down.rearrange("p (k n) -> p k n", k=IB),
                         a["L1_ffn_down_w"].rearrange("(k p) n -> p k n", p=P)).then_inc(ld_w["down1"], 16)
            sp.dma_start(s_gate1, row("L1_ffn_gate_scale", I1)).then_inc(ld_w["scales1"], 16)
            sp.dma_start(s_up1, row("L1_ffn_up_scale", I1)).then_inc(ld_w["scales1"], 16)
            sp.dma_start(keys2T[:], keys_dram.rearrange("t p a q -> p t a q")).then_inc(ld_keys, 16)
            for lane in lanes:
                sp.sem_inc(lane.stored, 16)
            with sp.Fori(0, PAIRS - 1) as b:
                for lane in lanes:
                    sp.wait_ge(lane.x_ready, b * 3 + 1)
                    sp.dma_start(lane.x[3], mid[b * LANES + LANES + lane.i]).then_inc(lane.ld_mid, 16)
                for lane in lanes:
                    sp.wait_ge(lane.x_ready, b * 3 + 3)
                    sp.dma_start(out[b * LANES + lane.i], lane.x[debug]).then_inc(lane.stored, 16)
            for lane in lanes:
                sp.wait_ge(lane.x_ready, PAIRS * 3)
                sp.dma_start(out[TILES - LANES + lane.i], lane.x[debug]).then_inc(lane.stored, 16)
            for lane in lanes:
                sp.wait_ge(lane.stored, 16 * PAIRS + 16)

        @block.gpsimd
        def _(pool):
            nc.gpsimd.memset(neg_half[:], -0.5).then_inc(pool_prep, 1)
            nc.gpsimd.memset(v_all[:], 1.0).then_inc(pool_prep, 1)
            pool.wait_ge(pool_prep, 1)

            def power(N, b, i):
                pool.wait_ge(N.varied, b * 3 + i + 1)
                nc.gpsimd.tensor_tensor(N.rstd[:], N.mean_var[:, 1:2], neg_half[:, 0:1], ALU.pow)\
                    .then_inc(N.rstd_ready, 1)

            with pool.Fori(0, TILES) as b:
                for c in range(5):
                    pool.wait_ge(msq, b * 5 + c + 1)
                    if c >= 2:
                        pool.wait_ge(normed, b * 5 + c - 1)
                    nc.gpsimd.tensor_tensor(rms[:, c % 2, :], mean_sq[:, c % 2, :], neg_half[:], ALU.pow)\
                        .then_inc(rmsed, 1)
                for i in range(3):
                    power(N0, b, i)
            if debug <= 3:
                return
            pool.wait_ge(c_vals, 1)
            nc.gpsimd.partition_all_reduce(res[:], att[:], P, REDUCE_ABSMAX).then_inc(c_amax, 1)
            pool.wait_ge(v_scaled, 1)
            nc.gpsimd.tensor_tensor(values, values, att[:].unsqueeze(1).broadcast_to([P, TILES, D]), ALU.mult)\
                .then_inc(v_quantised, 1)
            pool.wait_ge(v_quantised, 1)
            nc.gpsimd.tensor_scalar(values, values, ROUND, ROUND, ALU.add, ALU.subtract).then_inc(v_quantised, 1)
            pool.wait_ge(v_quantised, 2)
            nc.gpsimd.tensor_scalar(vals2[:], values, 127.0, -127.0, ALU.min, ALU.max).then_inc(v_quantised, 1)
            with pool.Fori(0, PAIRS) as b:
                for step, i in SCHEDULE:
                    if step in NORM_OF:
                        power(lanes[i], b, NORM_OF[step])

        @block.scalar
        def _(act):
            act.wait_ge(ld_const, 16 * 8)
            nc.scalar.activation(tanh_gate[:], tanh_gate[:], ACT.Tanh).then_inc(act_prep, 1)

            def evac(L, b, key, dst, n=512):
                act.wait_ge(L.trans, L.t.done(b, key))
                src = ps_t[:, L.t.at[key] % 2, 0:n]
                nc.scalar.activation(dst, src.bitcast(BF16) if dst.dtype == BF16 else src, ACT.Copy)\
                    .then_inc(L.trans_taken, 1)

            def flat(ap):
                return ap.rearrange("p a b -> p (a b)")

            def groups(L, b, g0, n, scale=1.0):
                for s in range(n + 2):
                    g = g0 + s
                    if s >= 2:
                        if g - 2 >= 2:
                            act.wait_ge(L.summed, b * L.groups + g - 3)
                        evac(L, b, L.group_key(g - 2), probsT[:, g % 2, :])
                    if s < n:
                        act.wait_ge(L.shifted, b * L.groups + g + 1)
                        nc.scalar.activation(probs[:, g % 4, :], probs[:, g % 4, :], ACT.Exp, scale=scale)\
                            .then_inc(L.exped, 1)

            with act.Fori(0, TILES) as b:
                def square(c):
                    act.wait_ge(L0.proj, b * P0.count + c + 1)
                    if c >= 2:
                        act.wait_ge(msq, b * 5 + c - 1)
                    nc.scalar.activation(squares[:, c % 2, :], ps_p[:, c % 2, :], ACT.Square).then_inc(squared, 1)

                square(0)
                square(1)
                square(2)
                for j in range(2):
                    evac(L0, b, ("k0", j), flat(k0T[:, 4 * j:4 * j + 4, :]))
                square(3)
                evac(L0, b, ("q0", 0), flat(bigT[:, 0:4, :]))
                square(4)
                for j in range(1, 4):
                    evac(L0, b, ("q0", j), flat(bigT[:, 4 * j:4 * j + 4, :]))
                groups(L0, b, 0, KV0)
                for j in range(4):
                    evac(L0, b, ("o0", j), flat(bigT[:, 4 * j:4 * j + 4, :]))

                for j in range(2):
                    evac(L0, b, ("ak", j), flat(akT[:, 4 * j:4 * j + 4, :]))
                evac(L0, b, ("x", 1), flat(xT[1][:]), D)
                for j in range(4):
                    evac(L0, b, ("qk", j), flat(qkT[:, 4 * j:4 * j + 4, :]))
                groups(L0, b, KV0, 2 * GX)
                evac(L0, b, ("ox", 0), flat(attT[:]), D)
                evac(L0, b, ("x", 2), flat(xT[2][:]), D)

                act.wait_ge(logit_max, b + 1)
                nc.scalar.activation(router[:, 1, 0:E], ps_p[:, P0.at["logits"] % 2, 0:E], ACT.Exp,
                                     bias=router[:, 0, 0:1], accum_out=router[:, 0, 1:2]).then_inc(logit_exp, 1)
                jt = 0
                for c in range(CHUNKS + 2):
                    if c < CHUNKS:
                        act.wait_ge(gate_up, b * CHUNKS + c + 1)
                        if c >= 2:
                            act.wait_ge(hidden, b * CHUNKS + c - 1)
                        nc.scalar.activation(th[:, c % 2, :], (ps_p if c % 2 else ps_s)[:, 0, 0:CW], ACT.Tanh,
                                             scale=0.5).then_inc(tanhed, 1)
                    while jt < len(HB) and (h_ready(jt) <= c - 2 or c == CHUNKS + 1):
                        n, k = HB[jt], HB0[jt]
                        evac(L0, b, ("h", jt), flat(bigT[:, k:k + n, :]), n * P)
                        jt += 1
                act.wait_ge(keys_stored, b * 16 + 16)
                for j in range(2):
                    evac(L0, b, ("c", j), flat(key_stackT[:, 4 * j:4 * j + 4, :]), 2 * P)

            if debug <= 3:
                return
            def layer1(b, step, lane):
                i, other = lane.i, lanes[0]
                if step == "qkv":
                    evac(L1, b, (("x", 3), i), flat(lane.xT[3]), D)
                    for j in range(2):
                        evac(L1, b, (("qk1", j), i), flat(lane.qkT[:, 4 * j:4 * j + 4, :]))
                elif step == "heads":
                    groups(L1, b, i * G1, G1, scale=HD1 ** -0.5)
                elif step == "out":
                    evac(L1, b, (("o1", 0), i), flat(lane.attT), D)
                elif step == "query":
                    evac(L1, b, (("x", 4), i), flat(lane.xT[4]), D)
                    evac(L1, b, (("qs", 0), i), flat(lane.stackT))
                elif step == "shared":
                    for h in range(H1 + 2):
                        if h >= 2:
                            if h >= 4:
                                act.wait_ge(lane.out2, b * (H1 - 1) + h - 3)
                            elif i and h == 2:
                                act.wait_ge(other.out2, b * (H1 - 1) + H1 - 1)
                            elif i:
                                act.wait_ge(L1.proj, L1.p.done(b, ("av2x", 0)))
                            evac(L1, b, (("n", h - 2), i), n2T[:, h % 2, :])
                        if h < H1:
                            act.wait_ge(lane.max2_ready, b * H1 + h + 1)
                            if h >= 2:
                                act.wait_ge(lane.round2, b * H1 + h - 1)
                            elif i:
                                act.wait_ge(other.round2, b * H1 + H1 - 1 + h)
                            nc.scalar.activation(e2[:, h % 2, :], flat((ps_s if h % 2 == 0 else ps_o)[:]),
                                                 ACT.Exp, scale=lane.q2s[:, 0, h:h + 1], bias=lane.max2[:, 1, h:h + 1],
                                                 accum_out=lane.q2s[:, 3, h:h + 1]).then_inc(lane.exp2, 1)
                elif step == "mix":
                    evac(L1, b, (("oq", 0), i), flat(lane.attT), D)
                elif step == "gate":
                    evac(L1, b, (("x", 5), i), flat(lane.xT[5]), D)
                    for c in range(2):
                        act.wait_ge(lane.scaled1, b * 2 + c + 1)
                        nc.scalar.activation(flat(th)[:, 0:FW], flat(gg)[:, 0:FW], ACT.Tanh, scale=0.5)\
                            .then_inc(lane.tanhed1, 1)
                else:
                    for j in range(len(FBS)):
                        evac(L1, b, (("f", j), i), flat(lane.fuseT[:, FB0[j]:FB0[j] + FBS[j], :]), FBS[j] * P)

            with act.Fori(0, PAIRS) as b:
                for step, i in SCHEDULE:
                    layer1(b, step, lanes[i])

        @block.vector
        def _(dve):
            count = [0]

            def step(ins):
                count[0] += 1
                ins.then_inc(dve_prep, 1)
                dve.wait_ge(dve_prep, count[0])

            step(nc.vector.memset(key_stack, 0.0))

            def quantise(src, dst_int, scales, tmp, link):
                link(nc.vector.tensor_reduce(scales[:, 0, :], heads(src, H1), X, ALU.max, apply_absolute_value=True))
                link(nc.vector.tensor_scalar(scales[:, 0, :], scales[:, 0, :], 1.0 / 127.0, 1e-8, ALU.mult, ALU.max))
                link(nc.vector.reciprocal(scales[:, 1, :], scales[:, 0, :]))
                link(nc.vector.tensor_tensor(heads(tmp, H1), heads(src, H1),
                                             scales[:, 1, :].unsqueeze(2).broadcast_to([P, H1, HD1]), ALU.mult))
                link(nc.vector.tensor_scalar(tmp, tmp, ROUND, ROUND, ALU.add, ALU.subtract))
                link(nc.vector.tensor_scalar(dst_int, tmp, 127.0, -127.0, ALU.min, ALU.max))

            dve.wait_ge(ld_prep, 16 * 3)
            step(nc.vector.tensor_copy(ident_b[:], ident[:]))

            dve.wait_ge(ld_const, 16 * 8)
            half = HD0 // 2
            for t, wrow in ((rope_q, squares[:, 0, 0:HD0]), (rope_k, squares[:, 1, 0:HD0])):
                step(nc.vector.tensor_tensor(t[:, 0, :], t[:, 0, :], wrow, ALU.mult))
                step(nc.vector.tensor_tensor(t[:, 1, 0:half], t[:, 1, 0:half], wrow[:, half:HD0], ALU.mult))
                step(nc.vector.tensor_tensor(t[:, 1, half:HD0], t[:, 1, half:HD0], wrow[:, 0:half], ALU.mult))

            dve.wait_ge(pool_prep, 2)
            dve.wait_ge(act_prep, 1)
            nc.vector.memset(row_max[:], 0.0).then_inc(dve_done, 1)
            nc.vector.memset(carrier[:], 0.0).then_inc(tile_done, 1)

            n = [0]

            def link(L, b, ins):
                n[0] += 1
                ins.then_inc(L.chain, 1)
                dve.wait_ge(L.chain, b * L.steps + n[0])

            def carry_wait():
                nc.vector.memset(carrier[:], 0.0)

            def bank(L, key, w=512):
                return ps_p[:, L.p.at[key] % 2, 0:w]

            def taken(L, b, key, ins):
                ins.then_inc(L.proj_taken, 1)
                dve.wait_ge(L.proj_taken, L.p.done(b, key))

            def normalise(L, N, b, i, key, src, dst, add=None, scale=None):
                res, stats, mean_var, rstd = (t[:] for t in (N.res, N.stats, N.mean_var, N.rstd))
                dve.wait_ge(L.proj, L.p.done(b, key))
                if scale is not None:
                    taken(L, b, key, nc.vector.tensor_tensor(res, bank(L, key, D), scale, ALU.mult))
                    link(L, b, nc.vector.tensor_tensor(res, res, src[:], ALU.add))
                else:
                    taken(L, b, key, nc.vector.tensor_tensor(res, bank(L, key, D), src[:], ALU.add))
                if add is not None:
                    link(L, b, nc.vector.tensor_tensor(res, res, add, ALU.add))
                link(L, b, nc.vector.bn_stats(stats, res))
                carry_wait()
                link(L, b, nc.vector.bn_aggr(mean_var, stats))
                nc.vector.tensor_scalar(mean_var[:, 1:2], mean_var[:, 1:2], LN_EPS, None, ALU.add)\
                    .then_inc(N.varied, 1)
                dve.wait_ge(N.rstd_ready, b * 3 + i + 1)
                nc.vector.tensor_scalar(dst[:], res, mean_var[:, 0:1], rstd, ALU.subtract, ALU.mult)\
                    .then_inc(N.x_ready, 1)

            def group_step(L, b, g0, count, mask, s):
                g = g0 + s
                if s < count:
                    dve.wait_ge(L.scores, b * L.groups + g + 1)
                    if g >= 4:
                        dve.wait_ge(L.trans, L.t.done(b, L.group_key(g - 4)))
                    p = heads(probs[:, g % 4, :], GH)
                    if mask is not None:
                        nc.vector.tensor_tensor(p, heads(ps_s[:, g % 2, :], GH),
                                                mask.unsqueeze(1).broadcast_to([P, GH, P]), ALU.add)\
                            .then_inc(L.masked, 1)
                    else:
                        nc.vector.tensor_copy(p, heads(ps_s[:, g % 2, :], GH)).then_inc(L.masked, 1)
                if s >= 1:
                    q = heads(probs[:, (g - 1) % 4, :], GH)
                    dve.wait_ge(L.maxed, b * L.groups + g)
                    nc.vector.tensor_tensor(q, q, row_max[:, (g - 1) % 4, :].unsqueeze(2)
                                            .broadcast_to([P, GH, P]), ALU.subtract).then_inc(L.shifted, 1)
                if s < count:
                    dve.wait_ge(L.masked, b * L.groups + g + 1)
                    nc.vector.tensor_reduce(row_max[:, g % 4, :], p, X, ALU.max).then_inc(L.maxed, 1)

            with dve.Fori(0, TILES) as b:
                n[0] = 0
                half = HD0 // 2

                def rotate(c):
                    table = rope_k if c == 0 else rope_q
                    src = heads(ps_p[:, c % 2, :], 8)
                    t1, t2 = heads(ropes[:, c % 2, :], 8), heads(ropes[:, 2, :], 8)
                    dve.wait_ge(squared, b * 5 + c + 1)
                    if c >= 2:
                        dve.wait_ge(normed, b * 5 + c - 1)
                    if c >= 1:
                        dve.wait_ge(L0.proj_taken, b * P0.count + c)
                    nc.vector.tensor_tensor(t1, src, table[:, 0, :].unsqueeze(1).broadcast_to([P, 8, HD0]), ALU.mult)
                    nc.vector.tensor_tensor(t2[:, :, 0:half], src[:, :, half:HD0],
                                            table[:, 1, 0:half].unsqueeze(1).broadcast_to([P, 8, half]), ALU.mult)
                    link(L0, b, nc.vector.tensor_tensor(t2[:, :, half:HD0], src[:, :, 0:half],
                                                 table[:, 1, half:HD0].unsqueeze(1).broadcast_to([P, 8, half]),
                                                 ALU.mult))
                    nc.vector.tensor_tensor(t1, t1, t2, ALU.add).then_inc(L0.proj_taken, 1)
                    if c >= 2:
                        dve.wait_ge(rmsed, b * 5 + c - 1)
                    link(L0, b, nc.vector.tensor_reduce(mean_sq[:, c % 2, :], heads(squares[:, c % 2, :], 8), X, ALU.add))
                    nc.vector.tensor_scalar(mean_sq[:, c % 2, :], mean_sq[:, c % 2, :], 1.0 / HD0, RMS_EPS,
                                            ALU.mult, ALU.add).then_inc(msq, 1)

                def scale_heads(c):
                    dve.wait_ge(rmsed, b * 5 + c + 1)
                    dve.wait_ge(L0.proj_taken, b * P0.count + c + 1)
                    r = rms[:, c % 2, :].unsqueeze(2).broadcast_to([P, 8, HD0])
                    t1 = heads(ropes[:, c % 2, :], 8)
                    if c == 0:
                        nc.vector.tensor_tensor(kdup[:, :, 0, :], t1, r, ALU.mult)
                        nc.vector.tensor_tensor(kdup[:, :, 1, :], t1, r, ALU.mult).then_inc(normed, 1)
                    else:
                        nc.vector.tensor_tensor(heads(big[:, 512 * (c - 1):512 * c], 8), t1, r, ALU.mult)\
                            .then_inc(normed, 1)

                for c in range(6):
                    if c < 5:
                        rotate(c)
                    if c >= 1:
                        scale_heads(c - 1)
                dve.wait_ge(L0.proj, L0.p.done(b, "v"))
                nc.vector.tensor_copy(v0[:, :, 0:HD0], heads(bank(L0, "v"), KV0)).then_inc(L0.proj_taken, 1)

                def out0_norm(g):
                    dve.wait_ge(L0.summed, b * GROUPS0 + g + 1)
                    o = heads(ps_o[:, g % 2, :], GH)
                    if g >= 2:
                        dve.wait_ge(out0_ready, b * KV0 + g - 1)
                    r = recips[:, g % 2, 0:GH]
                    link(L0, b, nc.vector.reciprocal(r, o[:, :, HD0]))
                    nc.vector.tensor_tensor(heads(big[:, 512 * (g // 2):512 * (g // 2 + 1)], 8)[:, g % 2::2, :], o[:, :, 0:HD0],
                                            r.unsqueeze(2).broadcast_to([P, GH, HD0]), ALU.mult)\
                        .then_inc(out0_ready, 1)

                for s in range(KV0 + 1):
                    group_step(L0, b, 0, KV0, mask_window[:], s)
                    if s >= 4:
                        out0_norm(s - 4)
                for g in range(KV0 - 3, KV0):
                    out0_norm(g)

                dve.wait_ge(ld_tilectx, b * 32 + 32)
                link(L0, b, nc.vector.tensor_scalar(mask_in[:], mask_in[:], float(np.finfo(np.float32).min), None, ALU.max))
                if debug <= 3:
                    dve.wait_ge(mid_stored, b * 16 + 16)
                normalise(L0, N0, b, 0, "out0", xin, xa)
                dve.wait_ge(L0.proj, P0.done(b, "ck"))
                nc.vector.tensor_copy(ak_pad[:, :, 0:HDX], heads(bank(L0, "ck", D), HX)).then_inc(L0.proj_taken, 1)
                dve.wait_ge(L0.proj, P0.done(b, "cv"))
                nc.vector.tensor_copy(avx[:, :, 0:HDX], heads(bank(L0, "cv", D), HX)).then_inc(L0.proj_taken, 1)
                dve.wait_ge(L0.proj, L0.p.done(b, "k2"))
                nc.vector.tensor_tensor(kf, bank(L0, "k2", D), b_kv2[:, 0:D], ALU.add).then_inc(L0.proj_taken, 1)
                dve.wait_ge(L0.proj, L0.p.done(b, "v2"))
                dve.wait_ge(values_stored, b * 16 + 16)
                nc.vector.tensor_tensor(value_tile, bank(L0, "v2", D), b_kv2[:, D:2 * D], ALU.add)\
                    .then_inc(L0.proj_taken, 1)

                hh = HDX // 2
                dve.wait_ge(L0.proj, L0.p.done(b, "qkx"))
                src = bank(L0, "qkx").rearrange("p (s h d) -> p s h d", s=2, h=HX)
                t1 = ropes[:, 0, :].rearrange("p (s h d) -> p s h d", s=2, h=HX)
                t2 = ropes[:, 1, :].rearrange("p (s h d) -> p s h d", s=2, h=HX)
                for s in range(2):
                    nc.vector.tensor_tensor(t1[:, s], src[:, s], rope_x[:, 0, s, :].unsqueeze(1)
                                            .broadcast_to([P, HX, HDX]), ALU.mult)
                    nc.vector.tensor_tensor(t2[:, s, :, 0:hh], src[:, s, :, hh:HDX], rope_x[:, 1, s, 0:hh].unsqueeze(1)
                                            .broadcast_to([P, HX, hh]), ALU.mult)
                    ins = nc.vector.tensor_tensor(t2[:, s, :, hh:HDX], src[:, s, :, 0:hh], rope_x[:, 1, s, hh:HDX]
                                                  .unsqueeze(1).broadcast_to([P, HX, hh]), ALU.mult)
                ins.then_inc(L0.proj_taken, 1)
                dve.wait_ge(L0.proj_taken, L0.p.done(b, "qkx"))
                nc.vector.tensor_tensor(qk_pad[:, :, 0:HDX], heads(ropes[:, 0, :], 2 * HX),
                                        heads(ropes[:, 1, :], 2 * HX), ALU.add).then_inc(qkx_ready, 1)
                dve.wait_ge(L0.proj, L0.p.done(b, "vx"))
                nc.vector.tensor_copy(vx[:, :, 0:HDX], heads(bank(L0, "vx", D), HX)).then_inc(L0.proj_taken, 1)
                for s in range(GX + 1):
                    group_step(L0, b, KV0, GX, mask_in[:], s)
                for s in range(GX + 1):
                    group_step(L0, b, KV0 + GX, GX, None, s)
                wx = HX * (HDX + 1)
                o1, o2 = (ps_o[:, i, 0:wx].rearrange("p (a m d) -> p m a d", a=4, d=HDX + 1) for i in range(2))

                def hx(ap):
                    return ap.rearrange("p (m a d) -> p m a d", a=4, d=HDX)

                def rx(i):
                    return recips[:, i, :].rearrange("p (m a) -> p m a", a=4)

                dve.wait_ge(L0.summed, b * GROUPS0 + GROUPS0)
                link(L0, b, nc.vector.reciprocal(rx(0), o1[:, :, :, HDX]))
                link(L0, b, nc.vector.reciprocal(rx(1), o2[:, :, :, HDX]))
                link(L0, b, nc.vector.tensor_tensor(recips[:, 1, :], recips[:, 1, :], tanh_gate[:], ALU.mult))
                link(L0, b, nc.vector.tensor_tensor(hx(att[:]), o1[:, :, :, 0:HDX],
                                             rx(0).unsqueeze(3).broadcast_to([P, HX // 4, 4, HDX]), ALU.mult))
                link(L0, b, nc.vector.tensor_tensor(hx(res[:]), o2[:, :, :, 0:HDX],
                                             rx(1).unsqueeze(3).broadcast_to([P, HX // 4, 4, HDX]), ALU.mult))
                nc.vector.tensor_tensor(att[:], att[:], res[:], ALU.add).then_inc(heads_x, 1)
                normalise(L0, N0, b, 1, "outx", xa, xb)

                dve.wait_ge(L0.proj, L0.p.done(b, "logits"))
                lg = bank(L0, "logits", E)
                nc.vector.tensor_reduce(router[:, 0, 0:1], lg, X, ALU.max, negate=True).then_inc(logit_max, 1)
                dve.wait_ge(logit_exp, b + 1)
                nc.vector.reciprocal(router[:, 0, 2:3], router[:, 0, 1:2]).then_inc(L0.proj_taken, 1)
                dve.wait_ge(L0.proj_taken, L0.p.done(b, "logits"))
                link(L0, b, nc.vector.memset(router[:, 2, E:E + 1], -1.0))
                link(L0, b, nc.vector.memset(router[:, 2, E + 1:E + 2], -2.0))
                link(L0, b, nc.vector.tensor_scalar(router[:, 2, 0:E], router[:, 1, 0:E], router[:, 0, 2:3], None, ALU.mult))
                carry_wait()
                link(L0, b, nc.vector.max(router[:, 3, 0:8], router[:, 2, 0:E]))
                link(L0, b, nc.vector.tensor_copy(router[:, 3, TOPK:8], router[:, 2, E:E + 2]))
                carry_wait()
                link(L0, b, nc.vector.match_replace(router[:, 4, 0:E + 2], router[:, 3, 0:8], router[:, 2, 0:E + 2], -3.0))
                link(L0, b, nc.vector.tensor_scalar(router[:, 5, 0:E], router[:, 4, 0:E], -3.0, 0.5, ALU.is_equal, ALU.mult))
                link(L0, b, nc.vector.tensor_tensor(router[:, 6, 0:E], router[:, 5, 0:E], router[:, 2, 0:E], ALU.mult))
                def per_head(i):
                    return key_scale[:, i, :].unsqueeze(2).broadcast_to([P, H1, HD1])

                def context_keys(c):
                    if c == 0:
                        link(L0, b, nc.vector.tensor_reduce(key_scale[:, 0, :], heads(kf, H1), X, ALU.max,
                                                            apply_absolute_value=True))
                        link(L0, b, nc.vector.tensor_scalar(key_scale[:, 0, :], key_scale[:, 0, :], 1.0 / 127.0, 1e-8,
                                                            ALU.mult, ALU.max))
                    elif c == 1:
                        link(L0, b, nc.vector.reciprocal(key_scale[:, 1, :], key_scale[:, 0, :]))
                        link(L0, b, nc.vector.tensor_tensor(heads(kq, H1), heads(kf, H1), per_head(1), ALU.mult))
                    elif c == 2:
                        link(L0, b, nc.vector.tensor_scalar(kq, kq, ROUND, ROUND, ALU.add, ALU.subtract))
                        link(L0, b, nc.vector.tensor_scalar(kq, kq, 127.0, -127.0, ALU.min, ALU.max))
                    elif c == 3:
                        link(L0, b, nc.vector.tensor_tensor(heads(kf, H1), heads(kq, H1), per_head(0), ALU.mult))
                        link(L0, b, nc.vector.tensor_copy(key_stack[:, :, 0:16], heads(kf, H1)))
                    elif c == 4:
                        link(L0, b, nc.vector.tensor_tensor(heads(r1, H1), heads(kf, H1), key_stack[:, :, 0:16],
                                                            ALU.subtract))
                        link(L0, b, nc.vector.tensor_copy(key_stack[:, :, 16:32], heads(r1, H1)))
                    elif c == 5:
                        link(L0, b, nc.vector.tensor_tensor(heads(r2, H1), heads(r1, H1), key_stack[:, :, 16:32],
                                                            ALU.subtract))
                        nc.vector.tensor_copy(key_stack[:, :, 32:48], heads(r2, H1)).then_inc(c_stack, 1)

                for c in range(CHUNKS):
                    g = (ps_p if c % 2 else ps_s)[:, 0, 0:CW]
                    u = (ps_p if c % 2 else ps_s)[:, 1, 0:CW]
                    dve.wait_ge(tanhed, b * CHUNKS + c + 1)
                    link(L0, b, nc.vector.scalar_tensor_tensor(gg[:, c % 2, :], th[:, c % 2, :], 1.0, g, ALU.add, ALU.mult))
                    for e in range(EC):
                        ins = nc.vector.scalar_tensor_tensor(
                            big[:, c * CW + e * F:c * CW + (e + 1) * F], gg[:, c % 2, e * F:(e + 1) * F],
                            router[:, 6, c * EC + e:c * EC + e + 1], u[:, e * F:(e + 1) * F], ALU.mult, ALU.mult)
                    ins.then_inc(hidden, 1)
                    context_keys(c)
                dve.wait_ge(mid_stored, b * 16 + 16)
                normalise(L0, N0, b, 2, "down", xb, xc)
                dve.wait_ge(N0.x_ready, b * 3 + 3)
                nc.vector.memset(carrier[:], 0.0).then_inc(tile_done, 1)
                assert n[0] == CHAIN0, n[0]

            if debug <= 3:
                return

            def round_fp8(src, dst, w):
                dst = dst.rearrange("p a b -> p (a b)")
                f8a, f8b = round_low.bitcast(FP8)[:, 0:w], round_high.bitcast(FP8)[:, 0:w]
                step(nc.vector.tensor_scalar(f8a, src, FP8_MAX, -FP8_MAX, ALU.min, ALU.max, saturate=False))
                step(nc.vector.tensor_scalar(f8b, src, 0.5, None, ALU.mult, saturate=False))
                step(nc.vector.tensor_scalar(round_sel.bitcast(U32)[:, 0:w], src.bitcast(U32), 1, 31,
                                             ALU.logical_shift_left, ALU.logical_shift_right))
                step(nc.vector.tensor_copy(dst, f8a))
                step(nc.vector.tensor_scalar(round_two[:, 0:w], f8b, 2.0, None, ALU.mult))
                step(nc.vector.copy_predicated(dst, round_sel.bitcast(U32)[:, 0:w], round_two[:, 0:w]))

            dve.wait_ge(ld_w["ffn"], 16 * 2)
            round_fp8(ffn_gate, w_gate1, KD * I1)
            dve.wait_ge(ld_values, 16)
            nc.vector.tensor_reduce(att[:], values.rearrange("p t n -> p n t"), X, ALU.max,
                                    apply_absolute_value=True).then_inc(c_vals, 1)
            round_fp8(ffn_up, w_up1, KD * I1)
            dve.wait_ge(c_amax, 1)
            step(nc.vector.tensor_scalar(v_scale[:], res[:], 1.0 / 127.0, 1e-8, ALU.mult, ALU.max))
            nc.vector.reciprocal(att[:], v_scale[:]).then_inc(v_scaled, 1)
            dve.wait_ge(ld_w["down1"], 16)
            round_fp8(ffn_down, w_down1, IB * D)
            for lane in lanes:
                step(nc.vector.memset(lane.v_wide, 1.0))
                step(nc.vector.memset(lane.stack, 0.0))
            step(nc.vector.memset(lanes[1].qk_pad, 0.0))
            nc.vector.memset(carrier[:], 0.0).then_inc(pair_done, 1)
            dve.wait_ge(ld_w["l1"], 16 * 9)
            dve.wait_ge(ld_w["scales1"], 16 * 2)

            def split(b, src, parts, tmp):
                link(L1, b, nc.vector.tensor_copy(parts[0], src))
                link(L1, b, nc.vector.tensor_tensor(tmp, src, parts[0], ALU.subtract))
                link(L1, b, nc.vector.tensor_copy(parts[1], tmp))
                return nc.vector.tensor_tensor(parts[2], tmp, parts[1], ALU.subtract)

            def layer1(b, name, lane):
                i = lane.i
                key = (STEPS[name][1][-1], i) if STEPS[name][1] else None
                q2, q2s, max2, att, v1 = lane.q2, lane.q2s, lane.max2, lane.att, lane.v
                if name == "qkv":
                    for half, part in enumerate(("q1", "k1")):
                        dve.wait_ge(L1.proj, L1.p.done(b, (part, i)))
                        nc.vector.tensor_tensor(lane.qk_pad[:, H1 * half:H1 * (half + 1), 0:HD1],
                                                heads(bank(L1, (part, i), D), H1),
                                                heads(b_qkv1[:, D * half:D * (half + 1)], H1), ALU.add)\
                            .then_inc(L1.proj_taken, 1)
                    dve.wait_ge(L1.proj, L1.p.done(b, key))
                    nc.vector.tensor_tensor(v1[:, :, 0:HD1], heads(bank(L1, key, D), H1),
                                            heads(b_qkv1[:, 2 * D:3 * D], H1), ALU.add).then_inc(L1.proj_taken, 1)
                elif name == "heads":
                    dve.wait_ge(v_quantised, 1)
                    for s in range(G1 + 1):
                        group_step(L1, b, i * G1, G1, mask_causal[:], s)
                    o1 = ps_o[:, i, 0:H1 * (HD1 + 1)].rearrange("p (a m d) -> p m a d", a=4, d=HD1 + 1)
                    r1x = recips[:, i, 0:H1].rearrange("p (m a) -> p m a", a=4)
                    dve.wait_ge(L1.summed, b * GROUPS1 + (i + 1) * G1)
                    link(L1, b, nc.vector.reciprocal(r1x, o1[:, :, :, HD1]))
                    nc.vector.tensor_tensor(att.rearrange("p (m a d) -> p m a d", a=4, d=HD1), o1[:, :, :, 0:HD1],
                                            r1x.unsqueeze(3).broadcast_to([P, H1 // 4, 4, HD1]), ALU.mult)\
                        .then_inc(lane.heads_1, 1)
                elif name == "out":
                    normalise(L1, lane, b, 0, key, lane.x[3], lane.x[4], add=b_out1)
                elif name == "query":
                    dve.wait_ge(L1.proj, L1.p.done(b, key))
                    nc.vector.tensor_tensor(q2, bank(L1, key, D), b_q2, ALU.add).then_inc(L1.proj_taken, 1)
                    dve.wait_ge(L1.proj_taken, L1.p.done(b, key))
                    link(L1, b, nc.vector.tensor_scalar(q2, q2, HD1 ** -0.5, None, ALU.mult))
                    quantise(q2, q2, q2s, q2, lambda ins: link(L1, b, ins))
                    link(L1, b, nc.vector.tensor_scalar(q2s[:, 2, :], q2s[:, 0, :], -1.0, None, ALU.mult))
                    for part in range(3):
                        ins = nc.vector.tensor_copy(lane.stack[:, :, 16 * part:16 * part + 16], heads(q2, H1))
                    ins.then_inc(lane.q2_ready, 1)
                elif name == "shared":
                    for h in range(H1 + 1):
                        if h < H1:
                            dve.wait_ge(lane.s2, b * H1 + h + 1)
                            link(L1, b, nc.vector.tensor_reduce(max2[:, 0, h:h + 1],
                                                                (ps_s if h % 2 == 0 else ps_o)[:]
                                                                .rearrange("p a b -> p (a b)"), X, ALU.max))
                            nc.vector.tensor_scalar(max2[:, 1, h:h + 1], max2[:, 0, h:h + 1], q2s[:, 2, h:h + 1],
                                                    LN255, ALU.mult, ALU.add).then_inc(lane.max2_ready, 1)
                        if h >= 1:
                            dve.wait_ge(lane.exp2, b * H1 + h)
                            if h >= 3:
                                dve.wait_ge(L1.trans, L1.t.done(b, (("n", h - 3), i)))
                            elif i:
                                dve.wait_ge(L1.trans, L1.t.done(b, (("n", H1 - 3 + h), 0)))
                            nc.vector.tensor_scalar(n2[:, (h - 1) % 2, :], e2[:, (h - 1) % 2, :], ROUND, ROUND,
                                                    ALU.add, ALU.subtract).then_inc(lane.round2, 1)
                    dve.wait_ge(L1.proj, L1.p.done(b, key))
                    link(L1, b, nc.vector.reciprocal(recips[:, i, 0:H1], q2s[:, 3, :]))
                    nc.vector.tensor_tensor(heads(att, H1), heads(bank(L1, key, D), H1),
                                            recips[:, i, 0:H1].unsqueeze(2).broadcast_to([P, H1, HD1]), ALU.mult)\
                        .then_inc(L1.proj_taken, 1)
                    dve.wait_ge(L1.proj_taken, L1.p.done(b, key))
                    nc.vector.tensor_tensor(att, att, v_scale[:], ALU.mult).then_inc(lane.heads_2, 1)
                elif name == "mix":
                    normalise(L1, lane, b, 1, key, lane.x[4], lane.x[5], add=b_p2)
                elif name == "gate":
                    dve.wait_ge(L1.trans_taken, L1.t.done(b, (("x", 5), i)))
                    r = lane.res.rearrange("p (k q) -> p k q", k=KD)
                    split(b, lane.xT[5], [lane.x5p[:, part] for part in range(3)], r).then_inc(lane.parts5, 1)
                    gs = gg.rearrange("p a b -> p (a b)")[:, 0:FW]
                    tt = th.rearrange("p a b -> p (a b)")[:, 0:FW]
                    us = ropes[:].rearrange("p a b -> p (a b)")[:, 2 * CW:2 * CW + FW]
                    for c in range(2):
                        cols = slice(c * FW, (c + 1) * FW)
                        gp, up = (ps_s if c == 0 else ps_o)[:, 0, 0:FW], (ps_s if c == 0 else ps_o)[:, 1, 0:FW]
                        dve.wait_ge(lane.gate_up1, b * 2 + c + 1)
                        if c:
                            dve.wait_ge(lane.fused, b * 2 + c)
                        elif i:
                            dve.wait_ge(lanes[0].fused, b * 2 + 2)
                        nc.vector.tensor_tensor(gs, gp, s_gate1[:, cols], ALU.mult).then_inc(lane.scaled1, 1)
                        link(L1, b, nc.vector.tensor_tensor(us, up, s_up1[:, cols], ALU.mult))
                        dve.wait_ge(lane.tanhed1, b * 2 + c + 1)
                        link(L1, b, nc.vector.scalar_tensor_tensor(gs, tt, 1.0, gs, ALU.add, ALU.mult))
                        nc.vector.scalar_tensor_tensor(lane.fuse[:, cols], gs, 0.5, us, ALU.mult, ALU.mult)\
                            .then_inc(lane.fused, 1)
                else:
                    r = lane.res.rearrange("p (k q) -> p k q", k=KD)
                    for j, (k, w) in enumerate(zip(FB0, FBS)):
                        dve.wait_ge(L1.trans_taken, L1.t.done(b, (("f", j), i)))
                        if j:
                            dve.wait_ge(lane.fparts, b * len(FBS) + j)
                        split(b, lane.fuseT[:, k:k + w, :], [lane.fusep[:, part, k:k + w, :] for part in range(3)],
                              r[:, 0:w, :]).then_inc(lane.fparts, 1)
                    dve.wait_ge(lane.stored, b * 16 + 16)
                    normalise(L1, lane, b, 2, key, lane.x[5], lane.x[6], scale=s_down1)

            with dve.Fori(0, PAIRS) as b:
                n[0] = 0
                for name, i in SCHEDULE:
                    layer1(b, name, lanes[i])
                dve.wait_ge(lanes[1].x_ready, b * 3 + 3)
                nc.vector.memset(carrier[:], 0.0).then_inc(pair_done, 1)
                assert n[0] == CHAIN1, n[0]

        @block.tensor
        def _(pe):
            pe.wait_ge(ld_prep, 16 * 3)
            pe.wait_ge(dve_done, 1)
            pe.wait_ge(ld_w["k0"], 16)

            def project(L, b, key, xTi, w, col, width):
                n = L.p.at[key]
                if n >= 2:
                    pe.wait_ge(L.proj_taken, b * L.p.count + n - 1)
                kk = w.shape[1]
                for k in range(kk):
                    ins = nc.tensor.matmul(ps_p[:, n % 2, 0:width], xTi[:, k, :], w[:, k, col:col + width],
                                           start=(k == 0), stop=(k == kk - 1))
                ins.then_inc(L.proj, 1)

            def transpose(L, b, key, src, nblocks, bf=False):
                t = L.t.at[key]
                if t >= 2:
                    pe.wait_ge(L.trans_taken, b * L.t.count + t - 1)
                dst = ps_t[:, t % 2, :].bitcast(BF16) if bf else ps_t[:, t % 2, :]
                for i in range(nblocks):
                    ins = nc.tensor.transpose(dst[:, i * P:(i + 1) * P], src(i), ident_b[:] if bf else ident[:])
                ins.then_inc(L.trans, 1)

            def keep_warm():
                for _ in range(WARM):
                    nc.tensor.matmul(ps_s[:, 0, 0:P], ident_b[:], ident_b[:], start=True, stop=True)

            def group_scores(L, b, g, q, k):
                if g >= 2:
                    pe.wait_ge(L.masked, b * L.groups + g - 1)
                for i in range(GH):
                    ins = nc.tensor.matmul(ps_s[:, g % 2, i * P:(i + 1) * P], q(i), k(i), start=True, stop=True)
                ins.then_inc(L.scores, 1)

            def group_transpose(L, b, g):
                pe.wait_ge(L.exped, b * L.groups + g + 1)
                transpose(L, b, L.group_key(g), lambda i: probs[:, g % 4, i * P:(i + 1) * P], GH)

            def group_sum(L, b, g, dst, v):
                pe.wait_ge(L.trans_taken, L.t.done(b, L.group_key(g)))
                for i in range(GH):
                    ins = nc.tensor.matmul(dst(i), probsT[:, g % 2, i * P:(i + 1) * P], v(i), start=True, stop=True)
                ins.then_inc(L.summed, 1)

            def wide(ap, n, w):
                return ap[:, n * w:n * w + WIDE]

            def x_transpose(L, b, key, x):
                transpose(L, b, key, lambda k: x[:, k * P:(k + 1) * P], KD)
                pe.wait_ge(L.trans_taken, L.t.done(b, key))

            def padded(ap, first):
                return ap[:, first:first + 4, :].rearrange("p a b -> p (a b)")

            with pe.Fori(0, TILES) as b:
                pe.wait_ge(ld_x, b * 32 + 32)
                nq = H0 * HD0
                project(L0, b, "k", xT[0], w_qkv0, nq, 512)
                pe.wait_ge(tile_done, b + 1)
                pe.wait_ge(ld_w["qkv0"], 16 * 2)
                project(L0, b, "q0", xT[0], w_qkv0, 0, 512)
                project(L0, b, "q1", xT[0], w_qkv0, 512, 512)
                pe.wait_ge(normed, b * 5 + 1)
                for j in range(2):
                    transpose(L0, b, ("k0", j), lambda i: kdup[:, 4 * j + i].rearrange("p a b -> p (a b)"), 4)
                project(L0, b, "q2", xT[0], w_qkv0, 1024, 512)

                def q0_transpose(j):
                    keep_warm()
                    pe.wait_ge(normed, b * 5 + j + 2)
                    transpose(L0, b, ("q0", j), lambda i: big[:, (4 * j + i) * P:(4 * j + i + 1) * P], 4)

                q0_transpose(0)
                project(L0, b, "q3", xT[0], w_qkv0, 1536, 512)
                q0_transpose(1)
                project(L0, b, "v", xT[0], w_qkv0, nq + 512, 512)
                q0_transpose(2)
                q0_transpose(3)
                pe.wait_ge(L0.trans_taken, L0.t.done(b, ("q0", 3)))
                pe.wait_ge(L0.proj_taken, L0.p.done(b, "v"))

                def rows(i):
                    return slice(HD0 * (i % 2), HD0 * (i % 2) + HD0)

                for s in range(KV0 + 3):
                    if s < KV0:
                        group_scores(L0, b, s, lambda i: bigT[rows(s), head0(s, i) // 2, :],
                                     lambda i: k0T[rows(s), head0(s, i) // 4, :])
                    if 2 <= s < KV0 + 2:
                        group_transpose(L0, b, s - 2)
                    if s >= 3:
                        g = s - 3
                        if g >= 2:
                            pe.wait_ge(out0_ready, b * KV0 + g - 1)
                        group_sum(L0, b, g, lambda i: ps_o[:, g % 2, i * WIDE:(i + 1) * WIDE],
                                  lambda i: wide(v0_wide, head0(g, i) // 4, HD0 + 1))
                for j in range(4):
                    pe.wait_ge(out0_ready, b * KV0 + 2 * j + 2)
                    transpose(L0, b, ("o0", j), lambda i: big[:, (4 * j + i) * P:(4 * j + i + 1) * P], 4)
                pe.wait_ge(L0.trans_taken, L0.t.done(b, ("o0", 3)))
                pe.wait_ge(ld_w["att0"], 16 * 5)
                project(L0, b, "out0", bigT, w_out0, 0, D)

                pe.wait_ge(ld_tilectx, b * 32 + 32)
                project(L0, b, "ck", ctxT, w_x, D, D)
                project(L0, b, "cv", ctxT, w_x, 2 * D, D)
                project(L0, b, "k2", ctxT, w_kv2, 0, D)
                project(L0, b, "v2", ctxT, w_kv2, D, D)
                pe.wait_ge(L0.proj_taken, P0.done(b, "ck"))
                for j in range(2):
                    transpose(L0, b, ("ak", j), lambda i: padded(ak_pad, 16 * j + 4 * i), 4)
                keep_warm()
                pe.wait_ge(N0.x_ready, b * 3 + 1)
                x_transpose(L0, b, ("x", 1), xa)
                project(L0, b, "qkx", xT[1], w_x, 0, 2 * D)
                project(L0, b, "vx", xT[1], w_x, 2 * D, D)
                keep_warm()
                pe.wait_ge(qkx_ready, b + 1)
                for j in range(4):
                    transpose(L0, b, ("qk", j), lambda i: padded(qk_pad, 16 * j + 4 * i), 4)
                pe.wait_ge(L0.trans_taken, L0.t.done(b, ("qk", 3)))
                pe.wait_ge(L0.proj_taken, L0.p.done(b, "vx"))
                gx, g0 = GX, KV0
                for s in range(2 * gx + 3):
                    if s < 2 * gx:
                        keysT, m = (qkT[:, 8:16, :], s) if s < gx else (akT, s - gx)
                        r = slice(PAD * (m // 2), PAD * (m // 2) + HDX)
                        group_scores(L0, b, g0 + s, lambda i: qkT[r, headx(m, i) // 4, :],
                                     lambda i: keysT[r, headx(m, i) // 4, :])
                    if 2 <= s < 2 * gx + 2:
                        group_transpose(L0, b, g0 + s - 2)
                    if s >= 3:
                        g = s - 3
                        vv, m, w = (vx_wide if g < gx else avx_wide), g % gx, HDX + 1
                        group_sum(L0, b, g0 + g, lambda i: wide(ps_o[:, g // gx, :], GH * m + i, w),
                                  lambda i: wide(vv, headx(m, i), w))
                pe.wait_ge(heads_x, b + 1)
                transpose(L0, b, ("ox", 0), lambda k: att[:, k * P:(k + 1) * P], KD)
                pe.wait_ge(L0.trans_taken, L0.t.done(b, ("ox", 0)))
                project(L0, b, "outx", attT, w_outx, 0, D)

                keep_warm()
                pe.wait_ge(N0.x_ready, b * 3 + 2)
                x_transpose(L0, b, ("x", 2), xb)
                pe.wait_ge(ld_w["moe"], 16 * 4)
                project(L0, b, "logits", xT[2], w_router, 0, E)
                down = P0.at["down"]

                def h_transpose(j):
                    nb, k0 = HB[j], HB0[j]
                    pe.wait_ge(hidden, b * CHUNKS + h_ready(j) + 1)
                    transpose(L0, b, ("h", j), lambda i: big[:, (k0 + i) * P:(k0 + i + 1) * P], nb)

                jt = 0
                for c in range(CHUNKS):
                    if c >= 2:
                        pe.wait_ge(hidden, b * CHUNKS + c - 1)
                    elif c == 1:
                        pe.wait_ge(L0.proj_taken, L0.p.done(b, "logits"))
                    bank = ps_p if c % 2 else ps_s
                    for half, w in ((0, w_gate), (1, w_up)):
                        for k in range(KD):
                            ins = nc.tensor.matmul(bank[:, half, 0:CW], xT[2][:, k, :], w[:, k, c * CW:(c + 1) * CW],
                                                   start=(k == 0), stop=(k == KD - 1))
                    ins.then_inc(gate_up, 1)
                    while jt < len(HB) and h_ready(jt) <= c - 2:
                        h_transpose(jt)
                        jt += 1
                while jt < len(HB):
                    h_transpose(jt)
                    jt += 1
                for k in range(FB):
                    if k in HB0:
                        pe.wait_ge(L0.trans_taken, T0.done(b, ("h", HB0.index(k))))
                    ins = nc.tensor.matmul(ps_p[:, down % 2, 0:D], bigT[:, k, :], w_down[:, k, :], start=(k == 0),
                                           stop=(k == FB - 1))
                ins.then_inc(L0.proj, 1)
                pe.wait_ge(c_stack, b + 1)
                for j in range(2):
                    transpose(L0, b, ("c", j), lambda i: key_stack[:, 8 * j + 2 * i:8 * j + 2 * i + 2, :]
                              .rearrange("p a b -> p (a b)"), 4, bf=True)
            if debug <= 3:
                return
            pe.wait_ge(tile_done, TILES + 1)
            pe.wait_ge(ld_w["l1"], 16 * 9)

            def layer1(b, step, lane):
                i, other = lane.i, lanes[0]
                if step == "qkv":
                    pe.wait_ge(lane.ld_mid, b * 16 + 16)
                    x_transpose(L1, b, (("x", 3), i), lane.x[3])
                    for part, name in enumerate(("q1", "k1", "v1")):
                        project(L1, b, (name, i), lane.xT[3], w_qkv1, part * D, D)
                        if part + i == 0:
                            pe.wait_ge(pair_done, b + 1)
                    pe.wait_ge(L1.proj_taken, L1.p.done(b, ("k1", i)))
                    for j in range(2):
                        transpose(L1, b, (("qk1", j), i), lambda n: padded(lane.qk_pad, 16 * j + 4 * n), 4)
                elif step == "heads":
                    pe.wait_ge(L1.trans_taken, L1.t.done(b, (("qk1", 1), i)))
                    pe.wait_ge(L1.proj_taken, L1.p.done(b, ("v1", i)))
                    g0, w = i * G1, HD1 + 1
                    for s in range(G1 + 3):
                        if s < G1:
                            group_scores(L1, b, g0 + s, lambda n: lane.qkT[PAD * s:PAD * s + HD1, head1(s, n) // 4, :],
                                         lambda n: lane.qkT[PAD * s:PAD * s + HD1, 4 + head1(s, n) // 4, :])
                        if 2 <= s < G1 + 2:
                            group_transpose(L1, b, g0 + s - 2)
                        if s >= 3:
                            g = s - 3
                            group_sum(L1, b, g0 + g, lambda n: wide(ps_o[:, i, :], GH * g + n, w),
                                      lambda n: wide(lane.v_wide, head1(g, n), w))
                elif step == "out":
                    pe.wait_ge(lane.heads_1, b + 1)
                    x_transpose(L1, b, (("o1", 0), i), lane.att)
                    project(L1, b, ("out1", i), lane.attT, w_out1, 0, D)
                elif step == "query":
                    pe.wait_ge(lane.x_ready, b * 3 + 1)
                    x_transpose(L1, b, (("x", 4), i), lane.x[4])
                    project(L1, b, ("q2x", i), lane.xT[4], w_q2, 0, D)
                    pe.wait_ge(lane.q2_ready, b + 1)
                    transpose(L1, b, (("qs", 0), i), lambda n: lane.stack[:, 2 * n:2 * n + 2, :]
                              .rearrange("p a b -> p (a b)"), 8, bf=True)
                elif step == "shared":
                    pe.wait_ge(ld_keys, 16)
                    pe.wait_ge(v_quantised, 3)
                    pe.wait_ge(L1.trans_taken, L1.t.done(b, (("qs", 0), i)))
                    av = L1.p.at["av2x", i]
                    pe.wait_ge(L1.proj_taken, b * L1.p.count + av - 1)
                    for s in range(H1 + 3):
                        if s < H1:
                            bank = ps_s if s % 2 == 0 else ps_o
                            r = slice(STK * (s % 2), STK * (s % 2) + 3 * HD1)
                            if s >= 2:
                                pe.wait_ge(lane.exp2, b * H1 + s - 1)
                            elif i:
                                pe.wait_ge(other.exp2, b * H1 + H1 - 1 + s)
                            else:
                                pe.wait_ge(L1.masked, b * GROUPS1 + GROUPS1)
                                pe.wait_ge(lanes[1].heads_1, b + 1)
                            for n in range(2):
                                ins = nc.tensor.matmul(bank[:, n, :], lane.stackT[r, s // 2, :],
                                                       keys2T[r, 4 * n:4 * n + 4, s // 2, :], start=True, stop=True)
                            ins.then_inc(lane.s2, 1)
                        if 2 <= s < H1 + 2:
                            h = s - 2
                            pe.wait_ge(lane.round2, b * H1 + h + 1)
                            transpose(L1, b, (("n", h), i), lambda n: n2[:, h % 2, n * P:(n + 1) * P], 8, bf=True)
                        if s >= 3:
                            h = s - 3
                            pe.wait_ge(L1.trans_taken, L1.t.done(b, (("n", h), i)))
                            for n in range(TILES):
                                ins = nc.tensor.matmul(ps_p[:, av % 2, h * HD1:(h + 1) * HD1],
                                                       n2T[:, h % 2, n * P:(n + 1) * P],
                                                       vals2[:, n, h * HD1:(h + 1) * HD1], start=(n == 0),
                                                       stop=(n == TILES - 1))
                            ins.then_inc(lane.out2 if h < H1 - 1 else L1.proj, 1)
                elif step == "mix":
                    pe.wait_ge(lane.heads_2, b + 1)
                    x_transpose(L1, b, (("oq", 0), i), lane.att)
                    project(L1, b, ("out2x", i), lane.attT, w_p2, 0, D)
                elif step == "gate":
                    pe.wait_ge(lane.x_ready, b * 3 + 2)
                    transpose(L1, b, (("x", 5), i), lambda k: lane.x[5][:, k * P:(k + 1) * P], KD)
                    pe.wait_ge(lane.parts5, b + 1)
                    if i:
                        pe.wait_ge(other.fused, b * 2 + 2)
                    else:
                        pe.wait_ge(lanes[1].exp2, b * H1 + H1)
                    for c in range(2):
                        bank = ps_s if c == 0 else ps_o
                        for half, w in ((0, w_gate1), (1, w_up1)):
                            for k in range(KD):
                                for part in range(3):
                                    ins = nc.tensor.matmul(bank[:, half, 0:FW], lane.x5p[:, part, k, :],
                                                           w[:, k, c * FW:(c + 1) * FW], start=(k + part == 0),
                                                           stop=(k == KD - 1 and part == 2))
                        ins.then_inc(lane.gate_up1, 1)
                else:
                    for j, (k, w) in enumerate(zip(FB0, FBS)):
                        pe.wait_ge(lane.fused, b * 2 + (1 if j == 0 else 2))
                        transpose(L1, b, (("f", j), i), lambda n: lane.fuse[:, (k + n) * P:(k + n + 1) * P], w)
                    d1 = L1.p.at["down1", i]
                    pe.wait_ge(L1.proj_taken, b * L1.p.count + d1 - 1)
                    for k in range(IB):
                        if k in FB0:
                            pe.wait_ge(lane.fparts, b * len(FBS) + FB0.index(k) + 1)
                        for part in range(3):
                            ins = nc.tensor.matmul(ps_p[:, d1 % 2, 0:D], lane.fusep[:, part, k, :], w_down1[:, k, :],
                                                   start=(k + part == 0), stop=(k == IB - 1 and part == 2))
                    ins.then_inc(L1.proj, 1)

            with pe.Fori(0, PAIRS) as b:
                for step, i in SCHEDULE:
                    layer1(b, step, lanes[i])
                pe.wait_ge(lanes[0].x_ready, b * 3 + 3)


CHAIN0, CHAIN1 = 46 + 11, 2 * 54

_OUT = (TILES, P, D)
_DIRECT = ["L0_attn_q_norm_w", "L0_attn_k_norm_w", "L0_xattn_Wq", "L0_xattn_Wk", "L0_xattn_Wv", "L0_xattn_Wo",
           "L1_attn_b_qkv", "L1_attn_b_out", "L1_xattn_Wq", "L1_xattn_bq", "L1_xattn_Wkv", "L1_xattn_bkv",
           "L1_xattn_Wp", "L1_xattn_bp", "L1_ffn_gate_w", "L1_ffn_up_w", "L1_ffn_down_w", "L1_ffn_gate_scale",
           "L1_ffn_up_scale", "L1_ffn_down_scale"]


def constants():
    pos = np.arange(P, dtype=np.float32)

    def tables(d):
        inv = (1.0 / 10000.0 ** (np.arange(0, d, 2, dtype=np.float32) / d)).astype(np.float32)
        ang = pos[:, None] * inv[None, :]
        ang = np.concatenate([ang, ang], -1)
        sign = np.where(np.arange(d) < d // 2, -1.0, 1.0).astype(np.float32)
        return np.stack([np.cos(ang), np.sin(ang) * sign], 1).astype(np.float32)

    c = {"ident": np.eye(P, dtype=np.float32)}
    q, k = np.arange(P)[:, None], np.arange(P)[None, :]
    c["mask_causal"] = np.where(q >= k, 0.0, -1e30).astype(np.float32)
    c["mask_window"] = np.where((q >= k) & (q - k < 64), 0.0, -1e30).astype(np.float32)
    c["rope_k"] = tables(HD0)
    c["rope_q"] = (tables(HD0) * np.float32(HD0 ** -0.5)).astype(np.float32)
    x = tables(HDX)
    c["rope_x"] = np.stack([x * np.float32(HDX ** -0.5), x], 2).astype(np.float32)
    return c


def lay_out(inputs):
    g = {n: np.asarray(v) for n, v in inputs.items()}

    def tiles_T(x):
        return np.ascontiguousarray(x.reshape(TILES, P, KD, P).transpose(0, 3, 2, 1))

    arrays = {n: np.ascontiguousarray(g[n]) for n in _DIRECT}
    arrays["x"] = np.ascontiguousarray(g["x"])
    arrays["xT"] = tiles_T(g["x"])
    arrays["ctxT"] = tiles_T(g["ctx_2048"])
    arrays["mask"] = np.ascontiguousarray(g["mask_Bx1xSxS_fk0"].reshape(TILES, P, P))
    arrays["gate"] = np.ascontiguousarray(g["L0_xattn_gate"].reshape(HX))
    arrays["wT_qkv0"] = np.ascontiguousarray(g["L0_attn_w_qkv"].T)
    arrays["wT_out0"] = np.ascontiguousarray(g["L0_attn_w_out"].T)
    arrays["wT_router"] = np.ascontiguousarray(g["L0_ffn_gate_w"].T)
    arrays["wT_gate"] = np.ascontiguousarray(g["L0_ffn_w_gate"].reshape(EF, D).T)
    arrays["wT_up"] = np.ascontiguousarray(g["L0_ffn_w_up"].reshape(EF, D).T)
    arrays["wT_down"] = np.ascontiguousarray(g["L0_ffn_w_down"].transpose(0, 2, 1).reshape(EF, D))
    arrays["wT_qkv1"] = np.ascontiguousarray(g["L1_attn_W_qkv"].T)
    arrays["wT_out1"] = np.ascontiguousarray(g["L1_attn_W_out"].T)
    arrays.update(constants())
    return arrays


def build(nc, arrays, debug=6):
    a = {n: nc.dram_tensor(f"in_{n}", v.shape, mybir.dt.from_np(v.dtype), kind="ExternalInput").ap()
         for n, v in arrays.items()}
    out = nc.dram_tensor("out_0", _OUT, F32, kind="ExternalOutput").ap()
    mid = nc.dram_tensor("mid", _OUT, F32, kind="Internal").ap() if debug > 3 else out
    keys = nc.dram_tensor("keys", (TILES, P, H1 // 2, P), BF16, kind="Internal").ap()
    values = nc.dram_tensor("values", (TILES, P, D), F32, kind="Internal").ap()
    decoder(nc, a, mid, keys, values, out, debug)


def kernel(**inputs):
    import concourse.bacc as bacc
    from concourse.bass_utils import run_bass_kernel_spmd

    arrays = lay_out(inputs)
    nc = bacc.Bacc("TRN2", target_bir_lowering=False, num_devices=1)
    build(nc, arrays)
    r = run_bass_kernel_spmd(nc, [{f"in_{n}": v for n, v in arrays.items()}], core_ids=[0])
    return r.results[0]["out_0"]
```

```python
from contextlib import ExitStack

import numpy as np
import concourse.bass as bass
from concourse import mybir

F32 = mybir.dt.float32
BF16 = mybir.dt.bfloat16
FP8 = mybir.dt.float8e4
U32 = mybir.dt.uint32
ALU = mybir.AluOpType
ACT = mybir.ActivationFunctionType
X = mybir.AxisListType.X
REDUCE_ABSMAX = bass.bass_isa.ReduceOp.absmax

P = 128
TILES = 8
D = 256
KD = D // P
H0, KV0, HD0 = 32, 8, 64
HX, HDX = 32, 8
H1, HD1 = 16, 16
E, F, TOPK = 16, 176, 6
EF = E * F
FB = EF // P
I1 = 768
IB = I1 // P
PAD = 32
STK = 64
GH = 4
EC = 2
ROUND = float(3 << 22)
LN_EPS, RMS_EPS = 1e-5, 1e-6
LN255 = float(np.log(255.0))
FP8_MAX = 240.0

HB = [3] * 6 + [4]
HB0 = [sum(HB[:j]) for j in range(len(HB))]
FBS = [2, 2, 1, 1]
FB0 = [sum(FBS[:j]) for j in range(len(FBS))]
WARM = 20
WIDE = 128
GX = HX // GH
G1 = H1 // GH


class Order:

    def __init__(self, keys):
        self.at = {key: n for n, key in enumerate(keys)}
        self.count = len(keys)
        assert self.count % 2 == 0

    def done(self, tile, key):
        return tile * self.count + self.at[key] + 1


T0 = Order([("k0", j) for j in range(2)] + [("q0", j) for j in range(4)] + [("p", g) for g in range(KV0)]
           + [("o0", j) for j in range(4)] + [("ak", j) for j in range(2)] + [("x", 1)]
           + [("qk", j) for j in range(4)] + [("p", KV0 + g) for g in range(2 * GX)] + [("ox", 0), ("x", 2)]
           + [("h", j) for j in range(len(HB))] + [("c", 0), ("c", 1)])
STEPS = {"qkv": ([("x", 3), ("qk1", 0), ("qk1", 1)], ["q1", "k1", "v1"]),
         "heads": ([("p", g) for g in range(G1)], []),
         "out": ([("o1", 0)], ["out1"]),
         "query": ([("x", 4), ("qs", 0)], ["q2x"]),
         "shared": ([("n", h) for h in range(H1)], ["av2x"]),
         "mix": ([("oq", 0)], ["out2x"]),
         "gate": ([("x", 5)], []),
         "down": ([("f", j) for j in range(len(FBS))], ["down1"])}
NORMS = ("out", "mix", "down")
LANES = 2
PAIRS = TILES // LANES


def order1(part):
    keys = []
    for name, batches in STEPS.items():
        if name in ("heads", "shared"):
            keys += [(key, lane) for lane in range(LANES) for key in batches[part]]
        else:
            keys += [(key, lane) for key in batches[part] for lane in range(LANES)]
    return Order(keys)


T1 = order1(0)
P0 = Order(["k", "q0", "q1", "q2", "q3", "v", "out0", "ck", "cv", "k2", "v2", "qkx", "vx", "outx", "logits", "down"])
P1 = order1(1)
GROUPS0, GROUPS1 = KV0 + 2 * GX, LANES * G1

CHUNKS = E // EC
CW = EC * F
HBATCH = 4 * P
FW = I1 // 2


def head0(g, i):
    return 8 * (g // 2) + g % 2 + 2 * i


def headx(g, i):
    return 4 * (4 * (g % 2) + i) + g // 2


def head1(g, i):
    return 4 * i + g


def h_ready(j):
    return min(CHUNKS - 1, -(-P * (HB0[j] + HB[j]) // CW) - 1)


class Layer:

    def __init__(self, sem, name, transposes, projections, groups, masks, chain, group_key):
        self.t, self.p, self.groups, self.steps, self.group_key = transposes, projections, groups, chain, group_key
        self.masks = masks
        self.proj = sem(f"proj{name}")
        self.proj_taken = sem(f"proj_taken{name}")
        self.trans = sem(f"trans{name}")
        self.trans_taken = sem(f"trans_taken{name}")
        self.scores = sem(f"scores{name}")
        self.masked = sem(f"masked{name}")
        self.maxed = sem(f"maxed{name}")
        self.shifted = sem(f"shifted{name}")
        self.exped = sem(f"exped{name}")
        self.summed = sem(f"summed{name}")
        self.chain = sem(f"chain{name}")


class Norms:

    def __init__(self, sem, name, res, stats, mean_var, rstd):
        self.res, self.stats, self.mean_var, self.rstd = res, stats, mean_var, rstd
        self.varied = sem(f"varied{name}")
        self.rstd_ready = sem(f"rstd_ready{name}")
        self.x_ready = sem(f"x_ready{name}")


class Lane(Norms):

    def __init__(self, sem, i, norms, xin, xinT, xa, xaT, xb, xbT, xc, qk_pad, qkT, v_wide, att, attT, stack,
                 stackT, q2, q2s, max2, x5p, fuse, fuseT, fusep):
        super().__init__(sem, f"_lane{i}", *norms)
        self.i = i
        self.x = {3: xin, 4: xa, 5: xb, 6: xc}
        self.xT = {3: xinT, 4: xaT, 5: xbT}
        self.qk_pad, self.qkT, self.v_wide, self.att, self.attT = qk_pad, qkT, v_wide, att, attT
        self.v = v_wide[:, 0:H1 * (HD1 + 1)].rearrange("p (h d) -> p h d", h=H1)
        self.stack, self.stackT, self.q2, self.q2s, self.max2 = stack, stackT, q2, q2s, max2
        self.x5p, self.fuse, self.fuseT, self.fusep = x5p, fuse, fuseT, fusep

        def lane(name):
            return sem(f"{name}_lane{i}")

        self.ld_mid, self.stored = lane("ld_mid"), lane("stored")
        self.heads_1 = lane("heads_1")
        self.heads_2 = lane("heads_2")
        self.q2_ready = lane("q2_ready")
        self.s2 = lane("s2")
        self.max2_ready = lane("max2_ready")
        self.exp2 = lane("exp2")
        self.round2 = lane("round2")
        self.out2 = lane("out2")
        self.parts5 = lane("parts5")
        self.gate_up1 = lane("gate_up1")
        self.scaled1 = lane("scaled1")
        self.tanhed1 = lane("tanhed1")
        self.fused = lane("fused")
        self.fparts = lane("fparts")


def decoder(nc, a, mid, keys_dram, values_dram, out, debug=6):
    ctx = ExitStack()
    with ctx:
        def sb(name, shape, dt=F32):
            return ctx.enter_context(nc.sbuf_tensor(name, shape, dt))

        def ps(name, shape, dt=F32):
            return ctx.enter_context(nc.psum_tensor(name, shape, dt))

        def sem(name):
            return ctx.enter_context(nc.semaphore(name))

        w_qkv0 = sb("w_qkv0", [P, KD, (H0 + 2 * KV0) * HD0])
        w_out0 = sb("w_out0", [P, H0 * HD0 // P, D])
        w_x = sb("w_x", [P, KD, 3 * D])
        w_outx = sb("w_outx", [P, KD, D])
        w_router = sb("w_router", [P, KD, E])
        w_moe = sb("w_moe", [P, 3 * KD * EF])
        w_gate = w_moe[:, 0:KD * EF].rearrange("p (k n) -> p k n", k=KD)
        w_up = w_moe[:, KD * EF:2 * KD * EF].rearrange("p (k n) -> p k n", k=KD)
        w_down = w_moe[:, 2 * KD * EF:3 * KD * EF].rearrange("p (k n) -> p k n", k=FB)

        class Region:

            def __init__(self, ap):
                self.ap, self.at = ap, 0

            def take(self, *dims, dt=F32):
                n = int(np.prod(dims)) // (1 if dt is F32 else 2)
                v = self.ap[:, self.at:self.at + n]
                self.at += n
                if dt is not F32:
                    v = v.bitcast(dt)
                if len(dims) == 1:
                    return v
                names = "abc"[:len(dims)]
                return v.rearrange(f"p ({' '.join(names)}) -> p {' '.join(names)}",
                                   **{c: d for c, d in zip(names[:-1], dims)})

        over = Region(w_qkv0[:].rearrange("p a b -> p (a b)"))
        w_qkv1 = over.take(KD, 3 * D)
        w_out1 = over.take(KD, D)
        w_q2 = over.take(KD, D)
        w_p2 = over.take(KD, D)
        b_qkv1 = over.take(3 * D)
        b_out1, b_q2, b_p2, s_down1 = (over.take(D) for _ in range(4))
        over = Region(w_out0[:].rearrange("p a b -> p (a b)"))
        ffn_gate, ffn_up = over.take(KD * I1), over.take(KD * I1)
        over = Region(w_moe)
        w_gate1 = over.take(KD, I1, dt=BF16)
        w_up1 = over.take(KD, I1, dt=BF16)
        w_down1 = over.take(IB, D, dt=BF16)
        s_gate1, s_up1 = over.take(I1), over.take(I1)
        e2 = over.take(2, TILES * P)
        values = e2.rearrange("p a b -> p (a b)").rearrange("p (t n) -> p t n", t=TILES)
        n2 = over.take(2, TILES * P, dt=BF16)
        n2T = over.take(2, TILES * P, dt=BF16)
        words = IB * D + I1 + KD * I1 + KD * I1 // 2
        rounding = Region(over.take(words))
        ffn_down = rounding.take(IB * D)
        round_low, round_high = rounding.take(I1, dt=BF16), rounding.take(I1, dt=BF16)
        round_sel = rounding.take(KD * I1)
        round_two = rounding.take(KD * I1, dt=BF16)
        assert rounding.at == words
        rounding.at = 0
        rest = Region(w_moe[:, over.at:])

        ident = sb("ident", [P, P])
        ident_b = sb("ident_b", [P, P], BF16)
        mask_window = sb("mask_window", [P, P])
        mask_causal = sb("mask_causal", [P, P])
        rope_q = sb("rope_q", [P, 2, HD0])
        rope_k = sb("rope_k", [P, 2, HD0])
        rope_x = sb("rope_x", [P, 2, 2, HDX])
        tanh_gate = sb("tanh_gate", [P, HX])
        neg_half = sb("neg_half", [P, 8])
        keys2T = sb("keys2T", [P, TILES, H1 // 2, P], BF16)
        over = Region(keys2T[:].rearrange("p a b c -> p (a b c)").bitcast(F32))
        w_kv2 = over.take(KD, 2 * D)
        b_kv2 = over.take(2 * D)
        key_stack = over.take(H1, STK, dt=BF16)
        key_stackT = over.take(8, P, dt=BF16)
        value_tile = over.take(D)
        kf, kq, r1, r2 = (over.take(D) for _ in range(4))
        key_scale = over.take(2, H1)
        vals2 = sb("vals2", [P, TILES, D], BF16)
        v_scale = sb("v_scale", [P, D])
        xin = sb("xin", [P, D])
        xinT = sb("xinT", [P, KD, P])
        ctxT = sb("ctxT", [P, KD, P])
        mask_in = sb("mask_in", [P, P])
        xa, xb, xc = (sb(n, [P, D]) for n in ("xa", "xb", "xc"))
        xaT, xbT = (sb(n, [P, KD, P]) for n in ("xaT", "xbT"))
        xn = {0: xin, 1: xa, 2: xb, 3: xc}
        xT = {0: xinT, 1: xaT, 2: xbT}
        res = sb("res", [P, D])
        stats = sb("stats", [P, 6])
        mean_var = sb("mean_var", [P, 2])
        rstd = sb("rstd", [P, 1])
        carrier = sb("carrier", [P, 1])
        big = sb("big", [P, EF])
        bigT = sb("bigT", [P, FB, P])
        squares = sb("squares", [P, 2, 512])
        ropes = sb("ropes", [P, 3, 512])
        mean_sq = sb("mean_sq", [P, 2, 8])
        rms = sb("rms", [P, 2, 8])
        kdup = sb("kdup", [P, KV0, 2, HD0])
        k0T = sb("k0T", [P, KV0, P])
        nv0, nvx = KV0 * (HD0 + 1), HX * (HDX + 1)
        v_all = sb("v_all", [P, nv0 + 2 * nvx + WIDE])
        v0_wide, vx_wide, avx_wide = v_all[:, 0:], v_all[:, nv0:], v_all[:, nv0 + nvx:]
        v0 = v0_wide[:, 0:KV0 * (HD0 + 1)].rearrange("p (h d) -> p h d", h=KV0)
        probs = sb("probs", [P, 4, 512])
        probsT = sb("probsT", [P, 2, 512])
        row_max = sb("row_max", [P, 4, GH])
        recips = sb("recips", [P, 2, 32])
        qk_pad = big[:, 0:2 * HX * PAD].rearrange("p (h d) -> p h d", d=PAD)
        qkT = bigT[:, 0:16, :]
        ak_pad = kdup[:].rearrange("p a b c -> p (a b c)").rearrange("p (h d) -> p h d", d=PAD)
        akT = k0T
        vx, avx = (w[:, 0:HX * (HDX + 1)].rearrange("p (h d) -> p h d", h=HX) for w in (vx_wide, avx_wide))
        att = sb("att", [P, D])
        attT = sb("attT", [P, KD, P])
        router = sb("router", [P, 7, 20])
        th = squares[:].rearrange("p a b -> p (a b)")[:, 0:2 * CW].rearrange("p (a b) -> p a b", a=2)
        gg = ropes[:].rearrange("p a b -> p (a b)")[:, 0:2 * CW].rearrange("p (a b) -> p a b", a=2)
        q2s = sb("q2s", [P, 4, H1])
        stack = big[:, 1536:1536 + H1 * STK // 2].bitcast(BF16).rearrange("p (h d) -> p h d", h=H1)
        ps_s = ps("ps_s", [P, 2, 512])
        ps_o = ps("ps_o", [P, 2, 512])
        ps_t = ps("ps_t", [P, 2, 512])
        ps_p = ps("ps_p", [P, 2, 512])

        ld_ident = sem("ld_ident")
        ld_kv2 = sem("ld_kv2")
        ld_const = sem("ld_const")
        ld_w = {n: sem(f"ld_{n}") for n in ("k0", "qkv0", "att0", "moe", "l1", "scales1", "ffn", "down1")}
        ld_x = sem("ld_x")
        ld_tilectx = sem("ld_tilectx")
        dve_prep = sem("dve_prep")
        dve_done = sem("dve_done")
        pair_done = sem("pair_done")
        tile_done = sem("tile_done")
        act_prep = sem("act_prep")
        pool_prep = sem("pool_prep")
        c_stack = sem("c_stack")
        v_scaled = sem("v_scaled")
        v_quantised = sem("v_quantised")
        keys_stored = sem("keys_stored")
        values_stored = sem("values_stored")
        ld_keys = sem("ld_keys")
        ld_values = sem("ld_values")
        c_vals = sem("c_vals")
        c_amax = sem("c_amax")
        squared = sem("squared")
        msq = sem("msq")
        rmsed = sem("rmsed")
        normed = sem("normed")
        out0_ready = sem("out0_ready")
        heads_x = sem("heads_x")
        qkx_ready = sem("qkx_ready")
        logit_max = sem("logit_max")
        logit_exp = sem("logit_exp")
        gate_up = sem("gate_up")
        tanhed = sem("tanhed")
        hidden = sem("hidden")

        mid_stored = sem("mid_stored")
        L0 = Layer(sem, "0", T0, P0, GROUPS0, KV0 + GX, CHAIN0, lambda g: ("p", g))
        L1 = Layer(sem, "1", T1, P1, GROUPS1, GROUPS1, CHAIN1, lambda g: (("p", g % G1), g // G1))
        N0 = Norms(sem, "0", res, stats, mean_var, rstd)

        nv1 = H1 * (HD1 + 1) + WIDE - HD1 - 1

        def pads(ap):
            return ap.rearrange("p (h d) -> p h d", d=PAD)

        def stack_of(ap):
            return ap.bitcast(BF16).rearrange("p (h d) -> p h d", h=H1)

        spare = Region(bigT[:, 8:, :].rearrange("p a b -> p (a b)"))
        freed = Region(w_out0[:].rearrange("p a b -> p (a b)"))
        lanes = [
            Lane(sem, 0, (res[:], stats[:], mean_var[:], rstd[:]), xin[:], xinT[:], xa[:], xaT[:], xb[:],
                 xbT[:], xc[:], qk_pad=pads(big[:, 0:2 * H1 * PAD]), qkT=bigT[:, 0:8, :], att=att[:], attT=attT[:],
                 stack=stack, stackT=rest.take(8, P, dt=BF16), q2=rest.take(D), q2s=q2s, max2=rest.take(2, H1),
                 x5p=rest.take(3, KD, P, dt=BF16), fuse=rest.take(I1), fuseT=rest.take(IB, P),
                 fusep=rest.take(3, IB, P, dt=BF16), v_wide=rest.take(nv1)),
            Lane(sem, 1, (rounding.take(D), rounding.take(6), rounding.take(2), rounding.take(1)),
                 spare.take(D), spare.take(KD, P), rounding.take(D), rounding.take(KD, P), rounding.take(D),
                 rounding.take(KD, P), rounding.take(D), qk_pad=pads(freed.take(2 * H1 * PAD)), qkT=spare.take(8, P),
                 att=rounding.take(D), attT=rounding.take(KD, P), stack=stack_of(rounding.take(H1 * STK // 2)),
                 stackT=rounding.take(8, P, dt=BF16), q2=rounding.take(D), q2s=rounding.take(4, H1),
                 max2=rounding.take(2, H1), x5p=freed.take(3, KD, P, dt=BF16), fuse=freed.take(I1),
                 fuseT=freed.take(IB, P), fusep=freed.take(3, IB, P, dt=BF16), v_wide=rounding.take(nv1))]
        for i, lane in enumerate(lanes):
            lane.gs, lane.us = (ropes[:].rearrange("p a b -> p (a b)")[:, n * FW:(n + 1) * FW] for n in (i, 2 + i))
            lane.tt = squares[:].rearrange("p a b -> p (a b)")[:, i * FW:(i + 1) * FW]
        for region in (rest, rounding, spare, freed):
            assert region.at <= region.ap.shape[-1]

        block = ctx.enter_context(nc.Block())

        def heads(ap, n):
            return ap.rearrange("p (h d) -> p h d", h=n)

        def row(name, n):
            return a[name].rearrange("(o n) -> o n", o=1).broadcast_to([P, n])

        def two(name):
            return a[name].rearrange("(k p) n -> p k n", p=P)

        @block.sync
        def _(sp):
            sp.dma_start(ident[:], a["ident"]).then_inc(ld_ident, 16)
            nq = H0 * HD0
            sp.dma_start(w_qkv0[:, :, nq:nq + 512], two("wT_qkv0")[:, :, nq:nq + 512]).then_inc(ld_w["k0"], 16)
            sp.dma_start(xin[:], a["x"][0]).then_inc(ld_x, 16)
            sp.dma_start(xinT[:], a["xT"][0]).then_inc(ld_x, 16)
            sp.dma_start(w_qkv0[:, :, 0:nq], two("wT_qkv0")[:, :, 0:nq]).then_inc(ld_w["qkv0"], 16)
            sp.dma_start(w_qkv0[:, :, nq + 512:], two("wT_qkv0")[:, :, nq + 512:]).then_inc(ld_w["qkv0"], 16)
            sp.dma_start(w_kv2, two("L1_xattn_Wkv")).then_inc(ld_kv2, 16)
            sp.dma_start(b_kv2, row("L1_xattn_bkv", 2 * D)).then_inc(ld_kv2, 16)
            for t, src in ((w_out0[:], a["wT_out0"].rearrange("(k p) n -> p k n", p=P)),
                           (w_x[:, :, 0:D], two("L0_xattn_Wq")), (w_x[:, :, D:2 * D], two("L0_xattn_Wk")),
                           (w_x[:, :, 2 * D:3 * D], two("L0_xattn_Wv")),
                           (w_outx[:], two("L0_xattn_Wo"))):
                sp.dma_start(t, src).then_inc(ld_w["att0"], 16)
            sp.dma_start(ctxT[:], a["ctxT"][0]).then_inc(ld_tilectx, 16)
            sp.dma_start(mask_in[:], a["mask"][0]).then_inc(ld_tilectx, 16)
            for t, src in ((w_router[:], two("wT_router")), (w_gate, two("wT_gate")), (w_up, two("wT_up")),
                           (w_down, a["wT_down"].rearrange("(k p) n -> p k n", p=P))):
                sp.dma_start(t, src).then_inc(ld_w["moe"], 16)
            sp.sem_inc(mid_stored, 16)
            sp.sem_inc(keys_stored, 16)
            sp.sem_inc(values_stored, 16)

            def store_context(b):
                sp.wait_ge(L0.proj_taken, L0.p.done(b, "v2"))
                sp.dma_start(values_dram[b], value_tile).then_inc(values_stored, 16)

            def store_keys(b):
                sp.wait_ge(L0.trans_taken, L0.t.done(b, ("c", 1)))
                sp.dma_start(keys_dram[b], key_stackT).then_inc(keys_stored, 16)

            with sp.Fori(0, TILES - 1) as b:
                sp.wait_ge(N0.x_ready, b * 3 + 1)
                sp.dma_start(xin[:], a["x"][b + 1]).then_inc(ld_x, 16)
                sp.dma_start(xinT[:], a["xT"][b + 1]).then_inc(ld_x, 16)
                store_context(b)
                sp.wait_ge(N0.x_ready, b * 3 + 2)
                sp.dma_start(ctxT[:], a["ctxT"][b + 1]).then_inc(ld_tilectx, 16)
                sp.dma_start(mask_in[:], a["mask"][b + 1]).then_inc(ld_tilectx, 16)
                sp.wait_ge(N0.x_ready, b * 3 + 3)
                sp.dma_start(mid[b], xn[min(debug, 3)][:]).then_inc(mid_stored, 16)
                store_keys(b)
            store_context(TILES - 1)
            sp.wait_ge(L0.proj, L0.p.done(TILES - 1, "out0"))
            for t, src in ((ffn_gate, "L1_ffn_gate_w"), (ffn_up, "L1_ffn_up_w")):
                sp.dma_start(t.rearrange("p (k n) -> p k n", k=KD), two(src)).then_inc(ld_w["ffn"], 16)
            for t, src in ((w_qkv1, two("wT_qkv1")), (b_qkv1, row("L1_attn_b_qkv", 3 * D)),
                           (w_out1, two("wT_out1")), (w_q2, two("L1_xattn_Wq")), (w_p2, two("L1_xattn_Wp")),
                           (b_out1, row("L1_attn_b_out", D)), (b_q2, row("L1_xattn_bq", D)),
                           (b_p2, row("L1_xattn_bp", D)), (s_down1, row("L1_ffn_down_scale", D))):
                sp.dma_start(t, src).then_inc(ld_w["l1"], 16)
            sp.wait_ge(N0.x_ready, TILES * 3)
            sp.dma_start(mid[TILES - 1], xn[min(debug, 3)][:]).then_inc(mid_stored, 16)
            store_keys(TILES - 1)
            sp.wait_ge(values_stored, 16 * TILES + 16)
            sp.wait_ge(keys_stored, 16 * TILES + 16)
            if debug <= 3:
                sp.wait_ge(mid_stored, 16 * TILES + 16)
                return
            sp.wait_ge(mid_stored, 16 * TILES + 16)
            for lane in lanes:
                sp.dma_start(lane.x[3], mid[lane.i]).then_inc(lane.ld_mid, 16)
            sp.dma_start(values, values_dram.rearrange("t p n -> p t n")).then_inc(ld_values, 16)
            sp.dma_start(ffn_down.rearrange("p (k n) -> p k n", k=IB),
                         a["L1_ffn_down_w"].rearrange("(k p) n -> p k n", p=P)).then_inc(ld_w["down1"], 16)
            sp.dma_start(s_gate1, row("L1_ffn_gate_scale", I1)).then_inc(ld_w["scales1"], 16)
            sp.dma_start(s_up1, row("L1_ffn_up_scale", I1)).then_inc(ld_w["scales1"], 16)
            sp.dma_start(keys2T[:], keys_dram.rearrange("t p a q -> p t a q")).then_inc(ld_keys, 16)
            for lane in lanes:
                sp.sem_inc(lane.stored, 16)
            with sp.Fori(0, PAIRS - 1) as b:
                for lane in lanes:
                    sp.wait_ge(lane.x_ready, b * 3 + 1)
                    sp.dma_start(lane.x[3], mid[b * LANES + LANES + lane.i]).then_inc(lane.ld_mid, 16)
                for lane in lanes:
                    sp.wait_ge(lane.x_ready, b * 3 + 3)
                    sp.dma_start(out[b * LANES + lane.i], lane.x[debug]).then_inc(lane.stored, 16)
            for lane in lanes:
                sp.wait_ge(lane.x_ready, PAIRS * 3)
                sp.dma_start(out[TILES - LANES + lane.i], lane.x[debug]).then_inc(lane.stored, 16)
            for lane in lanes:
                sp.wait_ge(lane.stored, 16 * PAIRS + 16)

        @block.gpsimd
        def _(pool):
            nc.gpsimd.memset(neg_half[:], -0.5).then_inc(pool_prep, 1)
            nc.gpsimd.memset(v_all[:], 1.0).then_inc(pool_prep, 1)
            pool.wait_ge(pool_prep, 1)

            def power(N, b, i):
                pool.wait_ge(N.varied, b * 3 + i + 1)
                nc.gpsimd.tensor_tensor(N.rstd[:], N.mean_var[:, 1:2], neg_half[:, 0:1], ALU.pow)\
                    .then_inc(N.rstd_ready, 1)

            with pool.Fori(0, TILES) as b:
                for c in range(5):
                    pool.wait_ge(msq, b * 5 + c + 1)
                    if c >= 2:
                        pool.wait_ge(normed, b * 5 + c - 1)
                    nc.gpsimd.tensor_tensor(rms[:, c % 2, :], mean_sq[:, c % 2, :], neg_half[:], ALU.pow)\
                        .then_inc(rmsed, 1)
                for i in range(3):
                    power(N0, b, i)
            if debug <= 3:
                return
            pool.wait_ge(c_vals, 1)
            nc.gpsimd.partition_all_reduce(res[:], att[:], P, REDUCE_ABSMAX).then_inc(c_amax, 1)
            pool.wait_ge(v_scaled, 1)
            nc.gpsimd.tensor_tensor(values, values, att[:].unsqueeze(1).broadcast_to([P, TILES, D]), ALU.mult)\
                .then_inc(v_quantised, 1)
            pool.wait_ge(v_quantised, 1)
            nc.gpsimd.tensor_scalar(values, values, ROUND, ROUND, ALU.add, ALU.subtract).then_inc(v_quantised, 1)
            pool.wait_ge(v_quantised, 2)
            nc.gpsimd.tensor_scalar(vals2[:], values, 127.0, -127.0, ALU.min, ALU.max).then_inc(v_quantised, 1)
            with pool.Fori(0, PAIRS) as b:
                for i in range(len(NORMS)):
                    for lane in lanes:
                        power(lane, b, i)

        @block.scalar
        def _(act):
            for t, n in ((mask_window, "mask_window"), (mask_causal, "mask_causal")):
                act.dma_start(t[:], a[n]).then_inc(ld_const, 16)
            act.dma_start(rope_q[:], a["rope_q"]).then_inc(ld_const, 16)
            act.dma_start(rope_k[:], a["rope_k"]).then_inc(ld_const, 16)
            act.dma_start(rope_x[:], a["rope_x"]).then_inc(ld_const, 16)
            act.dma_start(squares[:, 0, 0:HD0], row("L0_attn_q_norm_w", HD0)).then_inc(ld_const, 16)
            act.dma_start(squares[:, 1, 0:HD0], row("L0_attn_k_norm_w", HD0)).then_inc(ld_const, 16)
            act.dma_start(tanh_gate[:], row("gate", HX)).then_inc(ld_const, 16)
            act.wait_ge(ld_const, 16 * 8)
            nc.scalar.activation(tanh_gate[:], tanh_gate[:], ACT.Tanh).then_inc(act_prep, 1)

            def evac(L, b, key, dst, n=512):
                act.wait_ge(L.trans, L.t.done(b, key))
                src = ps_t[:, L.t.at[key] % 2, 0:n]
                nc.scalar.activation(dst, src.bitcast(BF16) if dst.dtype == BF16 else src, ACT.Copy)\
                    .then_inc(L.trans_taken, 1)

            def flat(ap):
                return ap.rearrange("p a b -> p (a b)")

            def groups(L, b, g0, n, scale=1.0):
                for s in range(n + 2):
                    g = g0 + s
                    if s >= 2:
                        if g - 2 >= 2:
                            act.wait_ge(L.summed, b * L.groups + g - 3)
                        evac(L, b, L.group_key(g - 2), probsT[:, g % 2, :])
                    if s < n:
                        act.wait_ge(L.shifted, b * L.groups + g + 1)
                        nc.scalar.activation(probs[:, g % 4, :], probs[:, g % 4, :], ACT.Exp, scale=scale)\
                            .then_inc(L.exped, 1)

            with act.Fori(0, TILES) as b:
                def square(c):
                    act.wait_ge(L0.proj, b * P0.count + c + 1)
                    if c >= 2:
                        act.wait_ge(msq, b * 5 + c - 1)
                    nc.scalar.activation(squares[:, c % 2, :], ps_p[:, c % 2, :], ACT.Square).then_inc(squared, 1)

                square(0)
                square(1)
                square(2)
                for j in range(2):
                    evac(L0, b, ("k0", j), flat(k0T[:, 4 * j:4 * j + 4, :]))
                square(3)
                evac(L0, b, ("q0", 0), flat(bigT[:, 0:4, :]))
                square(4)
                for j in range(1, 4):
                    evac(L0, b, ("q0", j), flat(bigT[:, 4 * j:4 * j + 4, :]))
                groups(L0, b, 0, KV0)
                for j in range(4):
                    evac(L0, b, ("o0", j), flat(bigT[:, 4 * j:4 * j + 4, :]))

                for j in range(2):
                    evac(L0, b, ("ak", j), flat(akT[:, 4 * j:4 * j + 4, :]))
                evac(L0, b, ("x", 1), flat(xT[1][:]), D)
                for j in range(4):
                    evac(L0, b, ("qk", j), flat(qkT[:, 4 * j:4 * j + 4, :]))
                groups(L0, b, KV0, 2 * GX)
                evac(L0, b, ("ox", 0), flat(attT[:]), D)
                evac(L0, b, ("x", 2), flat(xT[2][:]), D)

                act.wait_ge(logit_max, b + 1)
                nc.scalar.activation(router[:, 1, 0:E], ps_p[:, P0.at["logits"] % 2, 0:E], ACT.Exp,
                                     bias=router[:, 0, 0:1], accum_out=router[:, 0, 1:2]).then_inc(logit_exp, 1)
                jt = 0
                for c in range(CHUNKS + 2):
                    if c < CHUNKS:
                        act.wait_ge(gate_up, b * CHUNKS + c + 1)
                        if c >= 2:
                            act.wait_ge(hidden, b * CHUNKS + c - 1)
                        nc.scalar.activation(th[:, c % 2, :], (ps_p if c % 2 else ps_s)[:, 0, 0:CW], ACT.Tanh,
                                             scale=0.5).then_inc(tanhed, 1)
                    while jt < len(HB) and (h_ready(jt) <= c - 2 or c == CHUNKS + 1):
                        n, k = HB[jt], HB0[jt]
                        evac(L0, b, ("h", jt), flat(bigT[:, k:k + n, :]), n * P)
                        jt += 1
                act.wait_ge(keys_stored, b * 16 + 16)
                for j in range(2):
                    evac(L0, b, ("c", j), flat(key_stackT[:, 4 * j:4 * j + 4, :]), 2 * P)

            if debug <= 3:
                return
            def both(b, key, dst, n=512):
                for lane in lanes:
                    evac(L1, b, (key, lane.i), flat(dst(lane)), n)

            def shared(b, lane):
                i, other = lane.i, lanes[0]
                for h in range(H1 + 2):
                    if h >= 2:
                        if h >= 4:
                            act.wait_ge(lane.out2, b * (H1 - 1) + h - 3)
                        elif i and h == 2:
                            act.wait_ge(other.out2, b * (H1 - 1) + H1 - 1)
                        elif i:
                            act.wait_ge(L1.proj, L1.p.done(b, ("av2x", 0)))
                        evac(L1, b, (("n", h - 2), i), n2T[:, h % 2, :])
                    if h < H1:
                        act.wait_ge(lane.max2_ready, b * H1 + h + 1)
                        if h >= 2:
                            act.wait_ge(lane.round2, b * H1 + h - 1)
                        elif i:
                            act.wait_ge(other.round2, b * H1 + H1 - 1 + h)
                        nc.scalar.activation(e2[:, h % 2, :], flat((ps_s if h % 2 == 0 else ps_o)[:]),
                                             ACT.Exp, scale=lane.q2s[:, 0, h:h + 1], bias=lane.max2[:, 1, h:h + 1],
                                             accum_out=lane.q2s[:, 3, h:h + 1]).then_inc(lane.exp2, 1)

            with act.Fori(0, PAIRS) as b:
                both(b, ("x", 3), lambda lane: lane.xT[3], D)
                for j in range(2):
                    both(b, ("qk1", j), lambda lane: lane.qkT[:, 4 * j:4 * j + 4, :])
                for lane in lanes:
                    groups(L1, b, lane.i * G1, G1, scale=HD1 ** -0.5)
                both(b, ("o1", 0), lambda lane: lane.attT, D)
                both(b, ("x", 4), lambda lane: lane.xT[4], D)
                both(b, ("qs", 0), lambda lane: lane.stackT)
                for lane in lanes:
                    shared(b, lane)
                both(b, ("oq", 0), lambda lane: lane.attT, D)
                both(b, ("x", 5), lambda lane: lane.xT[5], D)
                for c in range(2):
                    for lane in lanes:
                        act.wait_ge(lane.scaled1, b * 2 + c + 1)
                        nc.scalar.activation(lane.tt, lane.gs, ACT.Tanh, scale=0.5).then_inc(lane.tanhed1, 1)
                for j in range(len(FBS)):
                    both(b, ("f", j), lambda lane: lane.fuseT[:, FB0[j]:FB0[j] + FBS[j], :], FBS[j] * P)

        @block.vector
        def _(dve):
            count = [0]

            def step(ins):
                count[0] += 1
                ins.then_inc(dve_prep, 1)
                dve.wait_ge(dve_prep, count[0])

            step(nc.vector.memset(key_stack, 0.0))

            dve.wait_ge(ld_ident, 16)
            step(nc.vector.tensor_copy(ident_b[:], ident[:]))

            dve.wait_ge(ld_const, 16 * 8)
            half = HD0 // 2
            for t, wrow in ((rope_q, squares[:, 0, 0:HD0]), (rope_k, squares[:, 1, 0:HD0])):
                step(nc.vector.tensor_tensor(t[:, 0, :], t[:, 0, :], wrow, ALU.mult))
                step(nc.vector.tensor_tensor(t[:, 1, 0:half], t[:, 1, 0:half], wrow[:, half:HD0], ALU.mult))
                step(nc.vector.tensor_tensor(t[:, 1, half:HD0], t[:, 1, half:HD0], wrow[:, 0:half], ALU.mult))

            dve.wait_ge(pool_prep, 2)
            dve.wait_ge(act_prep, 1)
            nc.vector.memset(row_max[:], 0.0).then_inc(dve_done, 1)
            nc.vector.memset(carrier[:], 0.0).then_inc(tile_done, 1)

            n = [0]

            def link(L, b, ins):
                n[0] += 1
                ins.then_inc(L.chain, 1)
                dve.wait_ge(L.chain, b * L.steps + n[0])

            def carry_wait():
                nc.vector.memset(carrier[:], 0.0)

            def bank(L, key, w=512):
                return ps_p[:, L.p.at[key] % 2, 0:w]

            def taken(L, b, key, ins):
                ins.then_inc(L.proj_taken, 1)
                dve.wait_ge(L.proj_taken, L.p.done(b, key))

            def normalise(L, N, b, i, key, src, dst, add=None, scale=None):
                res, stats, mean_var, rstd = (t[:] for t in (N.res, N.stats, N.mean_var, N.rstd))
                dve.wait_ge(L.proj, L.p.done(b, key))
                if scale is not None:
                    taken(L, b, key, nc.vector.tensor_tensor(res, bank(L, key, D), scale, ALU.mult))
                    link(L, b, nc.vector.tensor_tensor(res, res, src[:], ALU.add))
                else:
                    taken(L, b, key, nc.vector.tensor_tensor(res, bank(L, key, D), src[:], ALU.add))
                if add is not None:
                    link(L, b, nc.vector.tensor_tensor(res, res, add, ALU.add))
                link(L, b, nc.vector.bn_stats(stats, res))
                carry_wait()
                link(L, b, nc.vector.bn_aggr(mean_var, stats))
                nc.vector.tensor_scalar(mean_var[:, 1:2], mean_var[:, 1:2], LN_EPS, None, ALU.add)\
                    .then_inc(N.varied, 1)
                dve.wait_ge(N.rstd_ready, b * 3 + i + 1)
                nc.vector.tensor_scalar(dst[:], res, mean_var[:, 0:1], rstd, ALU.subtract, ALU.mult)\
                    .then_inc(N.x_ready, 1)

            def group_step(L, b, g0, count, mask, s):
                g = g0 + s
                psum = heads(ps_s[:, g % 2, :], GH)
                p = heads(probs[:, g % 4, :], GH)
                if s < count:
                    dve.wait_ge(L.scores, b * L.groups + g + 1)
                if s < count and mask is not None:
                    if g >= 4:
                        dve.wait_ge(L.trans, L.t.done(b, L.group_key(g - 4)))
                    nc.vector.tensor_tensor(p, psum, mask.unsqueeze(1).broadcast_to([P, GH, P]), ALU.add)\
                        .then_inc(L.masked, 1)
                if s >= 1:
                    q = heads(probs[:, (g - 1) % 4, :], GH)
                    if mask is None:
                        dve.wait_ge(L.trans, L.t.done(b, L.group_key(g - 5)))
                    dve.wait_ge(L.maxed, b * L.groups + g)
                    nc.vector.tensor_tensor(q, heads(ps_s[:, (g - 1) % 2, :], GH) if mask is None else q,
                                            row_max[:, (g - 1) % 4, :].unsqueeze(2).broadcast_to([P, GH, P]),
                                            ALU.subtract).then_inc(L.shifted, 1)
                if s < count:
                    if mask is not None:
                        dve.wait_ge(L.masked, b * L.masks + g + 1)
                    nc.vector.tensor_reduce(row_max[:, g % 4, :], psum if mask is None else p, X, ALU.max)\
                        .then_inc(L.maxed, 1)

            with dve.Fori(0, TILES) as b:
                n[0] = 0
                half = HD0 // 2

                def rotate(c):
                    table = rope_k if c == 0 else rope_q
                    src = heads(ps_p[:, c % 2, :], 8)
                    t1, t2 = heads(ropes[:, c % 2, :], 8), heads(ropes[:, 2, :], 8)
                    dve.wait_ge(squared, b * 5 + c + 1)
                    if c >= 2:
                        dve.wait_ge(normed, b * 5 + c - 1)
                    if c >= 1:
                        dve.wait_ge(L0.proj_taken, b * P0.count + c)
                    nc.vector.tensor_tensor(t1, src, table[:, 0, :].unsqueeze(1).broadcast_to([P, 8, HD0]), ALU.mult)
                    nc.vector.tensor_tensor(t2[:, :, 0:half], src[:, :, half:HD0],
                                            table[:, 1, 0:half].unsqueeze(1).broadcast_to([P, 8, half]), ALU.mult)
                    link(L0, b, nc.vector.tensor_tensor(t2[:, :, half:HD0], src[:, :, 0:half],
                                                 table[:, 1, half:HD0].unsqueeze(1).broadcast_to([P, 8, half]),
                                                 ALU.mult))
                    nc.vector.tensor_tensor(t1, t1, t2, ALU.add).then_inc(L0.proj_taken, 1)
                    if c >= 2:
                        dve.wait_ge(rmsed, b * 5 + c - 1)
                    link(L0, b, nc.vector.tensor_reduce(mean_sq[:, c % 2, :], heads(squares[:, c % 2, :], 8), X, ALU.add))
                    nc.vector.tensor_scalar(mean_sq[:, c % 2, :], mean_sq[:, c % 2, :], 1.0 / HD0, RMS_EPS,
                                            ALU.mult, ALU.add).then_inc(msq, 1)

                def scale_heads(c):
                    dve.wait_ge(rmsed, b * 5 + c + 1)
                    dve.wait_ge(L0.proj_taken, b * P0.count + c + 1)
                    r = rms[:, c % 2, :].unsqueeze(2).broadcast_to([P, 8, HD0])
                    t1 = heads(ropes[:, c % 2, :], 8)
                    if c == 0:
                        nc.vector.tensor_tensor(kdup[:, :, 0, :], t1, r, ALU.mult)
                        nc.vector.tensor_tensor(kdup[:, :, 1, :], t1, r, ALU.mult).then_inc(normed, 1)
                    else:
                        nc.vector.tensor_tensor(heads(big[:, 512 * (c - 1):512 * c], 8), t1, r, ALU.mult)\
                            .then_inc(normed, 1)

                for c in range(6):
                    if c < 5:
                        rotate(c)
                    if c >= 1:
                        scale_heads(c - 1)
                dve.wait_ge(L0.proj, L0.p.done(b, "v"))
                nc.vector.tensor_copy(v0[:, :, 0:HD0], heads(bank(L0, "v"), KV0)).then_inc(L0.proj_taken, 1)

                def out0_norm(g):
                    dve.wait_ge(L0.summed, b * GROUPS0 + g + 1)
                    o = heads(ps_o[:, g % 2, :], GH)
                    if g >= 2:
                        dve.wait_ge(out0_ready, b * KV0 + g - 1)
                    r = recips[:, g % 2, 0:GH]
                    link(L0, b, nc.vector.reciprocal(r, o[:, :, HD0]))
                    nc.vector.tensor_tensor(heads(big[:, 512 * (g // 2):512 * (g // 2 + 1)], 8)[:, g % 2::2, :], o[:, :, 0:HD0],
                                            r.unsqueeze(2).broadcast_to([P, GH, HD0]), ALU.mult)\
                        .then_inc(out0_ready, 1)

                for s in range(KV0 + 1):
                    group_step(L0, b, 0, KV0, mask_window[:], s)
                    if s >= 4:
                        out0_norm(s - 4)
                for g in range(KV0 - 3, KV0):
                    out0_norm(g)

                dve.wait_ge(ld_tilectx, b * 32 + 32)
                link(L0, b, nc.vector.tensor_scalar(mask_in[:], mask_in[:], float(np.finfo(np.float32).min), None, ALU.max))
                if debug <= 3:
                    dve.wait_ge(mid_stored, b * 16 + 16)
                normalise(L0, N0, b, 0, "out0", xin, xa)
                dve.wait_ge(L0.proj, P0.done(b, "ck"))
                nc.vector.tensor_copy(ak_pad[:, :, 0:HDX], heads(bank(L0, "ck", D), HX)).then_inc(L0.proj_taken, 1)
                dve.wait_ge(L0.proj, P0.done(b, "cv"))
                nc.vector.tensor_copy(avx[:, :, 0:HDX], heads(bank(L0, "cv", D), HX)).then_inc(L0.proj_taken, 1)
                dve.wait_ge(ld_kv2, 16 * 2)
                dve.wait_ge(L0.proj, L0.p.done(b, "k2"))
                nc.vector.tensor_tensor(kf, bank(L0, "k2", D), b_kv2[:, 0:D], ALU.add).then_inc(L0.proj_taken, 1)
                dve.wait_ge(L0.proj, L0.p.done(b, "v2"))
                dve.wait_ge(values_stored, b * 16 + 16)
                nc.vector.tensor_tensor(value_tile, bank(L0, "v2", D), b_kv2[:, D:2 * D], ALU.add)\
                    .then_inc(L0.proj_taken, 1)

                hh = HDX // 2
                dve.wait_ge(L0.proj, L0.p.done(b, "qkx"))
                src = bank(L0, "qkx").rearrange("p (s h d) -> p s h d", s=2, h=HX)
                t1 = ropes[:, 0, :].rearrange("p (s h d) -> p s h d", s=2, h=HX)
                t2 = ropes[:, 1, :].rearrange("p (s h d) -> p s h d", s=2, h=HX)
                for s in range(2):
                    nc.vector.tensor_tensor(t1[:, s], src[:, s], rope_x[:, 0, s, :].unsqueeze(1)
                                            .broadcast_to([P, HX, HDX]), ALU.mult)
                    nc.vector.tensor_tensor(t2[:, s, :, 0:hh], src[:, s, :, hh:HDX], rope_x[:, 1, s, 0:hh].unsqueeze(1)
                                            .broadcast_to([P, HX, hh]), ALU.mult)
                    ins = nc.vector.tensor_tensor(t2[:, s, :, hh:HDX], src[:, s, :, 0:hh], rope_x[:, 1, s, hh:HDX]
                                                  .unsqueeze(1).broadcast_to([P, HX, hh]), ALU.mult)
                ins.then_inc(L0.proj_taken, 1)
                dve.wait_ge(L0.proj_taken, L0.p.done(b, "qkx"))
                nc.vector.tensor_tensor(qk_pad[:, :, 0:HDX], heads(ropes[:, 0, :], 2 * HX),
                                        heads(ropes[:, 1, :], 2 * HX), ALU.add).then_inc(qkx_ready, 1)
                dve.wait_ge(L0.proj, L0.p.done(b, "vx"))
                nc.vector.tensor_copy(vx[:, :, 0:HDX], heads(bank(L0, "vx", D), HX)).then_inc(L0.proj_taken, 1)
                for s in range(GX + 1):
                    group_step(L0, b, KV0, GX, mask_in[:], s)
                for s in range(GX + 1):
                    group_step(L0, b, KV0 + GX, GX, None, s)
                wx = HX * (HDX + 1)
                o1, o2 = (ps_o[:, i, 0:wx].rearrange("p (a m d) -> p m a d", a=4, d=HDX + 1) for i in range(2))

                def hx(ap):
                    return ap.rearrange("p (m a d) -> p m a d", a=4, d=HDX)

                def rx(i):
                    return recips[:, i, :].rearrange("p (m a) -> p m a", a=4)

                dve.wait_ge(L0.summed, b * GROUPS0 + GROUPS0)
                link(L0, b, nc.vector.reciprocal(rx(0), o1[:, :, :, HDX]))
                link(L0, b, nc.vector.reciprocal(rx(1), o2[:, :, :, HDX]))
                link(L0, b, nc.vector.tensor_tensor(recips[:, 1, :], recips[:, 1, :], tanh_gate[:], ALU.mult))
                link(L0, b, nc.vector.tensor_tensor(hx(att[:]), o1[:, :, :, 0:HDX],
                                             rx(0).unsqueeze(3).broadcast_to([P, HX // 4, 4, HDX]), ALU.mult))
                link(L0, b, nc.vector.tensor_tensor(hx(res[:]), o2[:, :, :, 0:HDX],
                                             rx(1).unsqueeze(3).broadcast_to([P, HX // 4, 4, HDX]), ALU.mult))
                nc.vector.tensor_tensor(att[:], att[:], res[:], ALU.add).then_inc(heads_x, 1)
                normalise(L0, N0, b, 1, "outx", xa, xb)

                dve.wait_ge(L0.proj, L0.p.done(b, "logits"))
                lg = bank(L0, "logits", E)
                nc.vector.tensor_reduce(router[:, 0, 0:1], lg, X, ALU.max, negate=True).then_inc(logit_max, 1)
                dve.wait_ge(logit_exp, b + 1)
                nc.vector.reciprocal(router[:, 0, 2:3], router[:, 0, 1:2]).then_inc(L0.proj_taken, 1)
                dve.wait_ge(L0.proj_taken, L0.p.done(b, "logits"))
                link(L0, b, nc.vector.memset(router[:, 2, E:E + 1], -1.0))
                link(L0, b, nc.vector.memset(router[:, 2, E + 1:E + 2], -2.0))
                link(L0, b, nc.vector.tensor_scalar(router[:, 2, 0:E], router[:, 1, 0:E], router[:, 0, 2:3], None, ALU.mult))
                carry_wait()
                link(L0, b, nc.vector.max(router[:, 3, 0:8], router[:, 2, 0:E]))
                link(L0, b, nc.vector.tensor_copy(router[:, 3, TOPK:8], router[:, 2, E:E + 2]))
                carry_wait()
                link(L0, b, nc.vector.match_replace(router[:, 4, 0:E + 2], router[:, 3, 0:8], router[:, 2, 0:E + 2], -3.0))
                link(L0, b, nc.vector.tensor_scalar(router[:, 5, 0:E], router[:, 4, 0:E], -3.0, 0.5, ALU.is_equal, ALU.mult))
                link(L0, b, nc.vector.tensor_tensor(router[:, 6, 0:E], router[:, 5, 0:E], router[:, 2, 0:E], ALU.mult))
                def per_head(i):
                    return key_scale[:, i, :].unsqueeze(2).broadcast_to([P, H1, HD1])

                def context_keys(c):
                    if c == 0:
                        link(L0, b, nc.vector.tensor_reduce(key_scale[:, 0, :], heads(kf, H1), X, ALU.max,
                                                            apply_absolute_value=True))
                        link(L0, b, nc.vector.tensor_scalar(key_scale[:, 0, :], key_scale[:, 0, :], 1.0 / 127.0, 1e-8,
                                                            ALU.mult, ALU.max))
                    elif c == 1:
                        link(L0, b, nc.vector.reciprocal(key_scale[:, 1, :], key_scale[:, 0, :]))
                        link(L0, b, nc.vector.tensor_tensor(heads(kq, H1), heads(kf, H1), per_head(1), ALU.mult))
                    elif c == 2:
                        link(L0, b, nc.vector.tensor_scalar(kq, kq, ROUND, ROUND, ALU.add, ALU.subtract))
                        link(L0, b, nc.vector.tensor_scalar(kq, kq, 127.0, -127.0, ALU.min, ALU.max))
                    elif c == 3:
                        link(L0, b, nc.vector.tensor_tensor(heads(kf, H1), heads(kq, H1), per_head(0), ALU.mult))
                        link(L0, b, nc.vector.tensor_copy(key_stack[:, :, 0:16], heads(kf, H1)))
                    elif c == 4:
                        link(L0, b, nc.vector.tensor_tensor(heads(r1, H1), heads(kf, H1), key_stack[:, :, 0:16],
                                                            ALU.subtract))
                        link(L0, b, nc.vector.tensor_copy(key_stack[:, :, 16:32], heads(r1, H1)))
                    elif c == 5:
                        link(L0, b, nc.vector.tensor_tensor(heads(r2, H1), heads(r1, H1), key_stack[:, :, 16:32],
                                                            ALU.subtract))
                        nc.vector.tensor_copy(key_stack[:, :, 32:48], heads(r2, H1)).then_inc(c_stack, 1)

                for c in range(CHUNKS):
                    g = (ps_p if c % 2 else ps_s)[:, 0, 0:CW]
                    u = (ps_p if c % 2 else ps_s)[:, 1, 0:CW]
                    dve.wait_ge(tanhed, b * CHUNKS + c + 1)
                    link(L0, b, nc.vector.scalar_tensor_tensor(gg[:, c % 2, :], th[:, c % 2, :], 1.0, g, ALU.add, ALU.mult))
                    for e in range(EC):
                        ins = nc.vector.scalar_tensor_tensor(
                            big[:, c * CW + e * F:c * CW + (e + 1) * F], gg[:, c % 2, e * F:(e + 1) * F],
                            router[:, 6, c * EC + e:c * EC + e + 1], u[:, e * F:(e + 1) * F], ALU.mult, ALU.mult)
                    ins.then_inc(hidden, 1)
                    context_keys(c)
                dve.wait_ge(mid_stored, b * 16 + 16)
                normalise(L0, N0, b, 2, "down", xb, xc)
                dve.wait_ge(N0.x_ready, b * 3 + 3)
                nc.vector.memset(carrier[:], 0.0).then_inc(tile_done, 1)
                assert n[0] == CHAIN0, n[0]

            if debug <= 3:
                return

            def round_fp8(src, dst, w):
                dst = dst.rearrange("p a b -> p (a b)")
                f8a, f8b = round_low.bitcast(FP8)[:, 0:w], round_high.bitcast(FP8)[:, 0:w]
                step(nc.vector.tensor_scalar(f8a, src, FP8_MAX, -FP8_MAX, ALU.min, ALU.max, saturate=False))
                step(nc.vector.tensor_scalar(f8b, src, 0.5, None, ALU.mult, saturate=False))
                step(nc.vector.tensor_scalar(round_sel.bitcast(U32)[:, 0:w], src.bitcast(U32), 1, 31,
                                             ALU.logical_shift_left, ALU.logical_shift_right))
                step(nc.vector.tensor_copy(dst, f8a))
                step(nc.vector.tensor_scalar(round_two[:, 0:w], f8b, 2.0, None, ALU.mult))
                step(nc.vector.copy_predicated(dst, round_sel.bitcast(U32)[:, 0:w], round_two[:, 0:w]))

            dve.wait_ge(ld_w["ffn"], 16 * 2)
            round_fp8(ffn_gate, w_gate1, KD * I1)
            dve.wait_ge(ld_values, 16)
            nc.vector.tensor_reduce(att[:], values.rearrange("p t n -> p n t"), X, ALU.max,
                                    apply_absolute_value=True).then_inc(c_vals, 1)
            round_fp8(ffn_up, w_up1, KD * I1)
            dve.wait_ge(c_amax, 1)
            step(nc.vector.tensor_scalar(v_scale[:], res[:], 1.0 / 127.0, 1e-8, ALU.mult, ALU.max))
            nc.vector.reciprocal(att[:], v_scale[:]).then_inc(v_scaled, 1)
            dve.wait_ge(ld_w["down1"], 16)
            round_fp8(ffn_down, w_down1, IB * D)
            for lane in lanes:
                step(nc.vector.memset(lane.v_wide, 1.0))
                step(nc.vector.memset(lane.stack, 0.0))
            step(nc.vector.memset(lanes[1].qk_pad, 0.0))
            nc.vector.memset(carrier[:], 0.0).then_inc(pair_done, 1)
            dve.wait_ge(ld_w["l1"], 16 * 9)
            dve.wait_ge(ld_w["scales1"], 16 * 2)

            last = [0, 0]

            def both(b, make):
                for lane in lanes:
                    if last[lane.i]:
                        dve.wait_ge(L1.chain, b * L1.steps + last[lane.i])
                    make(lane).then_inc(L1.chain, 1)
                    n[0] += 1
                    last[lane.i] = n[0]

            def end_both(b, make, signal):
                for lane in lanes:
                    dve.wait_ge(L1.chain, b * L1.steps + last[lane.i])
                    make(lane).then_inc(signal(lane), 1)
                    last[lane.i] = 0

            def split_both(b, src, part, tmp, signal):
                both(b, lambda w: nc.vector.tensor_copy(part(w, 0), src(w)))
                both(b, lambda w: nc.vector.tensor_tensor(tmp(w), src(w), part(w, 0), ALU.subtract))
                both(b, lambda w: nc.vector.tensor_copy(part(w, 1), tmp(w)))
                end_both(b, lambda w: nc.vector.tensor_tensor(part(w, 2), tmp(w), part(w, 1), ALU.subtract), signal)

            def normalise_both(b, i, key, add=None, scale=None):
                for lane in lanes:
                    dve.wait_ge(L1.proj, L1.p.done(b, (key, lane.i)))
                    nc.vector.tensor_tensor(lane.res, bank(L1, (key, lane.i), D),
                                            lane.x[3 + i] if scale is None else scale,
                                            ALU.add if scale is None else ALU.mult).then_inc(L1.proj_taken, 1)
                for lane in lanes:
                    dve.wait_ge(L1.proj_taken, L1.p.done(b, (key, lane.i)))
                both(b, lambda w: nc.vector.tensor_tensor(w.res, w.res, add if scale is None else w.x[3 + i], ALU.add))
                both(b, lambda w: nc.vector.bn_stats(w.stats, w.res))
                for lane in lanes:
                    dve.wait_ge(L1.chain, b * L1.steps + last[lane.i])
                carry_wait()
                last[:] = 0, 0
                both(b, lambda w: nc.vector.bn_aggr(w.mean_var, w.stats))
                end_both(b, lambda w: nc.vector.tensor_scalar(w.mean_var[:, 1:2], w.mean_var[:, 1:2], LN_EPS, None,
                                                              ALU.add), lambda w: w.varied)
                for lane in lanes:
                    dve.wait_ge(lane.rstd_ready, b * 3 + i + 1)
                    nc.vector.tensor_scalar(lane.x[4 + i], lane.res, lane.mean_var[:, 0:1], lane.rstd, ALU.subtract,
                                            ALU.mult).then_inc(lane.x_ready, 1)

            def attention(b, lane):
                i, att = lane.i, lane.att
                if i == 0:
                    dve.wait_ge(v_quantised, 1)
                for s in range(G1 + 1):
                    group_step(L1, b, i * G1, G1, mask_causal[:], s)
                o1 = ps_o[:, i, 0:H1 * (HD1 + 1)].rearrange("p (a m d) -> p m a d", a=4, d=HD1 + 1)
                r1x = recips[:, i, 0:H1].rearrange("p (m a) -> p m a", a=4)
                dve.wait_ge(L1.summed, b * GROUPS1 + (i + 1) * G1)
                link(L1, b, nc.vector.reciprocal(r1x, o1[:, :, :, HD1]))
                nc.vector.tensor_tensor(att.rearrange("p (m a d) -> p m a d", a=4, d=HD1), o1[:, :, :, 0:HD1],
                                        r1x.unsqueeze(3).broadcast_to([P, H1 // 4, 4, HD1]), ALU.mult)\
                    .then_inc(lane.heads_1, 1)

            def queries(b):
                def scales(w, i):
                    return w.q2s[:, i, :]

                for lane in lanes:
                    dve.wait_ge(L1.proj, L1.p.done(b, ("q2x", lane.i)))
                    nc.vector.tensor_tensor(lane.q2, bank(L1, ("q2x", lane.i), D), b_q2, ALU.add)\
                        .then_inc(L1.proj_taken, 1)
                for lane in lanes:
                    dve.wait_ge(L1.proj_taken, L1.p.done(b, ("q2x", lane.i)))
                both(b, lambda w: nc.vector.tensor_scalar(w.q2, w.q2, HD1 ** -0.5, None, ALU.mult))
                both(b, lambda w: nc.vector.tensor_reduce(scales(w, 0), heads(w.q2, H1), X, ALU.max,
                                                          apply_absolute_value=True))
                both(b, lambda w: nc.vector.tensor_scalar(scales(w, 0), scales(w, 0), 1.0 / 127.0, 1e-8, ALU.mult,
                                                          ALU.max))
                both(b, lambda w: nc.vector.reciprocal(scales(w, 1), scales(w, 0)))
                both(b, lambda w: nc.vector.tensor_tensor(heads(w.q2, H1), heads(w.q2, H1), scales(w, 1).unsqueeze(2)
                                                          .broadcast_to([P, H1, HD1]), ALU.mult))
                both(b, lambda w: nc.vector.tensor_scalar(w.q2, w.q2, ROUND, ROUND, ALU.add, ALU.subtract))
                both(b, lambda w: nc.vector.tensor_scalar(w.q2, w.q2, 127.0, -127.0, ALU.min, ALU.max))
                both(b, lambda w: nc.vector.tensor_scalar(scales(w, 2), scales(w, 0), -1.0, None, ALU.mult))
                for lane in lanes:
                    dve.wait_ge(L1.chain, b * L1.steps + last[lane.i])
                    for part in range(3):
                        ins = nc.vector.tensor_copy(lane.stack[:, :, 16 * part:16 * part + 16], heads(lane.q2, H1))
                    ins.then_inc(lane.q2_ready, 1)
                last[:] = 0, 0

            def shared(b, lane):
                i, key = lane.i, ("av2x", lane.i)
                q2s, max2, att = lane.q2s, lane.max2, lane.att
                for h in range(H1 + 1):
                    if h < H1:
                        dve.wait_ge(lane.s2, b * H1 + h + 1)
                        link(L1, b, nc.vector.tensor_reduce(max2[:, 0, h:h + 1],
                                                            (ps_s if h % 2 == 0 else ps_o)[:]
                                                            .rearrange("p a b -> p (a b)"), X, ALU.max))
                        nc.vector.tensor_scalar(max2[:, 1, h:h + 1], max2[:, 0, h:h + 1], q2s[:, 2, h:h + 1],
                                                LN255, ALU.mult, ALU.add).then_inc(lane.max2_ready, 1)
                    if h >= 1:
                        dve.wait_ge(lane.exp2, b * H1 + h)
                        if h >= 3:
                            dve.wait_ge(L1.trans, L1.t.done(b, (("n", h - 3), i)))
                        elif i:
                            dve.wait_ge(L1.trans, L1.t.done(b, (("n", H1 - 3 + h), 0)))
                        nc.vector.tensor_scalar(n2[:, (h - 1) % 2, :], e2[:, (h - 1) % 2, :], ROUND, ROUND,
                                                ALU.add, ALU.subtract).then_inc(lane.round2, 1)
                dve.wait_ge(L1.proj, L1.p.done(b, key))
                link(L1, b, nc.vector.reciprocal(recips[:, i, 0:H1], q2s[:, 3, :]))
                nc.vector.tensor_tensor(heads(att, H1), heads(bank(L1, key, D), H1),
                                        recips[:, i, 0:H1].unsqueeze(2).broadcast_to([P, H1, HD1]), ALU.mult)\
                    .then_inc(L1.proj_taken, 1)
                dve.wait_ge(L1.proj_taken, L1.p.done(b, key))
                nc.vector.tensor_tensor(att, att, v_scale[:], ALU.mult).then_inc(lane.heads_2, 1)

            def ffn(b):
                for lane in lanes:
                    dve.wait_ge(L1.trans_taken, L1.t.done(b, (("x", 5), lane.i)))

                def tmp(lane, w=KD):
                    return lane.res.rearrange("p (k q) -> p k q", k=KD)[:, 0:w, :]

                split_both(b, lambda w: w.xT[5], lambda w, part: w.x5p[:, part], tmp, lambda w: w.parts5)
                for c in range(2):
                    cols = slice(c * FW, (c + 1) * FW)
                    for lane in lanes:
                        bank = ps_o if lane.i else ps_s
                        dve.wait_ge(lane.gate_up1, b * 2 + c + 1)
                        if c:
                            dve.wait_ge(lane.fused, b * 2 + c)
                        nc.vector.tensor_tensor(lane.gs, bank[:, 0, 0:FW], s_gate1[:, cols], ALU.mult)\
                            .then_inc(lane.scaled1, 1)
                        link(L1, b, nc.vector.tensor_tensor(lane.us, bank[:, 1, 0:FW], s_up1[:, cols], ALU.mult))
                    for lane in lanes:
                        dve.wait_ge(lane.tanhed1, b * 2 + c + 1)
                    both(b, lambda w: nc.vector.scalar_tensor_tensor(w.gs, w.tt, 1.0, w.gs, ALU.add, ALU.mult))
                    end_both(b, lambda w: nc.vector.scalar_tensor_tensor(w.fuse[:, cols], w.gs, 0.5, w.us, ALU.mult,
                                                                         ALU.mult), lambda w: w.fused)
                for j, (k, width) in enumerate(zip(FB0, FBS)):
                    for lane in lanes:
                        dve.wait_ge(L1.trans_taken, L1.t.done(b, (("f", j), lane.i)))
                        if j:
                            dve.wait_ge(lane.fparts, b * len(FBS) + j)
                    split_both(b, lambda w: w.fuseT[:, k:k + width, :], lambda w, part: w.fusep[:, part, k:k + width, :],
                               lambda w: tmp(w, width), lambda w: w.fparts)

            with dve.Fori(0, PAIRS) as b:
                n[0] = 0
                for i, part in enumerate(("q1", "k1")):
                    for lane in lanes:
                        dve.wait_ge(L1.proj, L1.p.done(b, (part, lane.i)))
                        nc.vector.tensor_tensor(lane.qk_pad[:, H1 * i:H1 * (i + 1), 0:HD1],
                                                heads(bank(L1, (part, lane.i), D), H1),
                                                heads(b_qkv1[:, D * i:D * (i + 1)], H1), ALU.add)\
                            .then_inc(L1.proj_taken, 1)
                for lane in lanes:
                    dve.wait_ge(L1.proj, L1.p.done(b, ("v1", lane.i)))
                    nc.vector.tensor_tensor(lane.v[:, :, 0:HD1], heads(bank(L1, ("v1", lane.i), D), H1),
                                            heads(b_qkv1[:, 2 * D:3 * D], H1), ALU.add).then_inc(L1.proj_taken, 1)
                for lane in lanes:
                    attention(b, lane)
                normalise_both(b, 0, "out1", add=b_out1)
                queries(b)
                for lane in lanes:
                    shared(b, lane)
                normalise_both(b, 1, "out2x", add=b_p2)
                ffn(b)
                for lane in lanes:
                    dve.wait_ge(lane.stored, b * 16 + 16)
                normalise_both(b, 2, "down1", scale=s_down1)
                for lane in lanes:
                    dve.wait_ge(lane.x_ready, b * 3 + 3)
                nc.vector.memset(carrier[:], 0.0).then_inc(pair_done, 1)
                assert n[0] == CHAIN1, n[0]

        @block.tensor
        def _(pe):
            pe.wait_ge(ld_ident, 16)
            pe.wait_ge(dve_done, 1)
            pe.wait_ge(ld_w["k0"], 16)

            def project(L, b, key, xTi, w, col, width):
                n = L.p.at[key]
                if n >= 2:
                    pe.wait_ge(L.proj_taken, b * L.p.count + n - 1)
                kk = w.shape[1]
                for k in range(kk):
                    ins = nc.tensor.matmul(ps_p[:, n % 2, 0:width], xTi[:, k, :], w[:, k, col:col + width],
                                           start=(k == 0), stop=(k == kk - 1))
                ins.then_inc(L.proj, 1)

            def transpose(L, b, key, src, nblocks, bf=False):
                t = L.t.at[key]
                if t >= 2:
                    pe.wait_ge(L.trans_taken, b * L.t.count + t - 1)
                dst = ps_t[:, t % 2, :].bitcast(BF16) if bf else ps_t[:, t % 2, :]
                for i in range(nblocks):
                    ins = nc.tensor.transpose(dst[:, i * P:(i + 1) * P], src(i), ident_b[:] if bf else ident[:])
                ins.then_inc(L.trans, 1)

            def keep_warm():
                for _ in range(WARM):
                    nc.tensor.matmul(ps_s[:, 0, 0:P], ident_b[:], ident_b[:], start=True, stop=True)

            def group_scores(L, b, g, q, k):
                if g >= 2:
                    if g - 2 < L.masks:
                        pe.wait_ge(L.masked, b * L.masks + g - 1)
                    else:
                        pe.wait_ge(L.shifted, b * L.groups + g - 1)
                for i in range(GH):
                    ins = nc.tensor.matmul(ps_s[:, g % 2, i * P:(i + 1) * P], q(i), k(i), start=True, stop=True)
                ins.then_inc(L.scores, 1)

            def group_transpose(L, b, g):
                pe.wait_ge(L.exped, b * L.groups + g + 1)
                transpose(L, b, L.group_key(g), lambda i: probs[:, g % 4, i * P:(i + 1) * P], GH)

            def group_sum(L, b, g, dst, v):
                pe.wait_ge(L.trans_taken, L.t.done(b, L.group_key(g)))
                for i in range(GH):
                    ins = nc.tensor.matmul(dst(i), probsT[:, g % 2, i * P:(i + 1) * P], v(i), start=True, stop=True)
                ins.then_inc(L.summed, 1)

            def wide(ap, n, w):
                return ap[:, n * w:n * w + WIDE]

            def x_transpose(L, b, key, x):
                transpose(L, b, key, lambda k: x[:, k * P:(k + 1) * P], KD)
                pe.wait_ge(L.trans_taken, L.t.done(b, key))

            def padded(ap, first):
                return ap[:, first:first + 4, :].rearrange("p a b -> p (a b)")

            with pe.Fori(0, TILES) as b:
                pe.wait_ge(ld_x, b * 32 + 32)
                nq = H0 * HD0
                project(L0, b, "k", xT[0], w_qkv0, nq, 512)
                pe.wait_ge(tile_done, b + 1)
                pe.wait_ge(ld_w["qkv0"], 16 * 2)
                project(L0, b, "q0", xT[0], w_qkv0, 0, 512)
                project(L0, b, "q1", xT[0], w_qkv0, 512, 512)
                pe.wait_ge(normed, b * 5 + 1)
                for j in range(2):
                    transpose(L0, b, ("k0", j), lambda i: kdup[:, 4 * j + i].rearrange("p a b -> p (a b)"), 4)
                project(L0, b, "q2", xT[0], w_qkv0, 1024, 512)

                def q0_transpose(j):
                    keep_warm()
                    pe.wait_ge(normed, b * 5 + j + 2)
                    transpose(L0, b, ("q0", j), lambda i: big[:, (4 * j + i) * P:(4 * j + i + 1) * P], 4)

                q0_transpose(0)
                project(L0, b, "q3", xT[0], w_qkv0, 1536, 512)
                q0_transpose(1)
                project(L0, b, "v", xT[0], w_qkv0, nq + 512, 512)
                q0_transpose(2)
                q0_transpose(3)
                pe.wait_ge(L0.trans_taken, L0.t.done(b, ("q0", 3)))
                pe.wait_ge(L0.proj_taken, L0.p.done(b, "v"))

                def rows(i):
                    return slice(HD0 * (i % 2), HD0 * (i % 2) + HD0)

                for s in range(KV0 + 3):
                    if s < KV0:
                        group_scores(L0, b, s, lambda i: bigT[rows(s), head0(s, i) // 2, :],
                                     lambda i: k0T[rows(s), head0(s, i) // 4, :])
                    if 2 <= s < KV0 + 2:
                        group_transpose(L0, b, s - 2)
                    if s >= 3:
                        g = s - 3
                        if g >= 2:
                            pe.wait_ge(out0_ready, b * KV0 + g - 1)
                        group_sum(L0, b, g, lambda i: ps_o[:, g % 2, i * WIDE:(i + 1) * WIDE],
                                  lambda i: wide(v0_wide, head0(g, i) // 4, HD0 + 1))
                for j in range(4):
                    pe.wait_ge(out0_ready, b * KV0 + 2 * j + 2)
                    transpose(L0, b, ("o0", j), lambda i: big[:, (4 * j + i) * P:(4 * j + i + 1) * P], 4)
                pe.wait_ge(L0.trans_taken, L0.t.done(b, ("o0", 3)))
                pe.wait_ge(ld_w["att0"], 16 * 5)
                project(L0, b, "out0", bigT, w_out0, 0, D)

                pe.wait_ge(ld_tilectx, b * 32 + 32)
                project(L0, b, "ck", ctxT, w_x, D, D)
                project(L0, b, "cv", ctxT, w_x, 2 * D, D)
                pe.wait_ge(ld_kv2, 16 * 2)
                project(L0, b, "k2", ctxT, w_kv2, 0, D)
                project(L0, b, "v2", ctxT, w_kv2, D, D)
                pe.wait_ge(L0.proj_taken, P0.done(b, "ck"))
                for j in range(2):
                    transpose(L0, b, ("ak", j), lambda i: padded(ak_pad, 16 * j + 4 * i), 4)
                keep_warm()
                pe.wait_ge(N0.x_ready, b * 3 + 1)
                x_transpose(L0, b, ("x", 1), xa)
                project(L0, b, "qkx", xT[1], w_x, 0, 2 * D)
                project(L0, b, "vx", xT[1], w_x, 2 * D, D)
                keep_warm()
                pe.wait_ge(qkx_ready, b + 1)
                for j in range(4):
                    transpose(L0, b, ("qk", j), lambda i: padded(qk_pad, 16 * j + 4 * i), 4)
                pe.wait_ge(L0.trans_taken, L0.t.done(b, ("qk", 3)))
                pe.wait_ge(L0.proj_taken, L0.p.done(b, "vx"))
                gx, g0 = GX, KV0
                for s in range(2 * gx + 3):
                    if s < 2 * gx:
                        keysT, m = (qkT[:, 8:16, :], s) if s < gx else (akT, s - gx)
                        r = slice(PAD * (m // 2), PAD * (m // 2) + HDX)
                        group_scores(L0, b, g0 + s, lambda i: qkT[r, headx(m, i) // 4, :],
                                     lambda i: keysT[r, headx(m, i) // 4, :])
                    if 2 <= s < 2 * gx + 2:
                        group_transpose(L0, b, g0 + s - 2)
                    if s >= 3:
                        g = s - 3
                        vv, m, w = (vx_wide if g < gx else avx_wide), g % gx, HDX + 1
                        group_sum(L0, b, g0 + g, lambda i: wide(ps_o[:, g // gx, :], GH * m + i, w),
                                  lambda i: wide(vv, headx(m, i), w))
                pe.wait_ge(heads_x, b + 1)
                transpose(L0, b, ("ox", 0), lambda k: att[:, k * P:(k + 1) * P], KD)
                pe.wait_ge(L0.trans_taken, L0.t.done(b, ("ox", 0)))
                project(L0, b, "outx", attT, w_outx, 0, D)

                keep_warm()
                pe.wait_ge(N0.x_ready, b * 3 + 2)
                x_transpose(L0, b, ("x", 2), xb)
                pe.wait_ge(ld_w["moe"], 16 * 4)
                project(L0, b, "logits", xT[2], w_router, 0, E)
                down = P0.at["down"]

                def h_transpose(j):
                    nb, k0 = HB[j], HB0[j]
                    pe.wait_ge(hidden, b * CHUNKS + h_ready(j) + 1)
                    transpose(L0, b, ("h", j), lambda i: big[:, (k0 + i) * P:(k0 + i + 1) * P], nb)

                jt = 0
                for c in range(CHUNKS):
                    if c >= 2:
                        pe.wait_ge(hidden, b * CHUNKS + c - 1)
                    elif c == 1:
                        pe.wait_ge(L0.proj_taken, L0.p.done(b, "logits"))
                    bank = ps_p if c % 2 else ps_s
                    for half, w in ((0, w_gate), (1, w_up)):
                        for k in range(KD):
                            ins = nc.tensor.matmul(bank[:, half, 0:CW], xT[2][:, k, :], w[:, k, c * CW:(c + 1) * CW],
                                                   start=(k == 0), stop=(k == KD - 1))
                    ins.then_inc(gate_up, 1)
                    while jt < len(HB) and h_ready(jt) <= c - 2:
                        h_transpose(jt)
                        jt += 1
                while jt < len(HB):
                    h_transpose(jt)
                    jt += 1
                for k in range(FB):
                    if k in HB0:
                        pe.wait_ge(L0.trans_taken, T0.done(b, ("h", HB0.index(k))))
                    ins = nc.tensor.matmul(ps_p[:, down % 2, 0:D], bigT[:, k, :], w_down[:, k, :], start=(k == 0),
                                           stop=(k == FB - 1))
                ins.then_inc(L0.proj, 1)
                pe.wait_ge(c_stack, b + 1)
                for j in range(2):
                    transpose(L0, b, ("c", j), lambda i: key_stack[:, 8 * j + 2 * i:8 * j + 2 * i + 2, :]
                              .rearrange("p a b -> p (a b)"), 4, bf=True)
            if debug <= 3:
                return
            pe.wait_ge(tile_done, TILES + 1)
            pe.wait_ge(ld_w["l1"], 16 * 9)

            def through(b, key, ready, src, name, dst, w):
                for lane in lanes:
                    ready(lane)
                    transpose(L1, b, (key, lane.i), lambda k: src(lane)[:, k * P:(k + 1) * P], KD)
                for lane in lanes:
                    pe.wait_ge(L1.trans_taken, L1.t.done(b, (key, lane.i)))
                    if name:
                        project(L1, b, (name, lane.i), dst(lane), w, 0, D)

            def attention(b, lane):
                i, g0, w = lane.i, lane.i * G1, HD1 + 1
                pe.wait_ge(L1.trans_taken, L1.t.done(b, (("qk1", 1), i)))
                pe.wait_ge(L1.proj_taken, L1.p.done(b, ("v1", i)))
                for s in range(G1 + 3):
                    if s < G1:
                        group_scores(L1, b, g0 + s, lambda n: lane.qkT[PAD * s:PAD * s + HD1, head1(s, n) // 4, :],
                                     lambda n: lane.qkT[PAD * s:PAD * s + HD1, 4 + head1(s, n) // 4, :])
                    if 2 <= s < G1 + 2:
                        group_transpose(L1, b, g0 + s - 2)
                    if s >= 3:
                        g = s - 3
                        group_sum(L1, b, g0 + g, lambda n: wide(ps_o[:, i, :], GH * g + n, w),
                                  lambda n: wide(lane.v_wide, head1(g, n), w))

            def shared(b, lane):
                i, other = lane.i, lanes[0]
                pe.wait_ge(ld_keys, 16)
                pe.wait_ge(v_quantised, 3)
                pe.wait_ge(L1.trans_taken, L1.t.done(b, (("qs", 0), i)))
                av = L1.p.at["av2x", i]
                pe.wait_ge(L1.proj_taken, b * L1.p.count + av - 1)
                for s in range(H1 + 3):
                    if s < H1:
                        bank = ps_s if s % 2 == 0 else ps_o
                        r = slice(STK * (s % 2), STK * (s % 2) + 3 * HD1)
                        if s >= 2:
                            pe.wait_ge(lane.exp2, b * H1 + s - 1)
                        elif i:
                            pe.wait_ge(other.exp2, b * H1 + H1 - 1 + s)
                        else:
                            pe.wait_ge(L1.masked, b * GROUPS1 + GROUPS1)
                            pe.wait_ge(lanes[1].heads_1, b + 1)
                        for n in range(2):
                            ins = nc.tensor.matmul(bank[:, n, :], lane.stackT[r, s // 2, :],
                                                   keys2T[r, 4 * n:4 * n + 4, s // 2, :], start=True, stop=True)
                        ins.then_inc(lane.s2, 1)
                    if 2 <= s < H1 + 2:
                        h = s - 2
                        pe.wait_ge(lane.round2, b * H1 + h + 1)
                        transpose(L1, b, (("n", h), i), lambda n: n2[:, h % 2, n * P:(n + 1) * P], 8, bf=True)
                    if s >= 3:
                        h = s - 3
                        pe.wait_ge(L1.trans_taken, L1.t.done(b, (("n", h), i)))
                        for n in range(TILES):
                            ins = nc.tensor.matmul(ps_p[:, av % 2, h * HD1:(h + 1) * HD1],
                                                   n2T[:, h % 2, n * P:(n + 1) * P],
                                                   vals2[:, n, h * HD1:(h + 1) * HD1], start=(n == 0),
                                                   stop=(n == TILES - 1))
                        ins.then_inc(lane.out2 if h < H1 - 1 else L1.proj, 1)

            with pe.Fori(0, PAIRS) as b:
                through(b, ("x", 3), lambda lane: pe.wait_ge(lane.ld_mid, b * 16 + 16), lambda lane: lane.x[3], None,
                        None, None)
                for part, name in enumerate(("q1", "k1", "v1")):
                    for lane in lanes:
                        project(L1, b, (name, lane.i), lane.xT[3], w_qkv1, part * D, D)
                        if part + lane.i == 0:
                            pe.wait_ge(pair_done, b + 1)
                for j in range(2):
                    for lane in lanes:
                        pe.wait_ge(L1.proj_taken, L1.p.done(b, (("q1", "k1")[j], lane.i)))
                        transpose(L1, b, (("qk1", j), lane.i), lambda n: padded(lane.qk_pad, 16 * j + 4 * n), 4)
                for lane in lanes:
                    attention(b, lane)
                through(b, ("o1", 0), lambda lane: pe.wait_ge(lane.heads_1, b + 1), lambda lane: lane.att, "out1",
                        lambda lane: lane.attT, w_out1)
                through(b, ("x", 4), lambda lane: pe.wait_ge(lane.x_ready, b * 3 + 1), lambda lane: lane.x[4], "q2x",
                        lambda lane: lane.xT[4], w_q2)
                for lane in lanes:
                    pe.wait_ge(lane.q2_ready, b + 1)
                    transpose(L1, b, (("qs", 0), lane.i), lambda n: lane.stack[:, 2 * n:2 * n + 2, :]
                              .rearrange("p a b -> p (a b)"), 8, bf=True)
                for lane in lanes:
                    shared(b, lane)
                through(b, ("oq", 0), lambda lane: pe.wait_ge(lane.heads_2, b + 1), lambda lane: lane.att, "out2x",
                        lambda lane: lane.attT, w_p2)
                through(b, ("x", 5), lambda lane: pe.wait_ge(lane.x_ready, b * 3 + 2), lambda lane: lane.x[5], None,
                        None, None)
                pe.wait_ge(lanes[1].exp2, b * H1 + H1)
                for c in range(2):
                    for lane in lanes:
                        bank = ps_o if lane.i else ps_s
                        if c == 0:
                            pe.wait_ge(lane.parts5, b + 1)
                        else:
                            pe.wait_ge(lane.fused, b * 2 + 1)
                        for half, w in ((0, w_gate1), (1, w_up1)):
                            for k in range(KD):
                                for part in range(3):
                                    ins = nc.tensor.matmul(bank[:, half, 0:FW], lane.x5p[:, part, k, :],
                                                           w[:, k, c * FW:(c + 1) * FW], start=(k + part == 0),
                                                           stop=(k == KD - 1 and part == 2))
                        ins.then_inc(lane.gate_up1, 1)
                for j, (k, w) in enumerate(zip(FB0, FBS)):
                    for lane in lanes:
                        pe.wait_ge(lane.fused, b * 2 + (1 if j == 0 else 2))
                        transpose(L1, b, (("f", j), lane.i), lambda n: lane.fuse[:, (k + n) * P:(k + n + 1) * P], w)
                for lane in lanes:
                    d1 = L1.p.at["down1", lane.i]
                    pe.wait_ge(L1.proj_taken, b * L1.p.count + d1 - 1)
                    for k in range(IB):
                        if k in FB0:
                            pe.wait_ge(lane.fparts, b * len(FBS) + FB0.index(k) + 1)
                        for part in range(3):
                            ins = nc.tensor.matmul(ps_p[:, d1 % 2, 0:D], lane.fusep[:, part, k, :], w_down1[:, k, :],
                                                   start=(k + part == 0), stop=(k == IB - 1 and part == 2))
                    ins.then_inc(L1.proj, 1)
                pe.wait_ge(lanes[0].x_ready, b * 3 + 3)


CHAIN0, CHAIN1 = 46 + 11, 2 * 54

_OUT = (TILES, P, D)
_DIRECT = ["L0_attn_q_norm_w", "L0_attn_k_norm_w", "L0_xattn_Wq", "L0_xattn_Wk", "L0_xattn_Wv", "L0_xattn_Wo",
           "L1_attn_b_qkv", "L1_attn_b_out", "L1_xattn_Wq", "L1_xattn_bq", "L1_xattn_Wkv", "L1_xattn_bkv",
           "L1_xattn_Wp", "L1_xattn_bp", "L1_ffn_gate_w", "L1_ffn_up_w", "L1_ffn_down_w", "L1_ffn_gate_scale",
           "L1_ffn_up_scale", "L1_ffn_down_scale"]


def constants():
    pos = np.arange(P, dtype=np.float32)

    def tables(d):
        inv = (1.0 / 10000.0 ** (np.arange(0, d, 2, dtype=np.float32) / d)).astype(np.float32)
        ang = pos[:, None] * inv[None, :]
        ang = np.concatenate([ang, ang], -1)
        sign = np.where(np.arange(d) < d // 2, -1.0, 1.0).astype(np.float32)
        return np.stack([np.cos(ang), np.sin(ang) * sign], 1).astype(np.float32)

    c = {"ident": np.eye(P, dtype=np.float32)}
    q, k = np.arange(P)[:, None], np.arange(P)[None, :]
    c["mask_causal"] = np.where(q >= k, 0.0, -1e30).astype(np.float32)
    c["mask_window"] = np.where((q >= k) & (q - k < 64), 0.0, -1e30).astype(np.float32)
    c["rope_k"] = tables(HD0)
    c["rope_q"] = (tables(HD0) * np.float32(HD0 ** -0.5)).astype(np.float32)
    x = tables(HDX)
    c["rope_x"] = np.stack([x * np.float32(HDX ** -0.5), x], 2).astype(np.float32)
    return c


def lay_out(inputs):
    g = {n: np.asarray(v) for n, v in inputs.items()}

    def tiles_T(x):
        return np.ascontiguousarray(x.reshape(TILES, P, KD, P).transpose(0, 3, 2, 1))

    arrays = {n: np.ascontiguousarray(g[n]) for n in _DIRECT}
    arrays["x"] = np.ascontiguousarray(g["x"])
    arrays["xT"] = tiles_T(g["x"])
    arrays["ctxT"] = tiles_T(g["ctx_2048"])
    arrays["mask"] = np.ascontiguousarray(g["mask_Bx1xSxS_fk0"].reshape(TILES, P, P))
    arrays["gate"] = np.ascontiguousarray(g["L0_xattn_gate"].reshape(HX))
    arrays["wT_qkv0"] = np.ascontiguousarray(g["L0_attn_w_qkv"].T)
    arrays["wT_out0"] = np.ascontiguousarray(g["L0_attn_w_out"].T)
    arrays["wT_router"] = np.ascontiguousarray(g["L0_ffn_gate_w"].T)
    arrays["wT_gate"] = np.ascontiguousarray(g["L0_ffn_w_gate"].reshape(EF, D).T)
    arrays["wT_up"] = np.ascontiguousarray(g["L0_ffn_w_up"].reshape(EF, D).T)
    arrays["wT_down"] = np.ascontiguousarray(g["L0_ffn_w_down"].transpose(0, 2, 1).reshape(EF, D))
    arrays["wT_qkv1"] = np.ascontiguousarray(g["L1_attn_W_qkv"].T)
    arrays["wT_out1"] = np.ascontiguousarray(g["L1_attn_W_out"].T)
    arrays.update(constants())
    return arrays


def build(nc, arrays, debug=6):
    a = {n: nc.dram_tensor(f"in_{n}", v.shape, mybir.dt.from_np(v.dtype), kind="ExternalInput").ap()
         for n, v in arrays.items()}
    out = nc.dram_tensor("out_0", _OUT, F32, kind="ExternalOutput").ap()
    mid = nc.dram_tensor("mid", _OUT, F32, kind="Internal").ap() if debug > 3 else out
    keys = nc.dram_tensor("keys", (TILES, P, H1 // 2, P), BF16, kind="Internal").ap()
    values = nc.dram_tensor("values", (TILES, P, D), F32, kind="Internal").ap()
    decoder(nc, a, mid, keys, values, out, debug)


def kernel(**inputs):
    import concourse.bacc as bacc
    from concourse.bass_utils import run_bass_kernel_spmd

    arrays = lay_out(inputs)
    nc = bacc.Bacc("TRN2", target_bir_lowering=False, num_devices=1)
    build(nc, arrays)
    r = run_bass_kernel_spmd(nc, [{f"in_{n}": v for n, v in arrays.items()}], core_ids=[0])
    return r.results[0]["out_0"]
```
